# Optimizing a Trainium2 kernel written in Bass

```python
import numpy as np
import jax
import jax.numpy as jnp

def _softmax(x, axis=-1):
    return jax.nn.softmax(x, axis=axis)

def _gelu(x):
    return jax.nn.gelu(x, approximate=True)

def _silu(x):
    return jax.nn.silu(x)

def _sigmoid(x):
    return jax.nn.sigmoid(x)

def _layernorm(x, axis=-1, eps=1e-05):
    m = jnp.mean(x, axis=axis, keepdims=True)
    v = jnp.var(x, axis=axis, keepdims=True)
    return (x - m) / jnp.sqrt(v + eps)

def _scatter_add(tgt, idx, src, axis=0):
    return tgt.at[idx].add(src)

def _segment_sum(src, seg, n):
    return jax.ops.segment_sum(src, seg, n)
kernel_name = 'mk_decoder_postln_d2_seqx_r4_7c6711'

def setup_inputs(seed: int=0):
    np.random.seed(seed)
    _w = jnp.asarray

    def _rec_inputs():
        import jax
        import jax.numpy as jnp
        _rk = jax.random.key(seed)
        x = -0.0002928 + 1 * jax.random.normal(jax.random.fold_in(_rk, 1), (32, 256, 256), jnp.float32)
        _lenS = 256 - jax.random.randint(jax.random.fold_in(_rk, 7), (32,), 0, max(1, 256 // 4) + 1, jnp.int32)
        _lenS2 = 256 - jax.random.randint(jax.random.fold_in(_rk, 8), (32,), 0, max(1, 256 // 4) + 1, jnp.int32)
        _ctx_1024P = jax.random.normal(jax.random.fold_in(_rk, 11), (32, 16, 256), jnp.float32)
        _ctx_1024c = jax.random.dirichlet(jax.random.fold_in(_rk, 511), 0.3 * jnp.ones((16,), jnp.float32), (32, 256))
        _ctx_1024t = jnp.einsum('bsk,bkd->bsd', _ctx_1024c, _ctx_1024P)
        _ctx_1024t = _ctx_1024t * jax.lax.rsqrt(jnp.mean(jnp.square(_ctx_1024t)) + 1e-12) * 0.953939
        ctx_1024 = -1.39393e-06 + 0.999914 * (_ctx_1024t + 0.3 * jax.random.normal(jax.random.fold_in(_rk, 611), (32, 256, 256), jnp.float32))
        _validS = jnp.arange(256)[None, :] < _lenS[:, None]
        _validS2 = jnp.arange(256)[None, :] < _lenS2[:, None]
        _causal = jnp.tril(jnp.ones((256, 256), dtype=bool))
        mask_1x1xSxS2_ik0 = jnp.where(jnp.broadcast_to(_validS2[0:1, None, None, :], (1, 1, 256, 256)), 0, 1).astype(jnp.int32)
        return (x, ctx_1024, mask_1x1xSxS2_ik0)
    x, ctx_1024, mask_1x1xSxS2_ik0 = _rec_inputs()

    def _L0_attn_setup():
        import jax, jax.numpy as jnp
        import numpy as np
        B, S, D = (2, 512, 256)
        QKV = 512
        H = 16
        HD = QKV // H
        SCALE = HD ** (-0.5)
        key = jax.random.key(seed)
        k1, k2, k3, k4, k5 = jax.random.split(key, 5)
        std = D ** (-0.5)
        return {'x': jax.random.normal(k1, (B, S, D), dtype=jnp.float32), 'wq': jax.random.normal(k2, (QKV, D), dtype=jnp.float32) * std, 'wk': jax.random.normal(k3, (QKV, D), dtype=jnp.float32) * std, 'wv': jax.random.normal(k4, (QKV, D), dtype=jnp.float32) * std, 'wo': jax.random.normal(k5, (D, QKV), dtype=jnp.float32) * QKV ** (-0.5)}
    _L0_attn_all = _L0_attn_setup()
    _L0_attn_in = {k: v for k, v in _L0_attn_all.items() if k in ('wq', 'wk', 'wv', 'wo')}
    del _L0_attn_all

    def _L0_xattn_setup():
        import jax, jax.numpy as jnp
        import numpy as np
        EPS = 1e-06
        LN_EPS = 1e-06

        def _mlstm_parallel_stabilized(q, k, v, igate_preact, fgate_preact):
            B, NH, S, DH = q.shape
            log_fg = jax.nn.log_sigmoid(fgate_preact[..., 0])
            cs = jnp.cumsum(log_fg, axis=-1)
            fg_mat = cs[..., :, None] - cs[..., None, :]
            mask = jnp.tril(jnp.ones((S, S), dtype=bool))
            log_D = jnp.where(mask, fg_mat + igate_preact[..., 0][..., None, :], -jnp.inf)
            max_log_D = jnp.max(log_D, axis=-1, keepdims=True)
            D = jnp.exp(log_D - max_log_D)
            k_scaled = k / jnp.sqrt(jnp.float32(DH)).astype(k.dtype)
            qk = jnp.einsum('bhsd,bhtd->bhst', q, k_scaled)
            C = qk * D
            normalizer = jnp.maximum(jnp.abs(jnp.sum(C, axis=-1, keepdims=True)), jnp.exp(-max_log_D))
            C_norm = C / (normalizer + EPS)
            return jnp.einsum('bhst,bhtd->bhsd', C_norm, v)

        def _multihead_layernorm(x, weight):
            mu = jnp.mean(x, axis=-1, keepdims=True)
            var = jnp.mean(jnp.square(x - mu), axis=-1, keepdims=True)
            xn = (x - mu) * jax.lax.rsqrt(var + LN_EPS)
            return xn * weight[None, :, None, :]
        key = jax.random.key(seed)
        ks = jax.random.split(key, 6)
        B, S, E, NH = (2, 512, 256, 8)
        q = jax.random.normal(ks[0], (B, S, E), dtype=jnp.float32)
        k = jax.random.normal(ks[1], (B, S, E), dtype=jnp.float32)
        v = jax.random.normal(ks[2], (B, S, E), dtype=jnp.float32)
        igate_kernel = jnp.zeros((3 * E, NH), dtype=jnp.float32)
        igate_bias = 0.1 * jax.random.normal(ks[3], (NH,), dtype=jnp.float32)
        fgate_kernel = jnp.zeros((3 * E, NH), dtype=jnp.float32)
        fgate_bias = jnp.linspace(3.0, 6.0, NH, dtype=jnp.float32)
        outnorm_weight = jnp.ones((NH, E // NH), dtype=jnp.float32)
        return {'q': q, 'k': k, 'v': v, 'igate_kernel': igate_kernel, 'igate_bias': igate_bias, 'fgate_kernel': fgate_kernel, 'fgate_bias': fgate_bias, 'outnorm_weight': outnorm_weight}
    _L0_xattn_all = _L0_xattn_setup()
    _L0_xattn_in = {k: v for k, v in _L0_xattn_all.items() if k in ('igate_kernel', 'igate_bias', 'fgate_kernel', 'fgate_bias', 'outnorm_weight')}
    del _L0_xattn_all

    def _L0_ffn_setup():
        import jax, jax.numpy as jnp
        import numpy as np
        NUM_COLUMNS = 16
        INPUT_DIM = 256
        NUM_NEURONS = 64
        SPARSITY = 0.05
        B, S = (4, 512)

        def _l2norm(v, axis=-1, eps=1e-12):
            n = jnp.sqrt(jnp.sum(v * v, axis=axis, keepdims=True))
            return v / jnp.maximum(n, eps)
        key = jax.random.key(seed)
        ks = jax.random.split(key, 12)
        D, C, N = (INPUT_DIM, NUM_COLUMNS, NUM_NEURONS)
        inp = {'x': jax.random.normal(ks[0], (B, S, D), dtype=jnp.float32), 'col_emb': jax.random.normal(ks[1], (C, D), dtype=jnp.float32) * 0.02, 'gate_w1': jax.random.normal(ks[2], (D, D // 2), dtype=jnp.float32) / np.sqrt(D), 'gate_b1': jnp.zeros((D // 2,), dtype=jnp.float32), 'gate_w2': jax.random.normal(ks[3], (D // 2, C), dtype=jnp.float32) / np.sqrt(D // 2), 'gate_b2': jnp.zeros((C,), dtype=jnp.float32), 'W_cols': jax.random.normal(ks[4], (C, D, N), dtype=jnp.float32) / np.sqrt(D), 'b_cols': jnp.zeros((C, N), dtype=jnp.float32), 'proj_w': jax.random.normal(ks[5], (C * N, D), dtype=jnp.float32) / np.sqrt(C * N), 'proj_b': jnp.zeros((D,), dtype=jnp.float32), 'ln_g': jnp.ones((D,), dtype=jnp.float32), 'ln_b': jnp.zeros((D,), dtype=jnp.float32)}
        return inp
    _L0_ffn_all = _L0_ffn_setup()
    _L0_ffn_in = {k: v for k, v in _L0_ffn_all.items() if k in ('col_emb', 'gate_w1', 'gate_b1', 'gate_w2', 'gate_b2', 'W_cols', 'b_cols', 'proj_w', 'proj_b', 'ln_g', 'ln_b')}
    del _L0_ffn_all

    def _L1_attn_setup():
        import jax, jax.numpy as jnp
        import numpy as np
        from jax import lax
        D_MODEL = 256
        D_STATE = 16
        D_CONV = 4
        EXPAND = 2
        D_INNER = EXPAND * D_MODEL
        DT_RANK = (D_MODEL + 15) // 16
        B, T = (2, 512)

        def _silu(v):
            return v * jax.nn.sigmoid(v)

        def _mamba_forward(x, in_proj_w, conv_w, conv_b, x_proj_w, dt_proj_w, dt_proj_b, A_log, Dp, out_proj_w):
            xz = jnp.einsum('btd,ed->bte', x, in_proj_w)
            xi, z = jnp.split(xz, 2, axis=-1)
            xt = jnp.pad(jnp.transpose(xi, (0, 2, 1)), ((0, 0), (0, 0), (D_CONV - 1, 0)))
            xc = lax.conv_general_dilated(xt, conv_w[:, None, :], window_strides=(1,), padding='VALID', feature_group_count=D_INNER, dimension_numbers=('NCH', 'OIH', 'NCH'))
            xc = _silu(xc + conv_b[None, :, None])
            xc = jnp.transpose(xc, (0, 2, 1))
            x_dbl = jnp.einsum('bti,ei->bte', xc, x_proj_w)
            dt_lo, Bp, Cp = jnp.split(x_dbl, [DT_RANK, DT_RANK + D_STATE], axis=-1)
            dt = jax.nn.softplus(jnp.einsum('btr,ir->bti', dt_lo, dt_proj_w) + dt_proj_b)
            A = -jnp.exp(A_log)
            h0 = jnp.zeros((x.shape[0], D_INNER, D_STATE), dtype=jnp.float32)

            def step(h, inp):
                dt_t, B_t, C_t, x_t = inp
                dA = jnp.exp(dt_t[..., None] * A[None])
                dBx = dt_t[..., None] * B_t[:, None, :] * x_t[..., None]
                h = dA * h + dBx
                y_t = jnp.sum(h * C_t[:, None, :], axis=-1)
                return (h, y_t)
            scan_in = (jnp.moveaxis(dt, 1, 0), jnp.moveaxis(Bp, 1, 0), jnp.moveaxis(Cp, 1, 0), jnp.moveaxis(xc, 1, 0))
            _, ys = lax.scan(step, h0, scan_in)
            y = jnp.moveaxis(ys, 0, 1) + Dp * xc
            y = y * _silu(z)
            return jnp.einsum('bti,di->btd', y, out_proj_w)
        key = jax.random.key(seed)
        ks = jax.random.split(key, 10)
        s = lambda n: 1.0 / np.sqrt(n)
        x = jax.random.normal(ks[0], (B, T, D_MODEL), dtype=jnp.float32)
        in_proj_w = jax.random.uniform(ks[1], (2 * D_INNER, D_MODEL), minval=-s(D_MODEL), maxval=s(D_MODEL))
        conv_w = jax.random.uniform(ks[2], (D_INNER, D_CONV), minval=-s(D_CONV), maxval=s(D_CONV))
        conv_b = jax.random.uniform(ks[3], (D_INNER,), minval=-s(D_CONV), maxval=s(D_CONV))
        x_proj_w = jax.random.uniform(ks[4], (DT_RANK + 2 * D_STATE, D_INNER), minval=-s(D_INNER), maxval=s(D_INNER))
        dt_proj_w = jax.random.uniform(ks[5], (D_INNER, DT_RANK), minval=-s(DT_RANK), maxval=s(DT_RANK))
        dt_proj_b = jax.random.uniform(ks[6], (D_INNER,), minval=-s(DT_RANK), maxval=s(DT_RANK))
        A_log = jnp.log(jnp.tile(jnp.arange(1, D_STATE + 1, dtype=jnp.float32), (D_INNER, 1)))
        Dp = jnp.ones((D_INNER,), dtype=jnp.float32)
        out_proj_w = jax.random.uniform(ks[7], (D_MODEL, D_INNER), minval=-s(D_INNER), maxval=s(D_INNER))
        return {'x': x, 'in_proj_w': in_proj_w, 'conv_w': conv_w, 'conv_b': conv_b, 'x_proj_w': x_proj_w, 'dt_proj_w': dt_proj_w, 'dt_proj_b': dt_proj_b, 'A_log': A_log, 'Dp': Dp, 'out_proj_w': out_proj_w}
    _L1_attn_all = _L1_attn_setup()
    _L1_attn_in = {k: v for k, v in _L1_attn_all.items() if k in ('in_proj_w', 'conv_w', 'conv_b', 'x_proj_w', 'dt_proj_w', 'dt_proj_b', 'A_log', 'Dp', 'out_proj_w')}
    del _L1_attn_all

    def _L1_xattn_setup():
        import jax, jax.numpy as jnp
        import numpy as np
        HEADS = 16
        key = jax.random.key(seed)
        ks = jax.random.split(key, 8)
        N, S, E = (2, 512, 256)
        scale = 1.0 / np.sqrt(E)
        inp = {'values': jax.random.normal(ks[0], (N, S, E), jnp.float32), 'keys': jax.random.normal(ks[1], (N, S, E), jnp.float32), 'query': jax.random.normal(ks[2], (N, S, E), jnp.float32), 'mask': jnp.tril(jnp.ones((1, 1, S, S), jnp.int32)), 'Wv': jax.random.normal(ks[3], (E, E), jnp.float32) * scale, 'bv': jnp.zeros((E,), jnp.float32), 'Wk': jax.random.normal(ks[4], (E, E), jnp.float32) * scale, 'bk': jnp.zeros((E,), jnp.float32), 'Wq': jax.random.normal(ks[5], (E, E), jnp.float32) * scale, 'bq': jnp.zeros((E,), jnp.float32), 'Wo': jax.random.normal(ks[6], (E, E), jnp.float32) * scale, 'bo': jnp.zeros((E,), jnp.float32)}
        return inp
    _L1_xattn_all = _L1_xattn_setup()
    _L1_xattn_in = {k: v for k, v in _L1_xattn_all.items() if k in ('Wv', 'bv', 'Wk', 'bk', 'Wq', 'bq', 'Wo', 'bo')}
    del _L1_xattn_all

    def _L1_ffn_setup():
        import jax, jax.numpy as jnp
        import numpy as np
        CAPACITY_FACTOR = 0.5
        NUM_HEADS = 16
        key = jax.random.key(seed)
        ks = jax.random.split(key, 6)
        B, N, D = (4, 1024, 256)
        s = 1.0 / np.sqrt(D)
        return {'token_inputs': jax.random.normal(ks[0], (B, N, D), jnp.float32), 'Wg': jax.random.normal(ks[1], (D, 1), jnp.float32) * s, 'Wq': jax.random.normal(ks[2], (D, D), jnp.float32) * s, 'Wk': jax.random.normal(ks[3], (D, D), jnp.float32) * s, 'Wv': jax.random.normal(ks[4], (D, D), jnp.float32) * s, 'Wo': jax.random.normal(ks[5], (D, D), jnp.float32) * s}
    _L1_ffn_all = _L1_ffn_setup()
    _L1_ffn_in = {k: v for k, v in _L1_ffn_all.items() if k in ('Wg', 'Wq', 'Wk', 'Wv', 'Wo')}
    del _L1_ffn_all
    return {'x': x, 'ctx_1024': ctx_1024, 'mask_1x1xSxS2_ik0': mask_1x1xSxS2_ik0, 'L0_attn_wq': _L0_attn_in['wq'], 'L0_attn_wk': _L0_attn_in['wk'], 'L0_attn_wv': _L0_attn_in['wv'], 'L0_attn_wo': _L0_attn_in['wo'], 'L0_xattn_igate_kernel': _L0_xattn_in['igate_kernel'], 'L0_xattn_igate_bias': _L0_xattn_in['igate_bias'], 'L0_xattn_fgate_kernel': _L0_xattn_in['fgate_kernel'], 'L0_xattn_fgate_bias': _L0_xattn_in['fgate_bias'], 'L0_xattn_outnorm_weight': _L0_xattn_in['outnorm_weight'], 'L0_ffn_col_emb': _L0_ffn_in['col_emb'], 'L0_ffn_gate_w1': _L0_ffn_in['gate_w1'], 'L0_ffn_gate_b1': _L0_ffn_in['gate_b1'], 'L0_ffn_gate_w2': _L0_ffn_in['gate_w2'], 'L0_ffn_gate_b2': _L0_ffn_in['gate_b2'], 'L0_ffn_W_cols': _L0_ffn_in['W_cols'], 'L0_ffn_b_cols': _L0_ffn_in['b_cols'], 'L0_ffn_proj_w': _L0_ffn_in['proj_w'], 'L0_ffn_proj_b': _L0_ffn_in['proj_b'], 'L0_ffn_ln_g': _L0_ffn_in['ln_g'], 'L0_ffn_ln_b': _L0_ffn_in['ln_b'], 'L1_attn_in_proj_w': _L1_attn_in['in_proj_w'], 'L1_attn_conv_w': _L1_attn_in['conv_w'], 'L1_attn_conv_b': _L1_attn_in['conv_b'], 'L1_attn_x_proj_w': _L1_attn_in['x_proj_w'], 'L1_attn_dt_proj_w': _L1_attn_in['dt_proj_w'], 'L1_attn_dt_proj_b': _L1_attn_in['dt_proj_b'], 'L1_attn_A_log': _L1_attn_in['A_log'], 'L1_attn_Dp': _L1_attn_in['Dp'], 'L1_attn_out_proj_w': _L1_attn_in['out_proj_w'], 'L1_xattn_Wv': _L1_xattn_in['Wv'], 'L1_xattn_bv': _L1_xattn_in['bv'], 'L1_xattn_Wk': _L1_xattn_in['Wk'], 'L1_xattn_bk': _L1_xattn_in['bk'], 'L1_xattn_Wq': _L1_xattn_in['Wq'], 'L1_xattn_bq': _L1_xattn_in['bq'], 'L1_xattn_Wo': _L1_xattn_in['Wo'], 'L1_xattn_bo': _L1_xattn_in['bo'], 'L1_ffn_Wg': _L1_ffn_in['Wg'], 'L1_ffn_Wq': _L1_ffn_in['Wq'], 'L1_ffn_Wk': _L1_ffn_in['Wk'], 'L1_ffn_Wv': _L1_ffn_in['Wv'], 'L1_ffn_Wo': _L1_ffn_in['Wo']}

def reference(x, ctx_1024, mask_1x1xSxS2_ik0, L0_attn_wq, L0_attn_wk, L0_attn_wv, L0_attn_wo, L0_xattn_igate_kernel, L0_xattn_igate_bias, L0_xattn_fgate_kernel, L0_xattn_fgate_bias, L0_xattn_outnorm_weight, L0_ffn_col_emb, L0_ffn_gate_w1, L0_ffn_gate_b1, L0_ffn_gate_w2, L0_ffn_gate_b2, L0_ffn_W_cols, L0_ffn_b_cols, L0_ffn_proj_w, L0_ffn_proj_b, L0_ffn_ln_g, L0_ffn_ln_b, L1_attn_in_proj_w, L1_attn_conv_w, L1_attn_conv_b, L1_attn_x_proj_w, L1_attn_dt_proj_w, L1_attn_dt_proj_b, L1_attn_A_log, L1_attn_Dp, L1_attn_out_proj_w, L1_xattn_Wv, L1_xattn_bv, L1_xattn_Wk, L1_xattn_bk, L1_xattn_Wq, L1_xattn_bq, L1_xattn_Wo, L1_xattn_bo, L1_ffn_Wg, L1_ffn_Wq, L1_ffn_Wk, L1_ffn_Wv, L1_ffn_Wo):
    import jax
    import jax.numpy as jnp

    def _L0_attn_ref(x, wq, wk, wv, wo):
        import jax, jax.numpy as jnp
        import numpy as np
        B, S, D = (2, 512, 256)
        QKV = 512
        H = 16
        HD = QKV // H
        SCALE = HD ** (-0.5)
        b, s, _ = x.shape
        q = (x @ wq.T).reshape(b, s, H, HD).transpose(0, 2, 1, 3)
        k = (x @ wk.T).reshape(b, s, H, HD).transpose(0, 2, 1, 3)
        v = (x @ wv.T).reshape(b, s, H, HD).transpose(0, 2, 1, 3)
        scores = jnp.einsum('bhqd,bhkd->bhqk', q, k) * SCALE
        causal = jnp.tril(jnp.ones((s, s), dtype=bool))
        scores = jnp.where(causal[None, None], scores, -jnp.inf)
        attn = jax.nn.softmax(scores, axis=-1)
        out = jnp.einsum('bhqk,bhkd->bhqd', attn, v)
        out = out.transpose(0, 2, 1, 3).reshape(b, s, QKV)
        return out @ wo.T

    def _L0_xattn_ref(q, k, v, igate_kernel, igate_bias, fgate_kernel, fgate_bias, outnorm_weight):
        import jax, jax.numpy as jnp
        import numpy as np
        EPS = 1e-06
        LN_EPS = 1e-06

        def _mlstm_parallel_stabilized(q, k, v, igate_preact, fgate_preact):
            B, NH, S, DH = q.shape
            log_fg = jax.nn.log_sigmoid(fgate_preact[..., 0])
            cs = jnp.cumsum(log_fg, axis=-1)
            fg_mat = cs[..., :, None] - cs[..., None, :]
            mask = jnp.tril(jnp.ones((S, S), dtype=bool))
            log_D = jnp.where(mask, fg_mat + igate_preact[..., 0][..., None, :], -jnp.inf)
            max_log_D = jnp.max(log_D, axis=-1, keepdims=True)
            D = jnp.exp(log_D - max_log_D)
            k_scaled = k / jnp.sqrt(jnp.float32(DH)).astype(k.dtype)
            qk = jnp.einsum('bhsd,bhtd->bhst', q, k_scaled)
            C = qk * D
            normalizer = jnp.maximum(jnp.abs(jnp.sum(C, axis=-1, keepdims=True)), jnp.exp(-max_log_D))
            C_norm = C / (normalizer + EPS)
            return jnp.einsum('bhst,bhtd->bhsd', C_norm, v)

        def _multihead_layernorm(x, weight):
            mu = jnp.mean(x, axis=-1, keepdims=True)
            var = jnp.mean(jnp.square(x - mu), axis=-1, keepdims=True)
            xn = (x - mu) * jax.lax.rsqrt(var + LN_EPS)
            return xn * weight[None, :, None, :]
        B, S, E = q.shape
        NH = igate_bias.shape[0]
        qkv = jnp.concatenate([q, k, v], axis=-1)
        igate_preact = qkv @ igate_kernel + igate_bias
        fgate_preact = qkv @ fgate_kernel + fgate_bias
        qh = q.reshape(B, S, NH, -1).transpose(0, 2, 1, 3)
        kh = k.reshape(B, S, NH, -1).transpose(0, 2, 1, 3)
        vh = v.reshape(B, S, NH, -1).transpose(0, 2, 1, 3)
        ig = igate_preact.transpose(0, 2, 1)[..., None]
        fg = fgate_preact.transpose(0, 2, 1)[..., None]
        h = _mlstm_parallel_stabilized(qh, kh, vh, ig, fg)
        h_norm = _multihead_layernorm(h, outnorm_weight)
        return h_norm.transpose(0, 2, 1, 3).reshape(B, S, -1)

    def _L0_ffn_ref(x, col_emb, gate_w1, gate_b1, gate_w2, gate_b2, W_cols, b_cols, proj_w, proj_b, ln_g, ln_b):
        import jax, jax.numpy as jnp
        import numpy as np
        NUM_COLUMNS = 16
        INPUT_DIM = 256
        NUM_NEURONS = 64
        SPARSITY = 0.05
        B, S = (4, 512)

        def _l2norm(v, axis=-1, eps=1e-12):
            n = jnp.sqrt(jnp.sum(v * v, axis=axis, keepdims=True))
            return v / jnp.maximum(n, eps)
        Bq, Sq, D = x.shape
        C = col_emb.shape[0]
        similarity = jnp.einsum('bsd,cd->bsc', _l2norm(x), _l2norm(col_emb))
        h = jax.nn.gelu(x @ gate_w1 + gate_b1, approximate=False)
        gate_values = jax.nn.sigmoid(h @ gate_w2 + gate_b2)
        logits = similarity + gate_values
        k = max(1, int(C * SPARSITY))
        _, top_idx = jax.lax.top_k(logits, k)
        mask = jnp.sum(jax.nn.one_hot(top_idx, C, dtype=logits.dtype), axis=-2)
        weights = mask * jax.nn.softmax(logits, axis=-1)
        cols = jax.nn.gelu(jnp.einsum('bsd,cdn->bscn', x, W_cols) + b_cols, approximate=False)
        cols = cols * weights[..., None]
        combined = cols.reshape(Bq, Sq, -1)
        y = combined @ proj_w + proj_b + x
        mu = jnp.mean(y, axis=-1, keepdims=True)
        var = jnp.mean((y - mu) ** 2, axis=-1, keepdims=True)
        out = (y - mu) * jax.lax.rsqrt(var + 1e-05) * ln_g + ln_b
        return out

    def _L1_attn_ref(x, in_proj_w, conv_w, conv_b, x_proj_w, dt_proj_w, dt_proj_b, A_log, Dp, out_proj_w):
        import jax, jax.numpy as jnp
        import numpy as np
        from jax import lax
        D_MODEL = 256
        D_STATE = 16
        D_CONV = 4
        EXPAND = 2
        D_INNER = EXPAND * D_MODEL
        DT_RANK = (D_MODEL + 15) // 16
        B, T = (2, 512)

        def _silu(v):
            return v * jax.nn.sigmoid(v)

        def _mamba_forward(x, in_proj_w, conv_w, conv_b, x_proj_w, dt_proj_w, dt_proj_b, A_log, Dp, out_proj_w):
            xz = jnp.einsum('btd,ed->bte', x, in_proj_w)
            xi, z = jnp.split(xz, 2, axis=-1)
            xt = jnp.pad(jnp.transpose(xi, (0, 2, 1)), ((0, 0), (0, 0), (D_CONV - 1, 0)))
            xc = lax.conv_general_dilated(xt, conv_w[:, None, :], window_strides=(1,), padding='VALID', feature_group_count=D_INNER, dimension_numbers=('NCH', 'OIH', 'NCH'))
            xc = _silu(xc + conv_b[None, :, None])
            xc = jnp.transpose(xc, (0, 2, 1))
            x_dbl = jnp.einsum('bti,ei->bte', xc, x_proj_w)
            dt_lo, Bp, Cp = jnp.split(x_dbl, [DT_RANK, DT_RANK + D_STATE], axis=-1)
            dt = jax.nn.softplus(jnp.einsum('btr,ir->bti', dt_lo, dt_proj_w) + dt_proj_b)
            A = -jnp.exp(A_log)
            h0 = jnp.zeros((x.shape[0], D_INNER, D_STATE), dtype=jnp.float32)

            def step(h, inp):
                dt_t, B_t, C_t, x_t = inp
                dA = jnp.exp(dt_t[..., None] * A[None])
                dBx = dt_t[..., None] * B_t[:, None, :] * x_t[..., None]
                h = dA * h + dBx
                y_t = jnp.sum(h * C_t[:, None, :], axis=-1)
                return (h, y_t)
            scan_in = (jnp.moveaxis(dt, 1, 0), jnp.moveaxis(Bp, 1, 0), jnp.moveaxis(Cp, 1, 0), jnp.moveaxis(xc, 1, 0))
            _, ys = lax.scan(step, h0, scan_in)
            y = jnp.moveaxis(ys, 0, 1) + Dp * xc
            y = y * _silu(z)
            return jnp.einsum('bti,di->btd', y, out_proj_w)
        return _mamba_forward(x, in_proj_w, conv_w, conv_b, x_proj_w, dt_proj_w, dt_proj_b, A_log, Dp, out_proj_w)

    def _L1_xattn_ref(values, keys, query, mask, Wv, bv, Wk, bk, Wq, bq, Wo, bo):
        import jax, jax.numpy as jnp
        import numpy as np
        HEADS = 16
        N, Lq, E = query.shape
        H = HEADS
        D = E // H
        v = (values @ Wv + bv).reshape(N, -1, H, D)
        k = (keys @ Wk + bk).reshape(N, -1, H, D)
        q = (query @ Wq + bq).reshape(N, Lq, H, D)
        energy = jnp.einsum('nqhd,nkhd->nhqk', q, k)
        neg = jnp.finfo(energy.dtype).min
        energy = jnp.where(mask == 0, neg, energy)
        attn = jax.nn.softmax(energy / jnp.sqrt(jnp.asarray(D, energy.dtype)), axis=-1)
        out = jnp.einsum('nhqk,nkhd->nqhd', attn, v).reshape(N, Lq, E)
        return out @ Wo + bo

    def _L1_ffn_ref(token_inputs, Wg, Wq, Wk, Wv, Wo):
        import jax, jax.numpy as jnp
        import numpy as np
        CAPACITY_FACTOR = 0.5
        NUM_HEADS = 16
        B, N, D = token_inputs.shape
        C = int(N * CAPACITY_FACTOR)
        H = NUM_HEADS
        dh = D // H
        gate = jax.nn.sigmoid((token_inputs @ Wg)[..., 0])
        _, idx = jax.lax.top_k(gate, C)
        attn_in = jnp.take_along_axis(token_inputs, idx[..., None], axis=1)
        q = (attn_in @ Wq).reshape(B, C, H, dh)
        k = (attn_in @ Wk).reshape(B, C, H, dh)
        v = (attn_in @ Wv).reshape(B, C, H, dh)
        scores = jnp.einsum('bqhd,bkhd->bhqk', q, k) / jnp.sqrt(jnp.float32(dh))
        attn = jax.nn.softmax(scores, axis=-1)
        o = jnp.einsum('bhqk,bkhd->bqhd', attn, v).reshape(B, C, D) @ Wo
        gate_sel = jnp.take_along_axis(gate, idx, axis=1)
        out = jnp.zeros_like(token_inputs)
        out = out.at[jnp.arange(B)[:, None], idx].set(o * gate_sel[..., None])
        return out
    x = _layernorm(x + _L0_attn_ref(x, L0_attn_wq, L0_attn_wk, L0_attn_wv, L0_attn_wo), axis=-1)
    x = _layernorm(x + _L0_xattn_ref(x, ctx_1024, ctx_1024, L0_xattn_igate_kernel, L0_xattn_igate_bias, L0_xattn_fgate_kernel, L0_xattn_fgate_bias, L0_xattn_outnorm_weight), axis=-1)
    x = _layernorm(x + _L0_ffn_ref(x, L0_ffn_col_emb, L0_ffn_gate_w1, L0_ffn_gate_b1, L0_ffn_gate_w2, L0_ffn_gate_b2, L0_ffn_W_cols, L0_ffn_b_cols, L0_ffn_proj_w, L0_ffn_proj_b, L0_ffn_ln_g, L0_ffn_ln_b), axis=-1)
    x = _layernorm(x + _L1_attn_ref(x, L1_attn_in_proj_w, L1_attn_conv_w, L1_attn_conv_b, L1_attn_x_proj_w, L1_attn_dt_proj_w, L1_attn_dt_proj_b, L1_attn_A_log, L1_attn_Dp, L1_attn_out_proj_w), axis=-1)
    x = _layernorm(x + _L1_xattn_ref(ctx_1024, ctx_1024, x, mask_1x1xSxS2_ik0, L1_xattn_Wv, L1_xattn_bv, L1_xattn_Wk, L1_xattn_bk, L1_xattn_Wq, L1_xattn_bq, L1_xattn_Wo, L1_xattn_bo), axis=-1)
    x = _layernorm(x + _L1_ffn_ref(x, L1_ffn_Wg, L1_ffn_Wq, L1_ffn_Wk, L1_ffn_Wv, L1_ffn_Wo), axis=-1)
    return x

_drawn_inputs = setup_inputs


def setup_inputs(seed=0):
    import zlib

    import numpy as np

    out = dict(_drawn_inputs(seed))
    spreads = {'L0_xattn_igate_kernel': (0.0, 0.1),
     'L0_xattn_fgate_kernel': (0.0, 0.1),
     'L0_xattn_outnorm_weight': (1.0, 0.2),
     'L0_ffn_gate_b1': (0.0, 0.8),
     'L0_ffn_gate_b2': (0.0, 0.8),
     'L0_ffn_b_cols': (0.0, 0.8),
     'L0_ffn_proj_b': (0.0, 0.1),
     'L0_ffn_ln_g': (1.0, 0.2),
     'L0_ffn_ln_b': (0.0, 0.1),
     'L1_attn_Dp': (1.0, 0.6),
     'L1_xattn_bv': (0.0, 0.1),
     'L1_xattn_bk': (0.0, 2.0),
     'L1_xattn_bq': (0.0, 0.1),
     'L1_xattn_bo': (0.0, 0.1)}
    factors = {'L0_xattn_igate_bias': 62.149,
     'L0_ffn_col_emb': 4.891,
     'L0_ffn_gate_w1': 4.97,
     'L0_ffn_gate_w2': 4.309,
     'L0_ffn_W_cols': 4.529,
     'L0_ffn_proj_w': 4.494,
     'L1_attn_x_proj_w': 7.061,
     'L1_attn_dt_proj_w': 8.0,
     'L1_attn_dt_proj_b': 8.0,
     'L1_attn_A_log': 8.0}
    for name, (base, spread) in spreads.items():
        noise = np.random.default_rng([zlib.crc32(name.encode()), seed]).standard_normal(out[name].shape)
        drawn = base * np.exp(spread * noise) if base else spread * noise
        out[name] = jnp.asarray(drawn.astype(out[name].dtype))
    for name, factor in factors.items():
        out[name] = (out[name] * factor).astype(out[name].dtype)
    return out
```

```python
import concourse.bass as bass
from concourse import mybir
from contextlib import ExitStack

NB, T, D, P = 32, 256, 256, 128
TT, DT = T // P, D // P
QKV0, HD0 = 512, 32
J0 = QKV0 // P
NH_M, HD_M = 8, 32
HID, NCOL, NNEU = 128, 16, 64
CM = NCOL * NNEU // P
DI, NS, KC = 512, 16, 4
JI = DI // P
HN = 4
B_ROW, C_ROW = 32, 64
CAP = T // 2
NBANK = 8
MASKED = -float(2 ** 126)

FILLS = {
    "attn0_in": ["x0T", "q0", "q1", "k0", "k1", "v0", "v1"],
    "mlstm_in": ["x1T", "cT", "gates"],
    "mlstm_rows": ["acol", "ebc"],
    "mlstm_norm": ["mean", "var", "hnT"],
    "ffn0_in": ["x2T", "hid", "sim"],
    "ffn0_gate": ["gate"],
    "ffn0_cols": ["c0", "c1", "c2", "c3"],
    "ffn0_out": ["m0", "m1", "m2", "m3", "y2"],
    "mamba_in": ["x3T", "xi0", "xi1", "z0", "z1"],
    "mamba_dt": ["xdbl", "dt0", "dt1"],
    "mamba_out": ["y3"],
    "xattn_in": ["x4T", "c4T", "xq", "xk", "xv"],
    "xattn_out": ["y4"],
    "moe_in": ["grow", "xsel", "permT", "fq", "fk", "fv"],
    "moe_out": ["fo", "y5"],
}
for _p in range(8):
    FILLS[f"attn0_s{_p}"] = [f"aSA{_p}", f"aSB{_p}"]
    FILLS[f"attn0_t{_p}"] = [f"aTA{_p}", f"aTB{_p}"]
for _j in range(4):
    FILLS[f"attn0_o{_j}"] = [f"aO{_j}"]
    FILLS[f"mlstm_s{_j}"] = [f"mMA{_j}", f"mMB{_j}", f"mKA{_j}", f"mKB{_j}"]
for _j in range(2):
    FILLS[f"mlstm_o{_j}"] = [f"mO{_j}"]
    FILLS[f"xattn_o{_j}"] = [f"xO{_j}"]
    FILLS[f"moe_o{_j}"] = [f"fO{_j}"]
FILLS["attn0_out"] = ["y0"]
for _g in range(8):
    FILLS[f"xattn_s{_g}"] = [f"xSA{_g}", f"xSB{_g}"]
    FILLS[f"xattn_t{_g}"] = [f"xTA{_g}", f"xTB{_g}"]
for _g in range(4):
    FILLS[f"moe_s{_g}"] = [f"fS{_g}"]
    FILLS[f"moe_t{_g}"] = [f"fT{_g}"]

FRONT = (["attn0_in", "attn0_s0"]
         + [s for p in range(8) for s in ([f"attn0_s{p + 1}"] if p < 7 else [])
            + [f"attn0_t{p}"] + ([f"attn0_o{p // 2}"] if p % 2 else [])]
         + ["attn0_out", "mlstm_in", "mlstm_rows", "mlstm_s0", "mlstm_s1", "mlstm_o0",
            "mlstm_s2", "mlstm_s3", "mlstm_o1", "mlstm_norm",
            "ffn0_in", "ffn0_cols", "ffn0_gate", "ffn0_out"])
BACK = (["mamba_in", "mamba_dt"] + [f"mamba_u{u}" for u in range(JI * NS // HN)] + ["mamba_out",
        "xattn_in", "xattn_s0"]
        + [s for g in range(8) for s in ([f"xattn_s{g + 1}"] if g < 7 else [])
           + [f"xattn_t{g}"] + ([f"xattn_o{g // 4}"] if g % 4 == 3 else [])]
        + ["xattn_out", "moe_in", "moe_s0", "moe_s1", "moe_t0", "moe_s2", "moe_t1", "moe_o0",
           "moe_s3", "moe_t2", "moe_t3", "moe_o1", "moe_out"])


def build(nc, a, out):
    f32, bf16, i32 = mybir.dt.float32, mybir.dt.bfloat16, mybir.dt.int32
    ALU, ACT, AX = mybir.AluOpType, mybir.ActivationFunctionType, mybir.AxisListType
    ctx = ExitStack()
    with ctx:
        def sb(name, shape, dt=f32):
            return ctx.enter_context(nc.sbuf_tensor(name, shape, dt))

        def sem(name):
            return ctx.enter_context(nc.semaphore(name))

        W = {}
        for n, shp in (("wq0", [P, DT, QKV0]), ("wk0", [P, DT, QKV0]), ("wv0", [P, DT, QKV0]), ("wo0", [P, J0, D]),
                       ("gw", [P, 6, 16]), ("w1", [P, DT, HID]), ("w2", [P, NCOL]), ("wcols", [P, DT, NCOL * NNEU]),
                       ("wproj", [P, CM, D]), ("win", [P, DT, 2 * DI]), ("wx", [P, JI, P]), ("wdt", [P, DI]),
                       ("wout", [P, JI, D]), ("xwq", [P, DT, D]), ("xwk", [P, DT, D]), ("xwv", [P, DT, D]),
                       ("xwo", [P, DT, D]), ("fwq", [P, DT, D]), ("fwk", [P, DT, D]), ("fwv", [P, DT, D]),
                       ("fwo", [P, DT, D]),
                       ("onw", [P, 2]), ("b1", [P, 1]), ("bcols", [P, CM]), ("convw", [P, JI, KC]), ("convb", [P, JI]),
                       ("bdt", [P, JI]), ("alog", [P, JI, NS]), ("dp", [P, JI]), ("xbq", [P, DT]), ("xbk", [P, DT]),
                       ("gib", [8, 1]), ("gfb", [8, 1])):
            W[n] = sb(n, shp)
        ROWS = {"b2r": NCOL, "pbr": D, "lngr": D, "lnbr": D, "xbvr": D, "xbor": D, "wgr": D}
        for n, w in ROWS.items():
            W[n] = sb(n, [P, w])

        ident, identb = sb("ident", [P, P]), sb("identb", [P, P], bf16)
        triq = sb("triq", [P, P], bf16)
        trik = sb("trik", [P, P], bf16)
        lower = sb("lower", [P, TT, T])
        onesv = sb("onesv", [P, 32])
        onesp = sb("onesp", [P, 2, 32])
        blk = sb("blk", [P, P])
        selh = sb("selh", [P, NH_M, P])
        sele = sb("sele", [P, 2, P])
        hmask0 = sb("hmask0", [P, 2])
        hmask1 = sb("hmask1", [P, 4])
        iota = sb("iota", [P, P])
        revc = sb("revc", [P, TT, NCOL])
        ones8 = sb("ones8", [8, T])
        xmask = sb("xmask", [P, TT, T], bf16)
        anew = sb("anew", [P, JI, NS])
        cst = sb("cst", [NCOL, 4])
        cenT = sb("cenT", [P, DT, NCOL])
        gwc = sb("gwc", [P, 4, 16])
        epsc = sb("epsc", [P, 2])
        blk16 = sb("blk16", [P, 8])

        big = sb("big", [P, 2 * NS * T + 4 * HN * T])
        top = [0]

        def room(*shape):
            n = 1
            for w in shape:
                n *= w
            v = big[:, top[0]:top[0] + n]
            top[0] += n
            assert top[0] <= 2 * NS * T + 4 * HN * T
            return v

        maski = room(TT, T).bitcast(i32).rearrange("p (t k) -> p t k", t=TT)
        maskf = room(TT, T).rearrange("p (t k) -> p t k", t=TT)
        cemb, cen = room(D)[0:NCOL, :], room(D)[0:NCOL, :]
        top[0] = 0
        qm = room(2, J0, T).rearrange("p (a j t) -> p a j t", a=2, j=J0)
        kT = room(J0, T).rearrange("p (j t) -> p j t", j=J0)
        v0 = room(TT, QKV0).rearrange("p (t n) -> p t n", t=TT)
        pr = room(2, 768).rearrange("p (s n) -> p s n", s=2)
        pT = room(4, 768).rearrange("p (s n) -> p s n", s=4)
        oT = room(J0, T).rearrange("p (j t) -> p j t", j=J0)
        rinv = room(2, T).rearrange("p (s t) -> p s t", s=2)
        cF = room(TT, D).rearrange("p (t d) -> p t d", t=TT)
        cT = room(DT, T).rearrange("p (d t) -> p d t", d=DT)
        xTm = qm[:, :, 0:2, :]
        ebc, hT, hcT, hsq, hnT = oT[:, 2:4, :], oT[:, 0:2, :], kT[:, 0:2, :], kT[:, 2:4, :], rinv
        cols = qm.rearrange("p a j t -> p (a j) t")
        v0r = v0.rearrange("p t (r n) -> p (t r) n", r=2)

        def row(i):
            return kT[0:8, i, :] if i < 4 else v0r[0:8, i - 4, :]

        top[0] = 0
        bbc = room(NS, T).rearrange("p (n t) -> p n t", n=NS)
        cbc = room(NS, T).rearrange("p (n t) -> p n t", n=NS)
        dA = [room(HN, T).rearrange("p (n t) -> p n t", n=HN) for _ in range(2)]
        hs = [room(HN, T).rearrange("p (n t) -> p n t", n=HN) for _ in range(2)]
        top[0] = 0
        c4 = room(TT, D).rearrange("p (t d) -> p t d", t=TT)
        c4T = room(DT, T).rearrange("p (d t) -> p d t", d=DT)
        xqm = room(4, DT, T).rearrange("p (m j t) -> p m j t", m=4, j=DT)
        xkT = room(DT, T).rearrange("p (j t) -> p j t", j=DT)
        vp = room(TT, 16, 32).rearrange("p (t h d) -> p t h d", t=TT, h=16)
        xpr = room(2, 1024).rearrange("p (s n) -> p s n", s=2)
        xpT = room(2, 2, 4, T).rearrange("p (s k h q) -> p s k h q", s=2, k=2, h=4)
        xoT = room(DT, T).rearrange("p (j t) -> p j t", j=DT)

        x0, x1, x3 = sb("x0", [P, TT, D]), sb("x1", [P, TT, D]), sb("x3", [P, TT, D])
        x2 = x0
        xT = sb("xT", [P, DT, T])
        nmx = sb("nmx", [P, 2, 4])
        yF = sb("yF", [P, TT, D])
        stF, agF, lnF, rsF = sb("stF", [P, TT, 6]), sb("agF", [P, TT, 2]), sb("lnF", [P, TT]), sb("rsF", [P, TT])
        nmr, er = sb("nmr", [P, T]), sb("er", [P, T])
        acol = sb("acol", [P, TT, 8])
        hidT = sb("hidT", [P, T])
        sm = sb("sm", [P, 12, TT, NCOL])
        s2 = sb("s2", [P, 8, TT])
        ohb = sb("ohb", [P, TT, NCOL], bf16)
        ohx = sb("ohx", [P, TT, NCOL, NNEU], bf16)
        sqj = sb("sqj", [P, D])

        x4, x5 = sb("x4", [P, TT, D]), sb("x5", [P, TT, D])
        x6 = x4
        bT = sb("bT", [P, DT, T])
        xp = sb("xp", [P, JI, KC - 1 + T])
        xc, sg, zs = sb("xc", [P, JI, T]), sb("sg", [P, JI, T]), sb("zs", [P, JI, T])
        dtv, yb = sb("dtv", [P, JI, T]), sb("yb", [P, JI, T])
        xd, part = sb("xd", [P, T]), sb("part", [P, 2, T])
        xnm, xri = sb("xnm", [P, 2, 4]), sb("xri", [P, 2, T])
        yB = sb("yB", [P, TT, D])
        stB, agB, lnB, rsB = sb("stB", [P, TT, 6]), sb("agB", [P, TT, 2]), sb("lnB", [P, TT]), sb("rsB", [P, TT])
        gg = sb("gg", [P, 8, TT])
        grep, grow = sb("grep", [P, TT, P]), sb("grow", [P, T])
        junk = sb("junk", [P, D])
        perm, permT = sb("perm", [P, TT, CAP]), sb("permT", [P, TT, P])
        xselT, fo = sb("xselT", [P, DT, CAP]), sb("fo", [P, D])

        scratch = nc.dram_tensor("bc_rows", (2, NS, T), f32, kind="Internal").ap()

        banks = [ctx.enter_context(nc.psum_tensor(f"bank{i}", [P, 512], f32)) for i in range(NBANK)]

        loaded, const_ready, go, stored = sem("loaded"), sem("const_ready"), sem("go"), sem("stored")
        s_set = sem("set_up")
        arrived = sem("arrived")
        bank_full = [sem(f"bank_full{i}") for i in range(NBANK)]
        bank_free = [sem(f"bank_free{i}") for i in range(NBANK)]
        chain = {n: sem(f"{n}_done") for n in ("dve", "act", "pool")}
        signals = {}
        last_sem = [chain["pool"].num]

        def sig(name):
            if name not in signals:
                signals[name] = sem(name)
                assert signals[name].num == last_sem[0] + 1 or not signals, name
                last_sem[0] = signals[name].num
            return signals[name]

        class Ring:

            def __init__(self, steps):
                self.at = {}
                for s in steps:
                    for f in FILLS.get(s, []):
                        self.at[f] = len(self.at)

            def open(self, pe, name):
                n = self.at[name]
                if n >= NBANK:
                    pe.wait_ge(bank_free[n % NBANK], n // NBANK)
                return banks[n % NBANK]

            def full(self, name):
                return bank_full[self.at[name] % NBANK]

            def made(self, eng, name):
                n = self.at[name]
                eng.wait_ge(bank_full[n % NBANK], n // NBANK + 1)
                return banks[n % NBANK]

            def taken(self, eng, name):
                n = self.at[name]
                eng.wait_ge(bank_free[n % NBANK], n // NBANK + 1)

            def free(self, name):
                return bank_free[self.at[name] % NBANK]

        class Chain:

            def __init__(self, eng, s):
                self.eng, self.s, self.n = eng, s, 0

            def __call__(self, ins):
                self.n += 1
                ins.then_inc(self.s, 1)
                self.eng.wait_ge(self.s, self.n)

        STEPS_ALL = FRONT + BACK
        NLOAD = len(W) + 2

        def run_clear(sp):
            sp.sem_clear(range(arrived.num, last_sem[0] + 1))

        with nc.Block() as block:

            @block.tensor
            def _(pe):
                mm = pe.matmul

                def run(steps):
                    ring = Ring(steps)

                    def transposes(name, src, kt=TT):
                        bk = ring.open(pe, name)
                        for d in range(DT):
                            for t in range(TT):
                                last = pe.transpose(bk[:, d * T + t * P:d * T + t * P + P],
                                                    src[:, t, d * P:d * P + P], ident[:, :])
                        last.then_inc(ring.full(name), 1)

                    def project(name, w, m0, src, n=T, nm=2, kt=DT):
                        bk = ring.open(pe, name)
                        for m in range(nm):
                            for k in range(kt):
                                last = mm(bk[:, m * n:(m + 1) * n], w[:, k, (m0 + m) * P:(m0 + m + 1) * P],
                                          src[:, k, 0:n], start=(k == 0), stop=(k == kt - 1))
                        last.then_inc(ring.full(name), 1)

                    def tokens(name, src, w, kt):
                        bk = ring.open(pe, name)
                        for t in range(TT):
                            for k in range(kt):
                                last = mm(bk[:, t * D:(t + 1) * D], src[:, k, t * P:(t + 1) * P], w[:, k, :],
                                          start=(k == 0), stop=(k == kt - 1))
                        last.then_inc(ring.full(name), 1)

                    for s in steps:
                        if s == "attn0_in":
                            pe.wait_ge(sig("x0_ready"), 16)
                            transposes("x0T", x0)
                            ring.taken(pe, "x0T")
                            for n, w in (("q", "wq0"), ("k", "wk0")):
                                for i in range(2):
                                    project(f"{n}{i}", W[w], 2 * i, xT)
                            for t in range(TT):
                                bk = ring.open(pe, f"v{t}")
                                for k in range(DT):
                                    last = mm(bk[:, :], xT[:, k, t * P:(t + 1) * P], W["wv0"][:, k, :],
                                              start=(k == 0), stop=(k == DT - 1))
                                last.then_inc(ring.full(f"v{t}"), 1)
                        elif s.startswith("attn0_s"):
                            p = int(s[7:])
                            if p == 0:
                                ring.taken(pe, "q1")
                                ring.taken(pe, "k1")
                            j, r = p // 2, 64 * (p % 2)
                            A = ring.open(pe, f"aSA{p}")
                            for h in range(2):
                                mm(A[:, h * P:(h + 1) * P], qm[r:r + 64, h, j, 0:P], kT[r:r + 64, j, 0:P],
                                   start=True, stop=False)
                                mm(A[:, h * P:(h + 1) * P], identb[:, :], triq[:, :], start=False, stop=True)
                            for h in range(2):
                                bk, c = (A, 256) if h == 0 else (ring.open(pe, f"aSB{p}"), 0)
                                mm(bk[:, c:c + T], qm[r:r + 64, h, j, P:T], kT[r:r + 64, j, :], start=True, stop=False)
                                mm(bk[:, c + P:c + T], identb[:, :], triq[:, :], start=False,
                                   stop=True).then_inc(ring.full(f"aSA{p}" if h == 0 else f"aSB{p}"), 1)
                        elif s.startswith("attn0_t"):
                            p = int(s[7:])
                            ring.taken(pe, f"aSB{p}")
                            A = ring.open(pe, f"aTA{p}")
                            src = pr[:, p % 2, :]
                            for h in range(2):
                                pe.transpose(A[:, h * T:h * T + P], src[:, h * P:(h + 1) * P], ident[:, :])
                                last = pe.transpose(A[:, h * T + P:(h + 1) * T], src[:, T + h * T:T + h * T + P],
                                                    ident[:, :])
                            last.then_inc(ring.full(f"aTA{p}"), 1)
                            Bk = ring.open(pe, f"aTB{p}")
                            for h in range(2):
                                last = pe.transpose(Bk[:, h * P:(h + 1) * P],
                                                    src[:, T + h * T + P:T + (h + 1) * T], ident[:, :])
                            last.then_inc(ring.full(f"aTB{p}"), 1)
                        elif s.startswith("attn0_o") and s != "attn0_out":
                            j = int(s[7:])
                            if j == 0:
                                ring.taken(pe, "v1")
                            ring.taken(pe, f"aTA{2 * j + 1}")
                            ring.taken(pe, f"aTB{2 * j + 1}")
                            bk = ring.open(pe, f"aO{j}")
                            for ones in (0, 1):
                                for k in range(2):
                                    for i in range(4):
                                        sl, h = (2 * j + i // 2) % 4, i % 2
                                        rhs = pT[:, sl, h * T:(h + 1) * T] if k == 0 else \
                                            pT[:, sl, 512 + h * P:512 + (h + 1) * P]
                                        c = 256 * ones + (P if k else 0)
                                        lh = onesv[:, :] if ones else v0[:, k, 128 * j + 32 * i:128 * j + 32 * i + 32]
                                        last = mm(bk[32 * i:32 * i + 32, c:256 * ones + T], lh, rhs,
                                                  start=(k == 0), stop=(k == 1))
                            last.then_inc(ring.full(f"aO{j}"), 1)
                        elif s == "attn0_out":
                            ring.taken(pe, "aO3")
                            tokens("y0", oT, W["wo0"], J0)
                        elif s == "mlstm_in":
                            pe.wait_ge(sig("cF_ready"), 16)
                            pe.wait_ge(sig("x1_ready"), 2)
                            transposes("x1T", x1)
                            transposes("cT", cF)
                            ring.taken(pe, "x1T")
                            ring.taken(pe, "cT")
                            bk = ring.open(pe, "gates")
                            for g in range(2):
                                for k in range(4):
                                    last = mm(bk[0:8, g * T:(g + 1) * T], gwc[:, k, g * 8:g * 8 + 8],
                                              (xT if k < 2 else cT)[:, k % 2, :], start=(k == 0), stop=(k == 3))
                            last.then_inc(ring.full("gates"), 1)
                        elif s == "mlstm_rows":
                            pe.wait_ge(sig("rows_ready"), 1)
                            bk = ring.open(pe, "acol")
                            for t in range(TT):
                                last = pe.transpose(bk[:, t * 8:t * 8 + 8], row(5)[:, t * P:(t + 1) * P],
                                                    ident[0:8, 0:8])
                            last.then_inc(ring.full("acol"), 1)
                            pe.wait_ge(sig("er_ready"), 1)
                            bk = ring.open(pe, "ebc")
                            for t in range(2):
                                last = mm(bk[:, t * T:(t + 1) * T], sele[:, t, :], er[:, :], start=True, stop=True)
                            last.then_inc(ring.full("ebc"), 1)
                        elif s.startswith("mlstm_s"):
                            q = int(s[7:])
                            j, r = q // 2, 64 * (q % 2)
                            if q == 0:
                                pe.wait_ge(sig("nmr_ready"), 1)
                            A = ring.open(pe, f"mMA{q}")
                            for h in range(2):
                                mm(A[:, h * T:(h + 1) * T], selh[:, 2 * q + h, :], nmr[:, :], start=True, stop=False)
                                last = mm(A[:, h * T:h * T + P], identb[:, :], trik[:, :], start=False, stop=True)
                            last.then_inc(ring.full(f"mMA{q}"), 1)
                            Bk = ring.open(pe, f"mMB{q}")
                            for h in range(2):
                                mm(Bk[:, h * P:(h + 1) * P], selh[:, 2 * q + h, :], nmr[:, P:T], start=True, stop=False)
                                last = mm(Bk[:, h * P:(h + 1) * P], identb[:, :], trik[:, :], start=False, stop=True)
                            last.then_inc(ring.full(f"mMB{q}"), 1)
                            A = ring.open(pe, f"mKA{q}")
                            for h in range(2):
                                last = mm(A[:, h * T:(h + 1) * T], cT[r:r + 64, j, 0:P], xTm[r:r + 64, h, j, :],
                                          start=True, stop=True)
                            last.then_inc(ring.full(f"mKA{q}"), 1)
                            Bk = ring.open(pe, f"mKB{q}")
                            for h in range(2):
                                last = mm(Bk[:, h * P:(h + 1) * P], cT[r:r + 64, j, P:T], xTm[r:r + 64, h, j, P:T],
                                          start=True, stop=True)
                            last.then_inc(ring.full(f"mKB{q}"), 1)
                        elif s.startswith("mlstm_o"):
                            j = int(s[7:])
                            ring.taken(pe, f"mKB{2 * j + 1}")
                            bk = ring.open(pe, f"mO{j}")
                            for ones in (0, 1):
                                for k in range(2):
                                    for i in range(4):
                                        sl, h = 2 * j + i // 2, i % 2
                                        rhs = pT[:, sl, h * T:(h + 1) * T] if k == 0 else \
                                            pT[:, sl, 512 + h * P:512 + (h + 1) * P]
                                        c = 256 * ones + (P if k else 0)
                                        lh = onesv[:, :] if ones else cF[:, k, 128 * j + 32 * i:128 * j + 32 * i + 32]
                                        last = mm(bk[32 * i:32 * i + 32, c:256 * ones + T], lh, rhs,
                                                  start=(k == 0), stop=(k == 1))
                            last.then_inc(ring.full(f"mO{j}"), 1)
                        elif s == "mlstm_norm":
                            for n, src in (("mean", hT), ("var", hsq)):
                                if n == "mean":
                                    ring.taken(pe, "mO1")
                                else:
                                    pe.wait_ge(sig("hsq_ready"), 1)
                                bk = ring.open(pe, n)
                                for t in range(2):
                                    last = mm(bk[:, t * T:(t + 1) * T], blk[:, :], src[:, t, :], start=True, stop=True)
                                last.then_inc(ring.full(n), 1)
                            pe.wait_ge(sig("hnT_ready"), 2)
                            bk = ring.open(pe, "hnT")
                            for t in range(TT):
                                for d in range(DT):
                                    last = pe.transpose(bk[:, t * D + d * P:t * D + d * P + P],
                                                        hnT[:, d, t * P:(t + 1) * P], ident[:, :])
                            last.then_inc(ring.full("hnT"), 1)
                        elif s == "ffn0_in":
                            pe.wait_ge(sig("x2_ready"), 2)
                            transposes("x2T", x2)
                            ring.taken(pe, "x2T")
                            project("hid", W["w1"], 0, xT, nm=1)
                            bk = ring.open(pe, "sim")
                            for t in range(TT):
                                for k in range(DT):
                                    last = mm(bk[:, t * NCOL:(t + 1) * NCOL], xT[:, k, t * P:(t + 1) * P],
                                              cenT[:, k, :], start=(k == 0), stop=(k == DT - 1))
                            last.then_inc(ring.full("sim"), 1)
                        elif s == "ffn0_cols":
                            for c in range(4):
                                project(f"c{c}", W["wcols"], 2 * c, xT)
                        elif s == "ffn0_gate":
                            ring.taken(pe, "hid")
                            bk = ring.open(pe, "gate")
                            for t in range(TT):
                                last = mm(bk[:, t * NCOL:(t + 1) * NCOL], hidT[:, t * P:(t + 1) * P], W["w2"][:, :],
                                          start=True, stop=True)
                            last.then_inc(ring.full("gate"), 1)
                        elif s == "ffn0_out":
                            pe.wait_ge(sig("onehot_wide"), 1)
                            for c in range(4):
                                bk = ring.open(pe, f"m{c}")
                                for m in range(2):
                                    for t in range(TT):
                                        cc = 2 * (2 * c + m)
                                        lh = ohx[:, t, cc:cc + 2, :].rearrange("p c n -> p (c n)")
                                        last = mm(bk[:, m * T + t * P:m * T + (t + 1) * P], lh, identb[:, :],
                                                  start=True, stop=True)
                                last.then_inc(ring.full(f"m{c}"), 1)
                            ring.taken(pe, "m3")
                            tokens("y2", cols, W["wproj"], CM)
                        elif s == "mamba_in":
                            pe.wait_ge(sig("x3_ready"), 2)
                            transposes("x3T", x3)
                            ring.taken(pe, "x3T")
                            for i in range(2):
                                project(f"xi{i}", W["win"], 2 * i, bT)
                            for i in range(2):
                                project(f"z{i}", W["win"], 4 + 2 * i, bT)
                        elif s == "mamba_dt":
                            pe.wait_ge(sig("xc_ready"), 1)
                            project("xdbl", W["wx"], 0, xc, nm=1, kt=JI)
                            ring.taken(pe, "xdbl")
                            for i in range(2):
                                bk = ring.open(pe, f"dt{i}")
                                for m in range(2):
                                    c = (2 * i + m) * P
                                    last = mm(bk[:, m * T:(m + 1) * T], W["wdt"][:, c:c + P], xd[:, :],
                                              start=True, stop=True)
                                last.then_inc(ring.full(f"dt{i}"), 1)
                        elif s == "mamba_out":
                            pe.wait_ge(sig("yb_ready"), 4)
                            tokens("y3", yb, W["wout"], JI)
                        elif s == "xattn_in":
                            pe.wait_ge(sig("x4_ready"), 2)
                            transposes("x4T", x4)
                            pe.wait_ge(sig("c4_ready"), 16)
                            transposes("c4T", c4)
                            ring.taken(pe, "x4T")
                            project("xq", W["xwq"], 0, bT)
                            ring.taken(pe, "c4T")
                            project("xk", W["xwk"], 0, c4T)
                            tokens("xv", c4T, W["xwv"], DT)
                        elif s.startswith("xattn_s"):
                            u = int(s[7:])
                            g, qt = u // 2, u % 2
                            j, r = g // 2, 64 * (g % 2)
                            if u == 0:
                                ring.taken(pe, "xq")
                                ring.taken(pe, "xk")
                            for n, m0 in (("xSA", 0), ("xSB", 2)):
                                bk = ring.open(pe, f"{n}{u}")
                                for m in range(2):
                                    mm(bk[:, m * T:(m + 1) * T], xqm[r:r + 64, m0 + m, j, qt * P:(qt + 1) * P],
                                       xkT[r:r + 64, j, :], start=True, stop=False)
                                    last = mm(bk[:, m * T:(m + 1) * T], identb[:, :], xmask[:, qt, :],
                                              start=False, stop=True)
                                last.then_inc(ring.full(f"{n}{u}"), 1)
                        elif s.startswith("xattn_t"):
                            u = int(s[7:])
                            ring.taken(pe, f"xSB{u}")
                            for n, k in (("xTA", 0), ("xTB", 1)):
                                bk = ring.open(pe, f"{n}{u}")
                                for m in range(4):
                                    last = pe.transpose(bk[:, m * P:(m + 1) * P],
                                                        xpr[:, u % 2, m * T + k * P:m * T + (k + 1) * P], ident[:, :])
                                last.then_inc(ring.full(f"{n}{u}"), 1)
                        elif s.startswith("xattn_o") and s != "xattn_out":
                            j = int(s[7:])
                            if j == 0:
                                ring.taken(pe, "xv")
                            ring.taken(pe, f"xTA{4 * j + 3}")
                            ring.taken(pe, f"xTB{4 * j + 3}")
                            bk = ring.open(pe, f"xO{j}")
                            for ones in (0, 1):
                                for n, (m, k) in enumerate((m, k) for m in range(2) for k in range(2)):
                                    for i in range(4):
                                        g, hh = i // 2, 2 * (i % 2) + m
                                        head = 8 * j + 4 * g + hh
                                        lh = onesp[:, m, :] if ones else vp[:, k, head, :]
                                        last = mm(bk[32 * i:32 * i + 32, 256 * ones:256 * ones + T], lh,
                                                  xpT[:, g, k, hh, :], start=(n == 0), stop=(n == 3))
                            last.then_inc(ring.full(f"xO{j}"), 1)
                        elif s == "xattn_out":
                            ring.taken(pe, "xO1")
                            tokens("y4", xoT, W["xwo"], DT)
                        elif s == "moe_in":
                            pe.wait_ge(sig("grep_ready"), 2)
                            bk = ring.open(pe, "grow")
                            for t in range(TT):
                                last = pe.transpose(bk[:, t * P:(t + 1) * P], grep[:, t, :], ident[:, :])
                            last.then_inc(ring.full("grow"), 1)
                            pe.wait_ge(sig("perm_ready"), 2)
                            bk = ring.open(pe, "xsel")
                            for d in range(DT):
                                for t in range(TT):
                                    last = mm(bk[:, d * CAP:(d + 1) * CAP], x5[:, t, d * P:(d + 1) * P],
                                              perm[:, t, :], start=(t == 0), stop=(t == TT - 1))
                            last.then_inc(ring.full("xsel"), 1)
                            bk = ring.open(pe, "permT")
                            for t in range(TT):
                                last = pe.transpose(bk[:, t * P:(t + 1) * P], perm[:, t, :], ident[:, :])
                            last.then_inc(ring.full("permT"), 1)
                            ring.taken(pe, "xsel")
                            project("fq", W["fwq"], 0, xselT, n=CAP)
                            project("fk", W["fwk"], 0, xselT, n=CAP)
                            bk = ring.open(pe, "fv")
                            for k in range(DT):
                                last = mm(bk[:, 0:D], xselT[:, k, :], W["fwv"][:, k, :], start=(k == 0),
                                          stop=(k == DT - 1))
                            last.then_inc(ring.full("fv"), 1)
                        elif s.startswith("moe_s"):
                            g = int(s[5:])
                            j, r = g // 2, 64 * (g % 2)
                            if g == 0:
                                ring.taken(pe, "fq")
                                ring.taken(pe, "fk")
                            bk = ring.open(pe, f"fS{g}")
                            for m in range(4):
                                last = mm(bk[:, m * P:(m + 1) * P], xqm[r:r + 64, m, j, 0:CAP],
                                          xkT[r:r + 64, j, 0:CAP], start=True, stop=True)
                            last.then_inc(ring.full(f"fS{g}"), 1)
                        elif s.startswith("moe_t"):
                            g = int(s[5:])
                            ring.taken(pe, f"fS{g}")
                            bk = ring.open(pe, f"fT{g}")
                            for m in range(4):
                                last = pe.transpose(bk[:, m * P:(m + 1) * P], xpr[:, g % 2, m * P:(m + 1) * P],
                                                    ident[:, :])
                            last.then_inc(ring.full(f"fT{g}"), 1)
                        elif s.startswith("moe_o") and s != "moe_out":
                            j = int(s[5:])
                            if j == 0:
                                ring.taken(pe, "fv")
                            ring.taken(pe, f"fT{2 * j + 1}")
                            bk = ring.open(pe, f"fO{j}")
                            for ones in (0, 1):
                                for m in range(2):
                                    for i in range(4):
                                        g, hh = 2 * j + i // 2, 2 * (i % 2) + m
                                        lh = onesp[:, m, :] if ones else vp[:, 0, 4 * g + hh, :]
                                        last = mm(bk[32 * i:32 * i + 32, CAP * ones:CAP * ones + CAP], lh,
                                                  xpT[:, g // 2, g % 2, hh, 0:CAP], start=(m == 0), stop=(m == 1))
                            last.then_inc(ring.full(f"fO{j}"), 1)
                        elif s == "moe_out":
                            ring.taken(pe, "fO1")
                            bk = ring.open(pe, "fo")
                            for k in range(DT):
                                last = mm(bk[:, 0:D], xoT[:, k, 0:CAP], W["fwo"][:, k, :], start=(k == 0),
                                          stop=(k == DT - 1))
                            last.then_inc(ring.full("fo"), 1)
                            ring.taken(pe, "fo")
                            ring.taken(pe, "permT")
                            bk = ring.open(pe, "y5")
                            for t in range(TT):
                                last = mm(bk[:, t * D:(t + 1) * D], permT[:, t, :], fo[:, :], start=True, stop=True)
                            last.then_inc(ring.full("y5"), 1)

                pe.wait_ge(const_ready, 1)
                pe.wait_ge(s_set, 1)
                for d in range(DT):
                    last = pe.transpose(banks[0][:, d * NCOL:(d + 1) * NCOL], cen[:, d * P:(d + 1) * P],
                                        ident[0:NCOL, 0:NCOL])
                last.then_inc(s_set, 1)
                pe.wait_ge(go, 1)
                with pe.Fori(0, NB) as b:
                    run(STEPS_ALL)
                    pe.drain().then_inc(arrived, 1)
                    pe.wait_ge(go, b + 2)

            @block.scalar
            def _(act):
                A = act.activation

                def run(steps):
                    ring = Ring(steps)
                    link = Chain(act, chain["act"])

                    def rstd(ag, ln, rs, eps, stats, ready):
                        act.wait_ge(sig(stats[0]), stats[1])
                        link(A(ln[:, :], ag[:, :, 1], ACT.Ln, bias=epsc[:, eps:eps + 1]))
                        A(rs[:, :], ln[:, :], ACT.Exp, scale=-0.5).then_inc(sig(ready), 1)

                    def copy_out(name, dst, **how):
                        bk = ring.made(act, name)
                        n = 1
                        for w in dst.shape[1:]:
                            n *= w
                        src = bk[:, 0:n]
                        if len(dst.shape) == 3:
                            src = src.rearrange("p (a b) -> p a b", a=dst.shape[1])
                        A(dst, src, ACT.Copy).then_inc(ring.free(name), 1)

                    def softplus_parts(name, i):
                        bk = ring.made(act, name)
                        for m in range(2):
                            c = 2 * i + m
                            A(dtv[:, c, :], bk[:, m * T:(m + 1) * T], ACT.Abs, bias=W["bdt"][:, c:c + 1])
                            last = A(yb[:, c, :], bk[:, m * T:(m + 1) * T], ACT.Relu, bias=W["bdt"][:, c:c + 1])
                        last.then_inc(ring.free(name), 1)

                    for s in steps:
                        if s == "attn0_in":
                            copy_out("x0T", xT[:, :, :])
                            for i in range(2):
                                copy_out(f"k{i}", kT[:, 2 * i:2 * i + 2, :])
                            for t in range(TT):
                                copy_out(f"v{t}", v0[:, t, :])
                        elif s.startswith("attn0_s"):
                            p = int(s[7:])
                            act.wait_ge(sig("attn0_max"), p + 1)
                            if p >= 2:
                                ring.made(act, f"aTB{p - 2}")
                            bA, bB = ring.made(act, f"aSA{p}"), ring.made(act, f"aSB{p}")
                            d = pr[:, p % 2, :]
                            for h in range(2):
                                A(d[:, h * P:(h + 1) * P], bA[:, h * P:(h + 1) * P], ACT.Exp,
                                  bias=nmx[:, p % 2, h:h + 1])
                            A(d[:, T:2 * T], bA[:, T:2 * T], ACT.Exp, bias=nmx[:, p % 2, 2:3])\
                                .then_inc(ring.free(f"aSA{p}"), 1)
                            A(d[:, 2 * T:3 * T], bB[:, 0:T], ACT.Exp, bias=nmx[:, p % 2, 3:4])\
                                .then_inc(ring.free(f"aSB{p}"), 1)
                        elif s.startswith("attn0_t"):
                            p = int(s[7:])
                            if p >= 4:
                                ring.made(act, f"aO{(p - 4) // 2}")
                            copy_out(f"aTB{p}", pT[:, p % 4, 512:768])
                        elif s == "attn0_out":
                            rstd(agF, lnF, rsF, 0, ("statsF", 1), "rstdF")
                        elif s == "mlstm_in":
                            copy_out("cT", cT)
                            ring.taken(act, "gates")
                            link(A(row(2), row(1), ACT.Abs))
                            link(A(row(3), row(2), ACT.Exp, scale=-1.0))
                            A(row(4), row(3), ACT.Ln, bias=1.0).then_inc(sig("lnf"), 1)
                        elif s == "mlstm_rows":
                            copy_out("acol", acol[:, :, :])
                            act.wait_ge(sig("maxd"), 1)
                            A(er[0:8, :], row(7), ACT.Exp, scale=-1.0).then_inc(sig("er_ready"), 1)
                            copy_out("ebc", ebc)
                        elif s.startswith("mlstm_s"):
                            q = int(s[7:])
                            ring.taken(act, "acol")
                            if q >= 2:
                                ring.taken(act, f"mKB{q - 2}")
                            bA = ring.made(act, f"mMA{q}")
                            d = pr[:, q % 2, :]
                            for h in range(2):
                                last = A(d[:, h * T:(h + 1) * T], bA[:, h * T:(h + 1) * T], ACT.Exp,
                                         bias=acol[:, 0, 2 * q + h:2 * q + h + 1])
                            last.then_inc(ring.free(f"mMA{q}"), 1)
                            bB = ring.made(act, f"mMB{q}")
                            for h in range(2):
                                last = A(d[:, 512 + h * P:512 + (h + 1) * P], bB[:, h * P:(h + 1) * P], ACT.Exp,
                                         bias=acol[:, 1, 2 * q + h:2 * q + h + 1])
                            last.then_inc(ring.free(f"mMB{q}"), 1)
                        elif s == "mlstm_norm":
                            ring.taken(act, "mean")
                            A(hsq, hcT, ACT.Square).then_inc(sig("hsq_ready"), 1)
                            bk = ring.made(act, "var")
                            A(hT, bk[:, :].rearrange("p (a b) -> p a b", a=2), ACT.Ln, bias=epsc[:, 1:2])\
                                .then_inc(ring.free("var"), 1)
                            ring.taken(act, "var")
                            A(hT, hT, ACT.Exp, scale=-0.5).then_inc(sig("hrs_ready"), 1)
                            rstd(agF, lnF, rsF, 0, ("statsF", 2), "rstdF")
                        elif s == "ffn0_in":
                            copy_out("x2T", xT[:, :, :])
                            for t in range(TT):
                                last = A(sqj[:, :], x2[:, t, :], ACT.Square, accum_out=s2[:, 0, t:t + 1])
                                if t == 0:
                                    link(last)
                            last.then_inc(sig("ssq_ready"), 1)
                            act.wait_ge(sig("ss_ready"), 1)
                            link(A(s2[:, 2, :], s2[:, 1, :], ACT.Ln, scale=float(2 ** 40)))
                            A(s2[:, 3, :], s2[:, 2, :], ACT.Exp, scale=-0.5).then_inc(sig("rn_ready"), 1)
                            bk = ring.made(act, "hid")
                            A(hidT[:, :], bk[:, 0:T], ACT.Gelu, bias=W["b1"][:, 0:1]).then_inc(ring.free("hid"), 1)
                        elif s == "ffn0_cols":
                            for c in range(4):
                                bk = ring.made(act, f"c{c}")
                                for m in range(2):
                                    last = A(cols[:, 2 * c + m, :], bk[:, m * T:(m + 1) * T], ACT.Gelu,
                                             bias=W["bcols"][:, 2 * c + m:2 * c + m + 1])
                                last.then_inc(ring.free(f"c{c}"), 1)
                        elif s == "ffn0_gate":
                            ring.taken(act, "gate")
                            A(sm[:, 2, :, :], sm[:, 1, :, :], ACT.Exp, scale=-1.0).then_inc(sig("gexp_ready"), 1)
                            act.wait_ge(sig("shifted"), 1)
                            A(sm[:, 6, :, :], sm[:, 5, :, :], ACT.Exp).then_inc(sig("pexp_ready"), 1)
                        elif s == "ffn0_out":
                            rstd(agF, lnF, rsF, 0, ("statsF", 3), "rstdF")
                            rstd(agF, lnF, rsF, 0, ("statsF", 4), "rstdF")
                        elif s == "mamba_in":
                            copy_out("x3T", bT[:, :, :])
                            for i in range(2):
                                copy_out(f"xi{i}", xp[:, 2 * i:2 * i + 2, KC - 1:])
                            for i in range(2):
                                bk = ring.made(act, f"z{i}")
                                v = bk[:, :].rearrange("p (a b) -> p a b", a=2)
                                A(zs[:, 2 * i:2 * i + 2, :], v, ACT.Copy)
                                A(sg[:, 2 * i:2 * i + 2, :], v, ACT.Exp, scale=-1.0).then_inc(ring.free(f"z{i}"), 1)
                            act.wait_ge(sig("conv_ready"), 1)
                            A(dtv[:, :, :], yb[:, :, :], ACT.Exp, scale=-1.0).then_inc(sig("cexp_ready"), 1)
                        elif s == "mamba_dt":
                            copy_out("xdbl", xd[:, :])
                            softplus_parts("dt0", 0)
                            softplus_parts("dt1", 1)
                            ring.taken(act, "dt1")
                            link(A(dtv[:, :, :], dtv[:, :, :], ACT.Exp, scale=-1.0))
                            A(dtv[:, :, :], dtv[:, :, :], ACT.Ln, bias=1.0).then_inc(sig("sp_ready"), 1)
                        elif s.startswith("mamba_u"):
                            u = int(s[7:])
                            ct, nq = u // 4, u % 4
                            if u == 0:
                                act.wait_ge(sig("dt_ready"), 1)
                                act.wait_ge(sig("dA_zeroed"), 2)
                            if u >= 2:
                                act.wait_ge(sig("scanned"), u - 1)
                            for n in range(HN):
                                nn = nq * HN + n
                                last = A(dA[u % 2][:, n, 1:T], dtv[:, ct, 1:T], ACT.Exp, scale=anew[:, ct, nn:nn + 1])
                            last.then_inc(sig("dA_ready"), 1)
                        elif s == "mamba_out":
                            rstd(agB, lnB, rsB, 0, ("statsB", 1), "rstdB")
                        elif s == "xattn_in":
                            copy_out("x4T", bT[:, :, :])
                            copy_out("c4T", c4T)
                            bk = ring.made(act, "xk")
                            for j in range(DT):
                                last = A(xkT[:, j, :], bk[:, j * T:(j + 1) * T], ACT.Identity,
                                         bias=W["xbk"][:, j:j + 1])
                            last.then_inc(ring.free("xk"), 1)
                        elif s.startswith("xattn_s"):
                            u = int(s[7:])
                            act.wait_ge(sig("xattn_max"), u + 1)
                            if u >= 2:
                                ring.made(act, f"xTB{u - 2}")
                            for n, m0 in (("xSA", 0), ("xSB", 2)):
                                bk = ring.made(act, f"{n}{u}")
                                for m in range(2):
                                    last = A(xpr[:, u % 2, (m0 + m) * T:(m0 + m + 1) * T], bk[:, m * T:(m + 1) * T],
                                             ACT.Exp, bias=xnm[:, u % 2, m0 + m:m0 + m + 1])
                                last.then_inc(ring.free(f"{n}{u}"), 1)
                        elif s.startswith("xattn_t"):
                            u = int(s[7:])
                            g, qt = u // 2, u % 2
                            if u >= 4:
                                ring.made(act, "xO0")
                            bk = ring.made(act, f"xTB{u}")
                            A(xpT[:, g % 2, 1, :, qt * P:(qt + 1) * P], bk[:, :].rearrange("p (m q) -> p m q", m=4),
                              ACT.Copy).then_inc(ring.free(f"xTB{u}"), 1)
                        elif s == "xattn_out":
                            rstd(agB, lnB, rsB, 0, ("statsB", 2), "rstdB")
                        elif s == "moe_in":
                            act.wait_ge(sig("fz_ready"), 2)
                            A(gg[:, 1, :], gg[:, 0, :], ACT.Exp, scale=-1.0).then_inc(sig("fexp_ready"), 1)
                            copy_out("grow", grow[:, :])
                            copy_out("xsel", xselT[:, :, :])
                            copy_out("permT", permT[:, :, :])
                            bk = ring.made(act, "fk")
                            A(xkT[:, :, 0:CAP], bk[:, 0:DT * CAP].rearrange("p (j t) -> p j t", j=DT), ACT.Copy)\
                                .then_inc(ring.free("fk"), 1)
                        elif s.startswith("moe_s"):
                            g = int(s[5:])
                            act.wait_ge(sig("moe_max"), g + 1)
                            if g >= 2:
                                ring.made(act, f"fT{g - 2}")
                            bk = ring.made(act, f"fS{g}")
                            for m in range(4):
                                last = A(xpr[:, g % 2, m * P:(m + 1) * P], bk[:, m * P:(m + 1) * P], ACT.Exp,
                                         bias=xnm[:, g % 2, m:m + 1])
                            last.then_inc(ring.free(f"fS{g}"), 1)
                        elif s == "moe_out":
                            copy_out("fo", fo[:, :])
                            rstd(agB, lnB, rsB, 0, ("statsB", 3), "rstdB")

                act.wait_ge(loaded, 16 * NLOAD)
                act.wait_ge(const_ready, 1)
                A(anew[:, :, :], W["alog"][:, :, :], ACT.Exp).then_inc(chain["act"], 1)
                A(junk[0:NCOL, :], cemb, ACT.Square, accum_out=cst[:, 0:1]).then_inc(chain["act"], 1)
                act.wait_ge(chain["act"], 2)
                A(cst[:, 1:2], cst[:, 0:1], ACT.Sqrt).then_inc(chain["act"], 1)
                act.wait_ge(go, 1)
                with act.Fori(0, NB) as b:
                    run(STEPS_ALL)
                    act.drain().then_inc(arrived, 1)
                    act.wait_ge(go, b + 2)

            @block.vector
            def _(dve):
                TS, TTn, STT = dve.tensor_scalar, dve.tensor_tensor, dve.scalar_tensor_tensor

                def over(v, shape):
                    return v.unsqueeze(2).to_broadcast(shape)

                def run(steps):
                    ring = Ring(steps)
                    link = Chain(dve, chain["dve"])
                    count = {"F": 0, "B": 0}

                    def layernorm(half, y, x, ready):
                        st, ag, rs = (stF, agF, rsF) if half == "F" else (stB, agB, rsB)
                        count[half] += 1
                        for t in range(TT):
                            last = dve.bn_stats(st[:, t, :], y[:, t, :])
                        link(last)
                        for t in range(TT):
                            last = dve.bn_aggr(ag[:, t, :], st[:, t, :])
                        last.then_inc(sig("stats" + half), 1)
                        dve.wait_ge(sig("rstd" + half), count[half])
                        for t in range(TT):
                            TS(x[:, t, :], y[:, t, :], ag[:, t, 0:1], rs[:, t:t + 1], ALU.subtract, ALU.mult)\
                                .then_inc(sig(ready), 1)

                    def halves(bk):
                        return bk[:, :].rearrange("p (a b) -> p a b", a=2)

                    def weighted(bk, n, ri, dst, name):
                        link(dve.reciprocal(ri, bk[:, n:2 * n] if n == CAP else bk[:, T:T + n]))
                        TTn(dst, bk[:, 0:n], ri, ALU.mult).then_inc(ring.free(name), 1)

                    def scan_sum(u):
                        ct, nq = u // 4, u % 4
                        dve.wait_ge(sig("hc_ready"), u + 1)
                        v = hs[u % 2].rearrange("p n t -> p t n")
                        if nq == 0:
                            link(dve.reduce_sum(yb[:, ct, :], v, AX.X))
                        else:
                            link(dve.reduce_sum(part[:, u % 2, :], v, AX.X))
                            link(TTn(yb[:, ct, :], yb[:, ct, :], part[:, u % 2, :], ALU.add))

                    for s in steps:
                        if s == "attn0_in":
                            for i in range(2):
                                bk = ring.made(dve, f"q{i}")
                                for h in range(2):
                                    last = TS(qm[:, h, 2 * i:2 * i + 2, :], halves(bk), hmask0[:, h:h + 1], None,
                                              ALU.mult)
                                last.then_inc(ring.free(f"q{i}"), 1)
                        elif s.startswith("attn0_s"):
                            p = int(s[7:])
                            if p >= 2:
                                ring.taken(dve, f"aSB{p - 2}")
                            bk = ring.made(dve, f"aSA{p}")
                            m = nmx[:, p % 2, :]
                            dve.tensor_reduce(m[:, 0:2], bk[:, 0:T].rearrange("p (h k) -> p h k", h=2), AX.X, ALU.max,
                                              negate=True)
                            dve.tensor_reduce(m[:, 2:3], bk[:, T:2 * T], AX.X, ALU.max, negate=True)
                            bk = ring.made(dve, f"aSB{p}")
                            dve.tensor_reduce(m[:, 3:4], bk[:, 0:T], AX.X, ALU.max, negate=True)\
                                .then_inc(sig("attn0_max"), 1)
                        elif s.startswith("attn0_t"):
                            p = int(s[7:])
                            if p >= 4:
                                ring.made(dve, f"aO{(p - 4) // 2}")
                            bk = ring.made(dve, f"aTA{p}")
                            dve.tensor_copy(pT[:, p % 4, 0:512], bk[:, :]).then_inc(ring.free(f"aTA{p}"), 1)
                        elif s.startswith("attn0_o") and s != "attn0_out":
                            j = int(s[7:])
                            weighted(ring.made(dve, f"aO{j}"), T, rinv[:, j % 2, :], oT[:, j, :], f"aO{j}")
                        elif s == "attn0_out":
                            bk = ring.made(dve, "y0")
                            TTn(yF[:, :, :], halves(bk), x0[:, :, :], ALU.add).then_inc(ring.free("y0"), 1)
                            ring.taken(dve, "y0")
                            layernorm("F", yF, x1, "x1_ready")
                        elif s == "mlstm_in":
                            bk = ring.made(dve, "x1T")
                            dve.tensor_copy(xT[:, :, :], halves(bk))
                            for h in range(2):
                                last = TS(xTm[:, h, :, :], halves(bk), hmask0[:, h:h + 1], None, ALU.mult)
                            last.then_inc(ring.free("x1T"), 1)
                            bk = ring.made(dve, "gates")
                            TS(row(0), bk[0:8, 0:T], W["gib"][:, 0:1], None, ALU.add)
                            TS(row(1), bk[0:8, T:2 * T], W["gfb"][:, 0:1], None, ALU.add)\
                                .then_inc(ring.free("gates"), 1)
                            ring.taken(dve, "gates")
                            dve.wait_ge(sig("lnf"), 1)
                            link(STT(row(3), row(1), 0.0, row(4), ALU.min, ALU.subtract))
                            link(dve.tensor_tensor_scan(row(6), ones8[:, :], row(3), 0.0, ALU.mult, ALU.add))
                            TTn(row(5), row(0), row(6), ALU.subtract).then_inc(sig("rows_ready"), 1)
                            dve.wait_ge(sig("rows_ready"), 1)
                            link(dve.tensor_tensor_scan(row(2), row(5), row(5), -3.0e38, ALU.max, ALU.max))
                            TS(nmr[0:8, :], row(2), -1.0, None, ALU.mult).then_inc(sig("nmr_ready"), 1)
                            TTn(row(7), row(6), row(2), ALU.add).then_inc(sig("maxd"), 1)
                        elif s.startswith("mlstm_s"):
                            q = int(s[7:])
                            bk = ring.made(dve, f"mKA{q}")
                            ring.taken(dve, f"mMA{q}")
                            TTn(pT[:, q, 0:512], bk[:, :], pr[:, q % 2, 0:512], ALU.mult)\
                                .then_inc(ring.free(f"mKA{q}"), 1)
                            bk = ring.made(dve, f"mKB{q}")
                            ring.taken(dve, f"mMB{q}")
                            TTn(pT[:, q, 512:768], bk[:, 0:256], pr[:, q % 2, 512:768], ALU.mult)\
                                .then_inc(ring.free(f"mKB{q}"), 1)
                        elif s.startswith("mlstm_o"):
                            j = int(s[7:])
                            bk = ring.made(dve, f"mO{j}")
                            ring.taken(dve, "ebc")
                            r = rinv[:, j, :]
                            link(STT(r, bk[:, T:2 * T], -1.0, ebc[:, j, :], ALU.mult, ALU.max))
                            link(TTn(r, bk[:, T:2 * T], r, ALU.max))
                            link(TS(r, r, 1e-6, None, ALU.add))
                            link(dve.reciprocal(r, r))
                            TTn(hT[:, j, :], bk[:, 0:T], r, ALU.mult).then_inc(ring.free(f"mO{j}"), 1)
                        elif s == "mlstm_norm":
                            bk = ring.made(dve, "mean")
                            ring.taken(dve, "mO1")
                            TTn(hcT, hT, halves(bk), ALU.subtract).then_inc(ring.free("mean"), 1)
                            dve.wait_ge(sig("hrs_ready"), 1)
                            for t in range(2):
                                STT(hnT[:, t, :], hcT[:, t, :], W["onw"][:, t:t + 1], hT[:, t, :], ALU.mult, ALU.mult)\
                                    .then_inc(sig("hnT_ready"), 1)
                            bk = ring.made(dve, "hnT")
                            TTn(yF[:, :, :], halves(bk), x1[:, :, :], ALU.add).then_inc(ring.free("hnT"), 1)
                            ring.taken(dve, "hnT")
                            layernorm("F", yF, x2, "x2_ready")
                        elif s == "ffn0_in":
                            dve.wait_ge(sig("ssq_ready"), 1)
                            TS(s2[:, 1, :], s2[:, 0, :], 1e-24, None, ALU.max).then_inc(sig("ss_ready"), 1)
                            dve.wait_ge(sig("rn_ready"), 1)
                            bk = ring.made(dve, "sim")
                            for t in range(TT):
                                last = TS(sm[:, 0, t, :], bk[:, t * NCOL:(t + 1) * NCOL], s2[:, 3, t:t + 1],
                                          float(2 ** 20), ALU.mult, ALU.mult)
                            last.then_inc(ring.free("sim"), 1)
                        elif s == "ffn0_gate":
                            v = [P, TT, NCOL]
                            bk = ring.made(dve, "gate")
                            TTn(sm[:, 1, :, :], bk[:, 0:TT * NCOL].rearrange("p (t c) -> p t c", t=TT),
                                W["b2r"][:, :].unsqueeze(1).to_broadcast(v), ALU.add).then_inc(ring.free("gate"), 1)
                            dve.wait_ge(sig("gexp_ready"), 1)
                            link(TS(sm[:, 3, :, :], sm[:, 2, :, :], 1.0, None, ALU.add))
                            link(dve.reciprocal(sm[:, 10, :, :], sm[:, 3, :, :]))
                            link(TTn(sm[:, 4, :, :], sm[:, 10, :, :], sm[:, 0, :, :], ALU.add))
                            link(dve.reduce_max(s2[:, 4, :], sm[:, 4, :, :], AX.X))
                            TTn(sm[:, 5, :, :], sm[:, 4, :, :], over(s2[:, 4, :], v), ALU.subtract)\
                                .then_inc(sig("shifted"), 1)
                            link(TTn(sm[:, 7, :, :], sm[:, 4, :, :], over(s2[:, 4, :], v), ALU.is_ge))
                            link(TTn(sm[:, 8, :, :], sm[:, 7, :, :], revc[:, :, :], ALU.mult))
                            link(dve.reduce_max(s2[:, 7, :], sm[:, 8, :, :], AX.X))
                            TTn(ohb[:, :, :], sm[:, 8, :, :], over(s2[:, 7, :], v), ALU.is_equal)\
                                .then_inc(sig("onehot_ready"), 1)
                            dve.wait_ge(sig("pexp_ready"), 1)
                            link(dve.reduce_sum(s2[:, 5, :], sm[:, 6, :, :], AX.X))
                            link(dve.reciprocal(s2[:, 6, :], s2[:, 5, :]))
                        elif s == "ffn0_out":
                            for c in range(4):
                                ring.taken(dve, f"c{c}")
                                bk = ring.made(dve, f"m{c}")
                                TTn(cols[:, 2 * c:2 * c + 2, :], halves(bk), cols[:, 2 * c:2 * c + 2, :], ALU.mult)\
                                    .then_inc(ring.free(f"m{c}"), 1)
                            bk = ring.made(dve, "y2")
                            dve.wait_ge(sig("ffn_base"), 1)
                            for t in range(TT):
                                last = STT(yF[:, t, :], bk[:, t * D:(t + 1) * D], s2[:, 6, t:t + 1], x1[:, t, :],
                                           ALU.mult, ALU.add)
                            last.then_inc(ring.free("y2"), 1)
                            ring.taken(dve, "y2")
                            layernorm("F", yF, x1, "ffn_norm")
                            dve.wait_ge(sig("ffn_norm"), 2)
                            v = [P, TT, D]
                            link(TTn(x1[:, :, :], x1[:, :, :], W["lngr"][:, :].unsqueeze(1).to_broadcast(v), ALU.mult))
                            link(TTn(x1[:, :, :], x1[:, :, :], W["lnbr"][:, :].unsqueeze(1).to_broadcast(v), ALU.add))
                            link(TTn(yF[:, :, :], x1[:, :, :], x2[:, :, :], ALU.add))
                            layernorm("F", yF, x3, "x3_ready")
                        elif s == "mamba_in":
                            ring.taken(dve, "xi1")
                            for ct in range(JI):
                                last = TS(yb[:, ct, :], xp[:, ct, KC - 1:], W["convw"][:, ct, KC - 1:KC],
                                          W["convb"][:, ct:ct + 1], ALU.mult, ALU.add)
                            link(last)
                            for k in range(KC - 1):
                                for ct in range(JI):
                                    last = STT(yb[:, ct, :], xp[:, ct, k:k + T], W["convw"][:, ct, k:k + 1],
                                               yb[:, ct, :], ALU.mult, ALU.add)
                                if k < KC - 2:
                                    link(last)
                            last.then_inc(sig("conv_ready"), 1)
                            ring.taken(dve, "z1")
                            link(TS(sg[:, :, :], sg[:, :, :], 1.0, None, ALU.add))
                            link(dve.reciprocal(sg[:, :, :], sg[:, :, :]))
                            link(TTn(zs[:, :, :], zs[:, :, :], sg[:, :, :], ALU.mult))
                            dve.wait_ge(sig("conv_ready"), 1)
                            dve.wait_ge(sig("cexp_ready"), 1)
                            link(TS(dtv[:, :, :], dtv[:, :, :], 1.0, None, ALU.add))
                            link(dve.reciprocal(dtv[:, :, :], dtv[:, :, :]))
                            TTn(xc[:, :, :], yb[:, :, :], dtv[:, :, :], ALU.mult).then_inc(sig("xc_ready"), 1)
                        elif s == "mamba_dt":
                            dve.wait_ge(sig("sp_ready"), 1)
                            TTn(dtv[:, :, :], dtv[:, :, :], yb[:, :, :], ALU.add).then_inc(sig("dt_ready"), 1)
                            dve.wait_ge(sig("dt_ready"), 1)
                            link(TTn(sg[:, :, :], dtv[:, :, :], xc[:, :, :], ALU.mult))
                        elif s.startswith("mamba_u"):
                            u = int(s[7:])
                            ct, nq = u // 4, u % 4
                            if u == 0:
                                dve.wait_ge(sig("bc_loaded"), 32)
                            v = hs[u % 2]
                            link(TTn(v, bbc[:, nq * HN:(nq + 1) * HN, :],
                                     sg[:, ct, :].unsqueeze(1).to_broadcast([P, HN, T]), ALU.mult))
                            dve.wait_ge(sig("dA_ready"), u + 1)
                            flat = v.rearrange("p n t -> p (n t)")
                            dve.tensor_tensor_scan(flat, dA[u % 2].rearrange("p n t -> p (n t)"), flat, 0.0, ALU.mult,
                                                   ALU.add).then_inc(sig("scanned"), 1)
                            if u >= 1:
                                scan_sum(u - 1)
                        elif s == "mamba_out":
                            scan_sum(JI * NS // HN - 1)
                            for ct in range(JI):
                                last = STT(yb[:, ct, :], xc[:, ct, :], W["dp"][:, ct:ct + 1], yb[:, ct, :], ALU.mult,
                                           ALU.add)
                            link(last)
                            for ct in range(JI):
                                TTn(yb[:, ct, :], yb[:, ct, :], zs[:, ct, :], ALU.mult).then_inc(sig("yb_ready"), 1)
                            bk = ring.made(dve, "y3")
                            TTn(yB[:, :, :], halves(bk), x3[:, :, :], ALU.add).then_inc(ring.free("y3"), 1)
                            ring.taken(dve, "y3")
                            layernorm("B", yB, x4, "x4_ready")
                        elif s == "xattn_in":
                            bk = ring.made(dve, "xq")
                            for m in range(4):
                                for j in range(DT):
                                    last = TS(xqm[:, m, j, :], bk[:, j * T:(j + 1) * T], W["xbq"][:, j:j + 1],
                                              hmask1[:, m:m + 1], ALU.add, ALU.mult)
                            last.then_inc(ring.free("xq"), 1)
                            bk = ring.made(dve, "xv")
                            dve.wait_ge(sig("vp_zeroed"), 1)
                            for t in range(TT):
                                src = bk[:, t * D:(t + 1) * D].rearrange("p (h o d) -> p h o d", o=2, d=16)
                                bias = W["xbvr"][:, :].rearrange("p (h o d) -> p h o d", o=2, d=16)
                                dst = vp[:, t, :, :].rearrange("p (h o) d -> p h o d", o=2)
                                for o in range(2):
                                    last = TTn(dst[:, :, o, 16 * o:16 * o + 16], src[:, :, o, :], bias[:, :, o, :],
                                               ALU.add)
                            last.then_inc(ring.free("xv"), 1)
                        elif s.startswith("xattn_s"):
                            u = int(s[7:])
                            if u >= 2:
                                ring.taken(dve, f"xSB{u - 2}")
                            for n, m0 in (("xSA", 0), ("xSB", 2)):
                                bk = ring.made(dve, f"{n}{u}")
                                last = dve.tensor_reduce(xnm[:, u % 2, m0:m0 + 2], halves(bk), AX.X, ALU.max,
                                                         negate=True)
                            last.then_inc(sig("xattn_max"), 1)
                        elif s.startswith("xattn_t"):
                            u = int(s[7:])
                            g, qt = u // 2, u % 2
                            if u >= 4:
                                ring.made(dve, "xO0")
                            bk = ring.made(dve, f"xTA{u}")
                            dve.tensor_copy(xpT[:, g % 2, 0, :, qt * P:(qt + 1) * P],
                                            bk[:, :].rearrange("p (m q) -> p m q", m=4))\
                                .then_inc(ring.free(f"xTA{u}"), 1)
                        elif s.startswith("xattn_o") and s != "xattn_out":
                            j = int(s[7:])
                            weighted(ring.made(dve, f"xO{j}"), T, xri[:, j, :], xoT[:, j, :], f"xO{j}")
                        elif s == "xattn_out":
                            bk = ring.made(dve, "y4")
                            dve.wait_ge(sig("xattn_base"), 1)
                            TTn(yB[:, :, :], halves(bk), yB[:, :, :], ALU.add).then_inc(ring.free("y4"), 1)
                            ring.taken(dve, "y4")
                            layernorm("B", yB, x5, "x5_ready")
                        elif s == "moe_in":
                            dve.wait_ge(sig("x5_ready"), 2)
                            for t in range(TT):
                                STT(junk[:, :], x5[:, t, :], 1.0, W["wgr"][:, :], ALU.mult, ALU.mult,
                                    accum_out=gg[:, 0, t:t + 1]).then_inc(sig("fz_ready"), 1)
                                dve.wait_ge(sig("fz_ready"), t + 1)
                            dve.wait_ge(sig("fexp_ready"), 1)
                            link(TS(gg[:, 2, :], gg[:, 1, :], 1.0, None, ALU.add))
                            link(dve.reciprocal(gg[:, 3, :], gg[:, 2, :]))
                            for t in range(TT):
                                dve.tensor_copy(grep[:, t, :], gg[:, 3, t:t + 1].to_broadcast([P, P]))\
                                    .then_inc(sig("grep_ready"), 1)
                            ring.taken(dve, "grow")
                            for t in range(TT):
                                g = gg[:, 3, t:t + 1]
                                link(TS(junk[:, :], grow[:, :], g, None, ALU.is_gt, ALU.add,
                                        accum_out=gg[:, 4, t:t + 1]))
                                link(STT(junk[:, :], grow[:, :], g, lower[:, t, :], ALU.is_equal, ALU.mult,
                                         accum_out=gg[:, 5, t:t + 1]))
                            link(TTn(gg[:, 6, :], gg[:, 4, :], gg[:, 5, :], ALU.add))
                            for t in range(TT):
                                TS(perm[:, t, :], iota[:, :], gg[:, 6, t:t + 1], None, ALU.is_equal)\
                                    .then_inc(sig("perm_ready"), 1)
                            bk = ring.made(dve, "fq")
                            for m in range(4):
                                last = TS(xqm[:, m, :, 0:CAP], bk[:, 0:DT * CAP].rearrange("p (j t) -> p j t", j=DT),
                                          hmask1[:, m:m + 1], None, ALU.mult)
                            last.then_inc(ring.free("fq"), 1)
                            bk = ring.made(dve, "fv")
                            src = bk[:, 0:D].rearrange("p (h o d) -> p h o d", o=2, d=16)
                            dst = vp[:, 0, :, :].rearrange("p (h o) d -> p h o d", o=2)
                            for o in range(2):
                                last = dve.tensor_copy(dst[:, :, o, 16 * o:16 * o + 16], src[:, :, o, :])
                            last.then_inc(ring.free("fv"), 1)
                        elif s.startswith("moe_s"):
                            g = int(s[5:])
                            if g >= 2:
                                ring.taken(dve, f"fS{g - 2}")
                            bk = ring.made(dve, f"fS{g}")
                            dve.tensor_reduce(xnm[:, g % 2, 0:4], bk[:, :].rearrange("p (m k) -> p m k", m=4), AX.X,
                                              ALU.max, negate=True).then_inc(sig("moe_max"), 1)
                        elif s.startswith("moe_t"):
                            g = int(s[5:])
                            bk = ring.made(dve, f"fT{g}")
                            dve.tensor_copy(xpT[:, g // 2, g % 2, :, 0:CAP],
                                            bk[:, :].rearrange("p (m q) -> p m q", m=4))\
                                .then_inc(ring.free(f"fT{g}"), 1)
                        elif s.startswith("moe_o") and s != "moe_out":
                            j = int(s[5:])
                            weighted(ring.made(dve, f"fO{j}"), CAP, xri[:, j, 0:CAP], xoT[:, j, 0:CAP], f"fO{j}")
                        elif s == "moe_out":
                            bk = ring.made(dve, "y5")
                            for t in range(TT):
                                last = STT(yB[:, t, :], bk[:, t * D:(t + 1) * D], gg[:, 3, t:t + 1], x5[:, t, :],
                                           ALU.mult, ALU.add)
                            last.then_inc(ring.free("y5"), 1)
                            ring.taken(dve, "y5")
                            layernorm("B", yB, x6, "x6_ready")

                link = Chain(dve, chain["dve"])
                dve.wait_ge(loaded, 16 * NLOAD)
                dve.wait_ge(const_ready, 1)
                dve.wait_ge(chain["act"], 3)
                link(TS(anew[:, :, :], anew[:, :, :], -1.0, None, ALU.mult))
                link(TS(cst[:, 2:3], cst[:, 1:2], 1e-12, None, ALU.max))
                link(dve.reciprocal(cst[:, 3:4], cst[:, 2:3]))
                TS(cen, cemb, cst[:, 3:4], None, ALU.mult).then_inc(s_set, 1)
                dve.tensor_copy(gwc[:, 0:2, :], W["gw"][:, 0:2, :])
                link(TTn(gwc[:, 2:4, :], W["gw"][:, 2:4, :], W["gw"][:, 4:6, :], ALU.add))
                link(dve.tensor_copy(maskf, maski))
                link(TS(xmask[:, :, :], maskf, 0.0, MASKED, ALU.is_equal, ALU.mult))
                dve.wait_ge(s_set, 2)
                dve.tensor_copy(cenT[:, :, :], banks[0][:, 0:DT * NCOL].rearrange("p (d c) -> p d c", d=DT))\
                    .then_inc(s_set, 1)
                dve.wait_ge(go, 1)
                with dve.Fori(0, NB) as b:
                    run(STEPS_ALL)
                    dve.drain().then_inc(arrived, 1)
                    dve.wait_ge(go, b + 2)

            @block.gpsimd
            def _(pool):
                def run(steps):
                    for s in steps:
                        if s == "ffn0_out":
                            pool.wait_ge(sig("x2_ready"), 2)
                            pool.tensor_tensor(x1[:, :, :], x2[:, :, :],
                                               W["pbr"][:, :].unsqueeze(1).to_broadcast([P, TT, D]), ALU.add)\
                                .then_inc(sig("ffn_base"), 1)
                            pool.wait_ge(sig("onehot_ready"), 1)
                            pool.tensor_copy(ohx[:, :, :, :].rearrange("p t c n -> p (t c) n"),
                                             ohb[:, :, :].rearrange("p t c -> p (t c)").unsqueeze(2)
                                             .to_broadcast([P, TT * NCOL, NNEU])).then_inc(sig("onehot_wide"), 1)
                        elif s == "mamba_in":
                            pool.wait_ge(sig("x3_ready"), 2)
                            for i in range(2):
                                pool.memset(dA[i][:, :, 0:1], 0.0).then_inc(sig("dA_zeroed"), 1)
                        elif s.startswith("mamba_u"):
                            u = int(s[7:])
                            nq = u % 4
                            pool.wait_ge(sig("scanned"), u + 1)
                            pool.tensor_tensor(hs[u % 2], hs[u % 2], cbc[:, nq * HN:(nq + 1) * HN, :], ALU.mult)\
                                .then_inc(sig("hc_ready"), 1)
                        elif s == "xattn_in":
                            pool.wait_ge(sig("x4_ready"), 2)
                            pool.memset(vp[:, :, :, :], 0.0).then_inc(sig("vp_zeroed"), 1)
                            pool.tensor_tensor(yB[:, :, :], x4[:, :, :],
                                               W["xbor"][:, :].unsqueeze(1).to_broadcast([P, TT, D]), ALU.add)\
                                .then_inc(sig("xattn_base"), 1)

                n = [0]

                def step(ins):
                    n[0] += 1
                    ins.then_inc(chain["pool"], 1)
                    pool.wait_ge(chain["pool"], n[0])

                for v, val in ((ident, 0.0), (triq, 0.0), (trik, 0.0), (lower, 1.0), (onesv, 1.0), (onesp, 0.0),
                               (blk, 0.0), (selh, 0.0), (sele, 0.0), (hmask0, 0.0), (ones8, 1.0), (nmr, 0.0),
                               (er, 0.0), (xp, 0.0), (blk16, 1.0)):
                    last = pool.memset(v[:] if len(v.shape) < 3 else v[:, :, :], val)
                pool.memset(epsc[:, 0:1], 1e-5)
                pool.memset(epsc[:, 1:2], 1e-6)
                step(pool.memset(cst[:, :], 0.0))
                step(pool.affine_select(out=ident[:, :], in_=ident[:, :], compare_op=ALU.not_equal, fill=1.0, base=0,
                                        pattern=[[-1, P]], channel_multiplier=1))
                step(pool.tensor_copy(identb[:, :], ident[:, :]))
                step(pool.affine_select(out=triq[:, :], in_=triq[:, :], compare_op=ALU.is_ge, fill=MASKED, base=0,
                                        pattern=[[-1, P]], channel_multiplier=1))
                step(pool.affine_select(out=trik[:, :], in_=trik[:, :], compare_op=ALU.is_ge, fill=MASKED, base=0,
                                        pattern=[[1, P]], channel_multiplier=-1))
                step(pool.affine_select(out=lower[:, :, :], in_=lower[:, :, :], compare_op=ALU.is_gt, fill=0.0, base=0,
                                        pattern=[[P, TT], [-1, T]], channel_multiplier=1))
                step(pool.affine_select(out=selh[:, :, :], in_=selh[:, :, :], compare_op=ALU.not_equal, fill=1.0,
                                        base=0, pattern=[[-1, NH_M], [0, P]], channel_multiplier=1))
                step(pool.affine_select(out=sele[:, :, :].rearrange("p t (h c) -> p t h c", c=32),
                                        in_=sele[:, :, :].rearrange("p t (h c) -> p t h c", c=32),
                                        compare_op=ALU.not_equal, fill=1.0, base=0,
                                        pattern=[[-4, 2], [-1, 4], [0, 32]], channel_multiplier=1))
                step(pool.affine_select(out=blk16[:, :], in_=blk16[:, :], compare_op=ALU.is_ge, fill=0.0, base=0,
                                        pattern=[[-16, 8]], channel_multiplier=1))
                step(pool.affine_select(out=blk16[:, :], in_=blk16[:, :], compare_op=ALU.is_ge, fill=0.0, base=15,
                                        pattern=[[16, 8]], channel_multiplier=-1))
                step(pool.tensor_tensor(hmask1[:, :], blk16[:, 0:4], blk16[:, 4:8], ALU.add))
                step(pool.tensor_scalar(hmask1[:, :], hmask1[:, :], 16 ** -0.5, None, ALU.mult))
                for i in range(4):
                    step(pool.memset(blk[32 * i:32 * i + 32, 32 * i:32 * i + 32], 1.0 / 32))
                    step(pool.memset(hmask0[32 * i:32 * i + 32, i % 2:i % 2 + 1], 32 ** -0.5))
                for o in range(2):
                    pool.memset(onesp[:, o, 16 * o:16 * o + 16], 1.0)
                pool.iota(iota[:, :], pattern=[[1, P]], base=0, channel_multiplier=0,
                          allow_small_or_imprecise_dtypes=True)
                pool.iota(revc[:, :, :], pattern=[[0, TT], [-1, NCOL]], base=NCOL, channel_multiplier=0,
                          allow_small_or_imprecise_dtypes=True).then_inc(const_ready, 1)
                pool.wait_ge(const_ready, 1)
                pool.wait_ge(go, 1)
                with pool.Fori(0, NB) as b:
                    run(STEPS_ALL)
                    pool.drain().then_inc(arrived, 1)
                    pool.wait_ge(go, b + 2)

            @block.sync
            def _(sp):
                def tiles(v):
                    return v.rearrange("b (t p) d -> p (b t) d", p=P)

                def run(steps, b):
                    for s in steps:
                        if s == "attn0_in":
                            sp.dma_start(x0[:, :, :], tiles(a["x"][bass.ds(b, 1), :, :])).then_inc(sig("x0_ready"), 16)
                        elif s == "mlstm_in":
                            sp.wait_ge(sig("attn0_max"), 8)
                            sp.dma_start(cF, tiles(a["ctx"][bass.ds(b, 1), :, :])).then_inc(sig("cF_ready"), 16)
                        elif s == "mamba_dt":
                            sp.wait_ge(bank_free[RING.at["xdbl"] % NBANK], RING.at["xdbl"] // NBANK + 1)
                            sp.dma_start(scratch[0, :, :], xd[B_ROW:B_ROW + NS, :]).then_inc(sig("bc_stored"), 16)
                            sp.dma_start(scratch[1, :, :], xd[C_ROW:C_ROW + NS, :]).then_inc(sig("bc_stored"), 16)
                            sp.wait_ge(sig("bc_stored"), 32)
                            for i, v in enumerate((bbc, cbc)):
                                sp.dma_start(v, scratch[i:i + 1, :, :].to_broadcast([P, NS, T]))\
                                    .then_inc(sig("bc_loaded"), 16)
                        elif s == "xattn_in":
                            sp.wait_ge(sig("x4_ready"), 2)
                            sp.dma_start(c4, tiles(a["ctx"][bass.ds(b, 1), :, :])).then_inc(sig("c4_ready"), 16)
                        elif s == "moe_out":
                            sp.wait_ge(sig("x6_ready"), 2)
                            sp.dma_start(tiles(out[bass.ds(b, 1), :, :]), x6[:, :, :]).then_inc(stored, 16)

                RING = Ring(STEPS_ALL)
                for n in W:
                    if n in ROWS:
                        sp.dma_start(W[n][:, :], a[n].to_broadcast([P, ROWS[n]])).then_inc(loaded, 16)
                    elif n != "cemb":
                        v = W[n]
                        sp.dma_start(v[:, :] if len(v.shape) == 2 else v[:, :, :], a[n]).then_inc(loaded, 16)
                sp.dma_start(cemb, a["cemb"]).then_inc(loaded, 16)
                sp.dma_start(maski, a["mask"]).then_inc(loaded, 16)
                sp.wait_ge(loaded, 16 * NLOAD)
                sp.wait_ge(s_set, 3)
                run_clear(sp)
                sp.sem_inc(go, 1)
                with sp.Fori(0, NB) as b:
                    run(STEPS_ALL, b)
                    sp.wait_ge(arrived, 4)
                    run_clear(sp)
                    sp.wait_ge(stored, b * 16 + 16)
                    sp.sem_inc(go, 1)


_OUT = ((NB, T, D), "float32")


def _layout(i):
    import numpy as np

    def f(n):
        return np.asarray(i[n])

    def kt(w):
        return np.ascontiguousarray(w.reshape(-1, P, w.shape[1]).transpose(1, 0, 2))

    def col(v):
        return np.ascontiguousarray(v.reshape(-1, P).T)

    def gates(w):
        return w

    wx = np.zeros((DI, P), np.float32)
    xw = f("L1_attn_x_proj_w").T
    wx[:, 0:16], wx[:, B_ROW:B_ROW + NS], wx[:, C_ROW:C_ROW + NS] = xw[:, 0:16], xw[:, 16:32], xw[:, 32:48]
    wdt = np.zeros((P, DI), np.float32)
    wdt[0:16] = f("L1_attn_dt_proj_w").T
    gw = np.concatenate([f("L0_xattn_igate_kernel"), f("L0_xattn_fgate_kernel")], axis=1)
    wc = f("L0_ffn_W_cols").transpose(1, 0, 2).reshape(D, NCOL * NNEU)
    return {
        "x": f("x"), "ctx": f("ctx_1024"), "mask": kt(f("mask_1x1xSxS2_ik0").reshape(T, T)),
        "wq0": kt(f("L0_attn_wq").T), "wk0": kt(f("L0_attn_wk").T), "wv0": kt(f("L0_attn_wv").T),
        "wo0": kt(f("L0_attn_wo").T), "gw": kt(gw), "w1": kt(f("L0_ffn_gate_w1")), "w2": f("L0_ffn_gate_w2"),
        "wcols": kt(wc), "wproj": kt(f("L0_ffn_proj_w")), "win": kt(f("L1_attn_in_proj_w").T), "wx": kt(wx),
        "wdt": wdt, "wout": kt(f("L1_attn_out_proj_w").T), "xwq": kt(f("L1_xattn_Wq")), "xwk": kt(f("L1_xattn_Wk")),
        "xwv": kt(f("L1_xattn_Wv")), "xwo": kt(f("L1_xattn_Wo")), "fwq": kt(f("L1_ffn_Wq")), "fwk": kt(f("L1_ffn_Wk")),
        "fwv": kt(f("L1_ffn_Wv")), "fwo": kt(f("L1_ffn_Wo")), "onw": col(f("L0_xattn_outnorm_weight").reshape(-1)),
        "b1": col(f("L0_ffn_gate_b1")), "bcols": col(f("L0_ffn_b_cols").reshape(-1)),
        "convw": kt(f("L1_attn_conv_w")), "convb": col(f("L1_attn_conv_b")), "bdt": col(f("L1_attn_dt_proj_b")),
        "alog": kt(f("L1_attn_A_log")), "dp": col(f("L1_attn_Dp")), "xbq": col(f("L1_xattn_bq")),
        "xbk": col(f("L1_xattn_bk")), "gib": f("L0_xattn_igate_bias").reshape(8, 1),
        "gfb": f("L0_xattn_fgate_bias").reshape(8, 1), "cemb": f("L0_ffn_col_emb"),
        "b2r": f("L0_ffn_gate_b2").reshape(1, -1), "pbr": f("L0_ffn_proj_b").reshape(1, -1),
        "lngr": f("L0_ffn_ln_g").reshape(1, -1), "lnbr": f("L0_ffn_ln_b").reshape(1, -1),
        "xbvr": f("L1_xattn_bv").reshape(1, -1), "xbor": f("L1_xattn_bo").reshape(1, -1),
        "wgr": f("L1_ffn_Wg").reshape(1, -1),
    }


def kernel(**inputs):
    import numpy as np
    import concourse.bacc as bacc
    from concourse.bass_utils import run_bass_kernel_spmd

    nc = bacc.Bacc("TRN2", target_bir_lowering=False, num_devices=1)
    arrays, aps = {}, {}
    for name, v in _layout(inputs).items():
        v = np.ascontiguousarray(v)
        arrays[f"in_{name}"] = v
        aps[name] = nc.dram_tensor(f"in_{name}", v.shape, mybir.dt.from_np(v.dtype), kind="ExternalInput").ap()
    out = nc.dram_tensor("out_0", _OUT[0], mybir.dt.float32, kind="ExternalOutput").ap()
    build(nc, aps, out)
    r = run_bass_kernel_spmd(nc, [arrays], core_ids=[0])
    return r.results[0]["out_0"]
```

```python
import concourse.bass as bass
from concourse import mybir
from contextlib import ExitStack

NB, T, D, P = 32, 256, 256, 128
TT, DT = T // P, D // P
QKV0, HD0 = 512, 32
J0 = QKV0 // P
NH_M, HD_M = 8, 32
HID, NCOL, NNEU = 128, 16, 64
CM = NCOL * NNEU // P
DI, NS, KC = 512, 16, 4
JI = DI // P
HN = 4
B_ROW, C_ROW = 32, 64
CAP = T // 2
NBANK = 8
LOG_EXP = "natural_log_exp_and_others"
MASKED = -float(2 ** 126)

FILLS = {
    "attn0_in": ["x0T", "q0", "q1", "k0", "k1", "v0", "v1"],
    "mlstm_in": ["x1T", "cT", "gates"],
    "mlstm_rows": ["acol", "ebc"],
    "mlstm_norm": ["mean", "var", "hnT"],
    "ffn0_in": ["x2T", "hid", "sim"],
    "ffn0_gate": ["gate"],
    "ffn0_cols": ["c0", "c1", "c2", "c3"],
    "ffn0_out": ["m0", "m1", "m2", "m3", "y2"],
    "mamba_in": ["x3T", "xi0", "xi1", "z0", "z1"],
    "mamba_dt": ["xdbl", "dt0", "dt1"],
    "mamba_out": ["y3"],
    "xattn_in": ["x4T", "c4T", "xq", "xk", "xv"],
    "xattn_out": ["y4"],
    "moe_in": ["grow", "xsel", "permT", "fq", "fk", "fv"],
    "moe_out": ["fo", "y5"],
}
for _p in range(8):
    FILLS[f"attn0_s{_p}"] = [f"aSA{_p}", f"aSB{_p}"]
    FILLS[f"attn0_t{_p}"] = [f"aTA{_p}", f"aTB{_p}"]
for _j in range(4):
    FILLS[f"attn0_o{_j}"] = [f"aO{_j}"]
    FILLS[f"mlstm_s{_j}"] = [f"mMA{_j}", f"mMB{_j}", f"mKA{_j}", f"mKB{_j}"]
for _j in range(2):
    FILLS[f"mlstm_o{_j}"] = [f"mO{_j}"]
    FILLS[f"xattn_o{_j}"] = [f"xO{_j}"]
    FILLS[f"moe_o{_j}"] = [f"fO{_j}"]
FILLS["attn0_out"] = ["y0"]
for _g in range(8):
    FILLS[f"xattn_s{_g}"] = [f"xSA{_g}", f"xSB{_g}"]
    FILLS[f"xattn_t{_g}"] = [f"xTA{_g}", f"xTB{_g}"]
for _g in range(4):
    FILLS[f"moe_s{_g}"] = [f"fS{_g}"]
    FILLS[f"moe_t{_g}"] = [f"fT{_g}"]

FRONT = (["attn0_in", "attn0_s0"]
         + [s for p in range(8) for s in ([f"attn0_s{p + 1}"] if p < 7 else [])
            + [f"attn0_t{p}"] + ([f"attn0_o{p // 2}"] if p % 2 else [])]
         + ["attn0_out", "mlstm_in", "mlstm_rows", "mlstm_s0", "mlstm_s1", "mlstm_o0",
            "mlstm_s2", "mlstm_s3", "mlstm_o1", "mlstm_norm",
            "ffn0_in", "ffn0_cols", "ffn0_gate", "ffn0_out"])
BACK = (["mamba_in", "mamba_dt"] + [f"mamba_u{u}" for u in range(JI * NS // HN)] + ["mamba_out",
        "xattn_in", "xattn_s0"]
        + [s for g in range(8) for s in ([f"xattn_s{g + 1}"] if g < 7 else [])
           + [f"xattn_t{g}"] + ([f"xattn_o{g // 4}"] if g % 4 == 3 else [])]
        + ["xattn_out", "moe_in", "moe_s0", "moe_s1", "moe_t0", "moe_s2", "moe_t1", "moe_o0",
           "moe_s3", "moe_t2", "moe_t3", "moe_o1", "moe_out"])


def _weave(front, back):
    out, i, j = [], 0, 0
    wf, wb = sum(map(_weight, front)), sum(map(_weight, back))
    f = b = 0.0
    while i < len(front) or j < len(back):
        if j == len(back) or (i < len(front) and f / wf <= b / wb):
            f += _weight(front[i])
            out.append(front[i])
            i += 1
        else:
            b += _weight(back[j])
            out.append(back[j])
            j += 1
    return out


def _weight(step):
    for start, w in (("attn0_in", 14), ("attn0_s", 3), ("attn0_t", 2), ("attn0_out", 9), ("attn0_o", 2),
                     ("mlstm_in", 12), ("mlstm_rows", 4), ("mlstm_s", 5), ("mlstm_o", 3), ("mlstm_norm", 12),
                     ("ffn0_in", 9), ("ffn0_cols", 8), ("ffn0_gate", 6), ("ffn0_out", 24),
                     ("mamba_in", 16), ("mamba_dt", 14), ("mamba_u", 5), ("mamba_out", 12),
                     ("xattn_in", 12), ("xattn_s", 3), ("xattn_t", 2), ("xattn_out", 8), ("xattn_o", 4),
                     ("moe_in", 14), ("moe_s", 2), ("moe_t", 1), ("moe_out", 9), ("moe_o", 2)):
        if step.startswith(start):
            return w
    raise KeyError(step)


BOTH = _weave(FRONT, BACK)


def build(nc, a, out):
    f32, bf16, i32 = mybir.dt.float32, mybir.dt.bfloat16, mybir.dt.int32
    ALU, ACT, AX = mybir.AluOpType, mybir.ActivationFunctionType, mybir.AxisListType
    ctx = ExitStack()
    with ctx:
        def sb(name, shape, dt=f32):
            return ctx.enter_context(nc.sbuf_tensor(name, shape, dt))

        def sem(name):
            return ctx.enter_context(nc.semaphore(name))

        W = {}
        for n, shp in (("wq0", [P, DT, QKV0]), ("wk0", [P, DT, QKV0]), ("wv0", [P, DT, QKV0]), ("wo0", [P, J0, D]),
                       ("gw", [P, 6, 16]), ("w1", [P, DT, HID]), ("w2", [P, NCOL]), ("wcols", [P, DT, NCOL * NNEU]),
                       ("wproj", [P, CM, D]), ("win", [P, DT, 2 * DI]), ("wx", [P, JI, P]), ("wdt", [P, DI]),
                       ("wout", [P, JI, D]), ("xwq", [P, DT, D]), ("xwk", [P, DT, D]), ("xwv", [P, DT, D]),
                       ("xwo", [P, DT, D]), ("fwq", [P, DT, D]), ("fwk", [P, DT, D]), ("fwv", [P, DT, D]),
                       ("fwo", [P, DT, D]),
                       ("onw", [P, 2]), ("b1", [P, 1]), ("bcols", [P, CM]), ("convw", [P, JI, KC]), ("convb", [P, JI]),
                       ("bdt", [P, JI]), ("alog", [P, JI, NS]), ("dp", [P, JI]), ("xbq", [P, DT]), ("xbk", [P, DT]),
                       ("gib", [8, 1]), ("gfb", [8, 1])):
            W[n] = sb(n, shp)
        ROWS = {"b2r": NCOL, "pbr": D, "lngr": D, "lnbr": D, "xbvr": D, "xbor": D, "wgr": D}
        for n, w in ROWS.items():
            W[n] = sb(n, [P, w])

        ident, identb = sb("ident", [P, P]), sb("identb", [P, P], bf16)
        triq = sb("triq", [P, P], bf16)
        trik = sb("trik", [P, P], bf16)
        lower = sb("lower", [P, TT, T])
        onesv = sb("onesv", [P, 32])
        onesp = sb("onesp", [P, 2, 32])
        blk = sb("blk", [P, P])
        selh = sb("selh", [P, NH_M, P])
        sele = sb("sele", [P, 2, P])
        hmask0 = sb("hmask0", [P, 2])
        hmask1 = sb("hmask1", [P, 4])
        iota = sb("iota", [P, P])
        revc = sb("revc", [P, TT, NCOL])
        ones8 = sb("ones8", [8, T])
        xmask = sb("xmask", [P, TT, T], bf16)
        anew = sb("anew", [P, JI, NS])
        cst = sb("cst", [NCOL, 4])
        cenT = sb("cenT", [P, DT, NCOL])
        gwc = sb("gwc", [P, 4, 16])
        epsc = sb("epsc", [P, 2])
        blk16 = sb("blk16", [P, 8])

        def arena(name, size):
            whole, top = sb(name, [P, size]), [0]

            def room(*shape, at=None):
                n = 1
                for w in shape:
                    n *= w
                o = top[0] if at is None else at
                top[0] = o + n
                assert top[0] <= size, (name, top[0])
                return whole[:, o:o + n]

            return room

        room = arena("front", 11 * 1024)
        qm = room(2, J0, T).rearrange("p (a j t) -> p a j t", a=2, j=J0)
        kT = room(J0, T)
        ohx = kT.bitcast(bf16).rearrange("p (t c n) -> p t c n", t=TT, c=NCOL)
        kT = kT.rearrange("p (j t) -> p j t", j=J0)
        v0 = room(TT, QKV0).rearrange("p (t n) -> p t n", t=TT)
        pr = room(2, 768)
        hidT, sqj = pr[:, 0:T], pr[:, T:T + D]
        pr = pr.rearrange("p (s n) -> p s n", s=2)
        pT = room(4, 768).rearrange("p (s n) -> p s n", s=4)
        oT = room(J0, T).rearrange("p (j t) -> p j t", j=J0)
        rinv = room(2, T).rearrange("p (s t) -> p s t", s=2)
        cF = room(TT, D).rearrange("p (t d) -> p t d", t=TT)
        cT = room(DT, T).rearrange("p (d t) -> p d t", d=DT)
        xTm = qm[:, :, 0:2, :]
        ebc, hT, hcT, hsq, hnT = oT[:, 2:4, :], oT[:, 0:2, :], kT[:, 0:2, :], kT[:, 2:4, :], rinv
        cols = qm.rearrange("p a j t -> p (a j) t")
        v0r = v0.rearrange("p t (r n) -> p (t r) n", r=2)

        def row(i):
            return kT[0:8, i, :] if i < 4 else v0r[0:8, i - 4, :]

        room = arena("back", 13 * 1024)
        bq, cq, dA, hs = ([room(HN, T).rearrange("p (n t) -> p n t", n=HN) for _ in range(2)] for _ in range(4))
        xc, sg, zs, dtv, yb = (room(JI, T).rearrange("p (j t) -> p j t", j=JI) for _ in range(5))
        xp = room(JI, KC - 1 + T, at=6 * HN * T).rearrange("p (j t) -> p j t", j=JI)
        c4 = room(TT, D, at=0).rearrange("p (t d) -> p t d", t=TT)
        c4T = room(DT, T).rearrange("p (d t) -> p d t", d=DT)
        xqm = room(4, DT, T).rearrange("p (m j t) -> p m j t", m=4, j=DT)
        xkT = room(DT, T).rearrange("p (j t) -> p j t", j=DT)
        vp = room(TT, 16, 32).rearrange("p (t h d) -> p t h d", t=TT, h=16)
        xpr = room(2, 1024).rearrange("p (s n) -> p s n", s=2)
        xpT = room(2, 2, 4, T).rearrange("p (s k h q) -> p s k h q", s=2, k=2, h=4)
        xoT = room(DT, T).rearrange("p (j t) -> p j t", j=DT)
        perm = room(TT, CAP).rearrange("p (t c) -> p t c", t=TT)
        permT, grep = (room(TT, P).rearrange("p (t c) -> p t c", t=TT) for _ in range(2))
        xselT = room(DT, CAP).rearrange("p (t c) -> p t c", t=DT)
        fo, grow, junk = room(D), room(T), room(D)
        maski = room(TT, T, at=0).bitcast(i32).rearrange("p (t k) -> p t k", t=TT)
        maskf = room(TT, T).rearrange("p (t k) -> p t k", t=TT)
        cemb, cen = room(D)[0:NCOL, :], room(D)[0:NCOL, :]

        x0, x1, x3 = sb("x0", [P, TT, D]), sb("x1", [P, TT, D]), sb("x3", [P, TT, D])
        x2 = x0
        xT = sb("xT", [P, DT, T])
        nmx = sb("nmx", [P, 2, 4])
        yF = sb("yF", [P, TT, D])
        stF, agF, lnF, rsF = sb("stF", [P, TT, 6]), sb("agF", [P, TT, 2]), sb("lnF", [P, TT]), sb("rsF", [P, TT])
        nmr, er = sb("nmr", [P, T]), sb("er", [P, T])
        acol = sb("acol", [P, TT, 8])
        sm = sb("sm", [P, 12, TT, NCOL])
        s2 = sb("s2", [P, 8, TT])
        ohb = sb("ohb", [P, TT, NCOL], bf16)

        x4, x5 = sb("x4", [P, TT, D]), sb("x5", [P, TT, D])
        x6 = x4
        bT = sb("bT", [P, DT, T])
        xd, x3b = sb("xd", [P, T]), sb("x3b", [P, TT, D])
        xnm, xri = sb("xnm", [P, 2, 4]), sb("xri", [P, 2, T])
        yB = sb("yB", [P, TT, D])
        stB, agB, lnB, rsB = sb("stB", [P, TT, 6]), sb("agB", [P, TT, 2]), sb("lnB", [P, TT]), sb("rsB", [P, TT])
        gg = sb("gg", [P, 8, TT])

        scratch = nc.dram_tensor("bc_rows", (2, NS, T), f32, kind="Internal").ap()

        banks = [ctx.enter_context(nc.psum_tensor(f"bank{i}", [P, 512], f32)) for i in range(NBANK)]

        loaded, const_ready, go, stored = sem("loaded"), sem("const_ready"), sem("go"), sem("stored")
        s_set = sem("set_up")
        arrived = sem("arrived")
        bank_full = [sem(f"bank_full{i}") for i in range(NBANK)]
        bank_free = [sem(f"bank_free{i}") for i in range(NBANK)]
        chain = {n: sem(f"{n}_done") for n in ("dve", "act", "pool")}
        signals = {}
        last_sem = [chain["pool"].num]

        def sig(name):
            if name not in signals:
                signals[name] = sem(name)
                assert signals[name].num == last_sem[0] + 1 or not signals, name
                last_sem[0] = signals[name].num
            return signals[name]

        class Ring:

            def __init__(self, steps):
                self.at = {}
                for s in steps:
                    for f in FILLS.get(s, []):
                        self.at[f] = len(self.at)

            def open(self, pe, name):
                n = self.at[name]
                if n >= NBANK:
                    pe.wait_ge(bank_free[n % NBANK], n // NBANK)
                return banks[n % NBANK]

            def full(self, name):
                return bank_full[self.at[name] % NBANK]

            def made(self, eng, name):
                n = self.at[name]
                eng.wait_ge(bank_full[n % NBANK], n // NBANK + 1)
                return banks[n % NBANK]

            def taken(self, eng, name):
                n = self.at[name]
                eng.wait_ge(bank_free[n % NBANK], n // NBANK + 1)

            def free(self, name):
                return bank_free[self.at[name] % NBANK]

        class Chain:

            def __init__(self, eng, s):
                self.eng, self.s, self.n = eng, s, 0

            def __call__(self, ins):
                self.n += 1
                ins.then_inc(self.s, 1)
                self.eng.wait_ge(self.s, self.n)

        NLOAD = len(W) + 2

        def run_clear(sp):
            sp.sem_clear(range(arrived.num, last_sem[0] + 1))

        with nc.Block() as block:

            @block.tensor
            def _(pe):
                mm = pe.matmul

                def run(steps):
                    ring = Ring(steps)

                    def transposes(name, src, kt=TT):
                        bk = ring.open(pe, name)
                        for d in range(DT):
                            for t in range(TT):
                                last = pe.transpose(bk[:, d * T + t * P:d * T + t * P + P],
                                                    src[:, t, d * P:d * P + P], ident[:, :])
                        last.then_inc(ring.full(name), 1)

                    def project(name, w, m0, src, n=T, nm=2, kt=DT):
                        bk = ring.open(pe, name)
                        for m in range(nm):
                            for k in range(kt):
                                last = mm(bk[:, m * n:(m + 1) * n], w[:, k, (m0 + m) * P:(m0 + m + 1) * P],
                                          src[:, k, 0:n], start=(k == 0), stop=(k == kt - 1))
                        last.then_inc(ring.full(name), 1)

                    def tokens(name, src, w, kt):
                        bk = ring.open(pe, name)
                        for t in range(TT):
                            for k in range(kt):
                                last = mm(bk[:, t * D:(t + 1) * D], src[:, k, t * P:(t + 1) * P], w[:, k, :],
                                          start=(k == 0), stop=(k == kt - 1))
                        last.then_inc(ring.full(name), 1)

                    for s in steps:
                        if s == "attn0_in":
                            pe.wait_ge(sig("x0_ready"), 16)
                            transposes("x0T", x0)
                            ring.taken(pe, "x0T")
                            for n, w in (("q", "wq0"), ("k", "wk0")):
                                for i in range(2):
                                    project(f"{n}{i}", W[w], 2 * i, xT)
                            for t in range(TT):
                                bk = ring.open(pe, f"v{t}")
                                for k in range(DT):
                                    last = mm(bk[:, :], xT[:, k, t * P:(t + 1) * P], W["wv0"][:, k, :],
                                              start=(k == 0), stop=(k == DT - 1))
                                last.then_inc(ring.full(f"v{t}"), 1)
                        elif s.startswith("attn0_s"):
                            p = int(s[7:])
                            if p == 0:
                                ring.taken(pe, "q1")
                                ring.taken(pe, "k1")
                            j, r = p // 2, 64 * (p % 2)
                            A = ring.open(pe, f"aSA{p}")
                            for h in range(2):
                                mm(A[:, h * P:(h + 1) * P], qm[r:r + 64, h, j, 0:P], kT[r:r + 64, j, 0:P],
                                   start=True, stop=False)
                                mm(A[:, h * P:(h + 1) * P], identb[:, :], triq[:, :], start=False, stop=True)
                            for h in range(2):
                                bk, c = (A, 256) if h == 0 else (ring.open(pe, f"aSB{p}"), 0)
                                mm(bk[:, c:c + T], qm[r:r + 64, h, j, P:T], kT[r:r + 64, j, :], start=True, stop=False)
                                mm(bk[:, c + P:c + T], identb[:, :], triq[:, :], start=False,
                                   stop=True).then_inc(ring.full(f"aSA{p}" if h == 0 else f"aSB{p}"), 1)
                        elif s.startswith("attn0_t"):
                            p = int(s[7:])
                            ring.taken(pe, f"aSB{p}")
                            A = ring.open(pe, f"aTA{p}")
                            src = pr[:, p % 2, :]
                            for h in range(2):
                                pe.transpose(A[:, h * T:h * T + P], src[:, h * P:(h + 1) * P], ident[:, :])
                                last = pe.transpose(A[:, h * T + P:(h + 1) * T], src[:, T + h * T:T + h * T + P],
                                                    ident[:, :])
                            last.then_inc(ring.full(f"aTA{p}"), 1)
                            Bk = ring.open(pe, f"aTB{p}")
                            for h in range(2):
                                last = pe.transpose(Bk[:, h * P:(h + 1) * P],
                                                    src[:, T + h * T + P:T + (h + 1) * T], ident[:, :])
                            last.then_inc(ring.full(f"aTB{p}"), 1)
                        elif s.startswith("attn0_o") and s != "attn0_out":
                            j = int(s[7:])
                            if j == 0:
                                ring.taken(pe, "v1")
                            ring.taken(pe, f"aTA{2 * j + 1}")
                            ring.taken(pe, f"aTB{2 * j + 1}")
                            bk = ring.open(pe, f"aO{j}")
                            for ones in (0, 1):
                                for k in range(2):
                                    for i in range(4):
                                        sl, h = (2 * j + i // 2) % 4, i % 2
                                        rhs = pT[:, sl, h * T:(h + 1) * T] if k == 0 else \
                                            pT[:, sl, 512 + h * P:512 + (h + 1) * P]
                                        c = 256 * ones + (P if k else 0)
                                        lh = onesv[:, :] if ones else v0[:, k, 128 * j + 32 * i:128 * j + 32 * i + 32]
                                        last = mm(bk[32 * i:32 * i + 32, c:256 * ones + T], lh, rhs,
                                                  start=(k == 0), stop=(k == 1))
                            last.then_inc(ring.full(f"aO{j}"), 1)
                        elif s == "attn0_out":
                            ring.taken(pe, "aO3")
                            tokens("y0", oT, W["wo0"], J0)
                        elif s == "mlstm_in":
                            pe.wait_ge(sig("cF_ready"), 16)
                            pe.wait_ge(sig("x1_ready"), 2)
                            transposes("x1T", x1)
                            transposes("cT", cF)
                            ring.taken(pe, "x1T")
                            ring.taken(pe, "cT")
                            bk = ring.open(pe, "gates")
                            for g in range(2):
                                for k in range(4):
                                    last = mm(bk[0:8, g * T:(g + 1) * T], gwc[:, k, g * 8:g * 8 + 8],
                                              (xT if k < 2 else cT)[:, k % 2, :], start=(k == 0), stop=(k == 3))
                            last.then_inc(ring.full("gates"), 1)
                        elif s == "mlstm_rows":
                            pe.wait_ge(sig("rows_ready"), 1)
                            bk = ring.open(pe, "acol")
                            for t in range(TT):
                                last = pe.transpose(bk[:, t * 8:t * 8 + 8], row(5)[:, t * P:(t + 1) * P],
                                                    ident[0:8, 0:8])
                            last.then_inc(ring.full("acol"), 1)
                            pe.wait_ge(sig("er_ready"), 1)
                            bk = ring.open(pe, "ebc")
                            for t in range(2):
                                last = mm(bk[:, t * T:(t + 1) * T], sele[:, t, :], er[:, :], start=True, stop=True)
                            last.then_inc(ring.full("ebc"), 1)
                        elif s.startswith("mlstm_s"):
                            q = int(s[7:])
                            j, r = q // 2, 64 * (q % 2)
                            if q == 0:
                                pe.wait_ge(sig("nmr_ready"), 1)
                            A = ring.open(pe, f"mMA{q}")
                            for h in range(2):
                                mm(A[:, h * T:(h + 1) * T], selh[:, 2 * q + h, :], nmr[:, :], start=True, stop=False)
                                last = mm(A[:, h * T:h * T + P], identb[:, :], trik[:, :], start=False, stop=True)
                            last.then_inc(ring.full(f"mMA{q}"), 1)
                            Bk = ring.open(pe, f"mMB{q}")
                            for h in range(2):
                                mm(Bk[:, h * P:(h + 1) * P], selh[:, 2 * q + h, :], nmr[:, P:T], start=True, stop=False)
                                last = mm(Bk[:, h * P:(h + 1) * P], identb[:, :], trik[:, :], start=False, stop=True)
                            last.then_inc(ring.full(f"mMB{q}"), 1)
                            A = ring.open(pe, f"mKA{q}")
                            for h in range(2):
                                last = mm(A[:, h * T:(h + 1) * T], cT[r:r + 64, j, 0:P], xTm[r:r + 64, h, j, :],
                                          start=True, stop=True)
                            last.then_inc(ring.full(f"mKA{q}"), 1)
                            Bk = ring.open(pe, f"mKB{q}")
                            for h in range(2):
                                last = mm(Bk[:, h * P:(h + 1) * P], cT[r:r + 64, j, P:T], xTm[r:r + 64, h, j, P:T],
                                          start=True, stop=True)
                            last.then_inc(ring.full(f"mKB{q}"), 1)
                        elif s.startswith("mlstm_o"):
                            j = int(s[7:])
                            ring.taken(pe, f"mKB{2 * j + 1}")
                            bk = ring.open(pe, f"mO{j}")
                            for ones in (0, 1):
                                for k in range(2):
                                    for i in range(4):
                                        sl, h = 2 * j + i // 2, i % 2
                                        rhs = pT[:, sl, h * T:(h + 1) * T] if k == 0 else \
                                            pT[:, sl, 512 + h * P:512 + (h + 1) * P]
                                        c = 256 * ones + (P if k else 0)
                                        lh = onesv[:, :] if ones else cF[:, k, 128 * j + 32 * i:128 * j + 32 * i + 32]
                                        last = mm(bk[32 * i:32 * i + 32, c:256 * ones + T], lh, rhs,
                                                  start=(k == 0), stop=(k == 1))
                            last.then_inc(ring.full(f"mO{j}"), 1)
                        elif s == "mlstm_norm":
                            for n, src in (("mean", hT), ("var", hsq)):
                                if n == "mean":
                                    ring.taken(pe, "mO1")
                                else:
                                    pe.wait_ge(sig("hsq_ready"), 1)
                                bk = ring.open(pe, n)
                                for t in range(2):
                                    last = mm(bk[:, t * T:(t + 1) * T], blk[:, :], src[:, t, :], start=True, stop=True)
                                last.then_inc(ring.full(n), 1)
                            pe.wait_ge(sig("hnT_ready"), 2)
                            bk = ring.open(pe, "hnT")
                            for t in range(TT):
                                for d in range(DT):
                                    last = pe.transpose(bk[:, t * D + d * P:t * D + d * P + P],
                                                        hnT[:, d, t * P:(t + 1) * P], ident[:, :])
                            last.then_inc(ring.full("hnT"), 1)
                        elif s == "ffn0_in":
                            pe.wait_ge(sig("x2_ready"), 2)
                            transposes("x2T", x2)
                            ring.taken(pe, "x2T")
                            project("hid", W["w1"], 0, xT, nm=1)
                            bk = ring.open(pe, "sim")
                            for t in range(TT):
                                for k in range(DT):
                                    last = mm(bk[:, t * NCOL:(t + 1) * NCOL], xT[:, k, t * P:(t + 1) * P],
                                              cenT[:, k, :], start=(k == 0), stop=(k == DT - 1))
                            last.then_inc(ring.full("sim"), 1)
                        elif s == "ffn0_cols":
                            for c in range(4):
                                project(f"c{c}", W["wcols"], 2 * c, xT)
                        elif s == "ffn0_gate":
                            ring.taken(pe, "hid")
                            bk = ring.open(pe, "gate")
                            for t in range(TT):
                                last = mm(bk[:, t * NCOL:(t + 1) * NCOL], hidT[:, t * P:(t + 1) * P], W["w2"][:, :],
                                          start=True, stop=True)
                            last.then_inc(ring.full("gate"), 1)
                        elif s == "ffn0_out":
                            pe.wait_ge(sig("onehot_wide"), 1)
                            for c in range(4):
                                bk = ring.open(pe, f"m{c}")
                                for m in range(2):
                                    for t in range(TT):
                                        cc = 2 * (2 * c + m)
                                        lh = ohx[:, t, cc:cc + 2, :].rearrange("p c n -> p (c n)")
                                        last = mm(bk[:, m * T + t * P:m * T + (t + 1) * P], lh, identb[:, :],
                                                  start=True, stop=True)
                                last.then_inc(ring.full(f"m{c}"), 1)
                            ring.taken(pe, "m3")
                            tokens("y2", cols, W["wproj"], CM)
                        elif s == "mamba_in":
                            pe.wait_ge(sig("x3b_ready"), 1)
                            transposes("x3T", x3b)
                            ring.taken(pe, "x3T")
                            for i in range(2):
                                project(f"xi{i}", W["win"], 2 * i, bT)
                            for i in range(2):
                                project(f"z{i}", W["win"], 4 + 2 * i, bT)
                        elif s == "mamba_dt":
                            pe.wait_ge(sig("xc_ready"), 1)
                            project("xdbl", W["wx"], 0, xc, nm=1, kt=JI)
                            ring.taken(pe, "xdbl")
                            for i in range(2):
                                bk = ring.open(pe, f"dt{i}")
                                for m in range(2):
                                    c = (2 * i + m) * P
                                    last = mm(bk[:, m * T:(m + 1) * T], W["wdt"][:, c:c + P], xd[:, :],
                                              start=True, stop=True)
                                last.then_inc(ring.full(f"dt{i}"), 1)
                        elif s == "mamba_out":
                            pe.wait_ge(sig("yb_ready"), 4)
                            tokens("y3", yb, W["wout"], JI)
                        elif s == "xattn_in":
                            pe.wait_ge(sig("x4_ready"), 2)
                            transposes("x4T", x4)
                            pe.wait_ge(sig("c4_ready"), 16)
                            transposes("c4T", c4)
                            ring.taken(pe, "x4T")
                            project("xq", W["xwq"], 0, bT)
                            ring.taken(pe, "c4T")
                            project("xk", W["xwk"], 0, c4T)
                            tokens("xv", c4T, W["xwv"], DT)
                        elif s.startswith("xattn_s"):
                            u = int(s[7:])
                            g, qt = u // 2, u % 2
                            j, r = g // 2, 64 * (g % 2)
                            if u == 0:
                                ring.taken(pe, "xq")
                                ring.taken(pe, "xk")
                            for n, m0 in (("xSA", 0), ("xSB", 2)):
                                bk = ring.open(pe, f"{n}{u}")
                                for m in range(2):
                                    mm(bk[:, m * T:(m + 1) * T], xqm[r:r + 64, m0 + m, j, qt * P:(qt + 1) * P],
                                       xkT[r:r + 64, j, :], start=True, stop=False)
                                    last = mm(bk[:, m * T:(m + 1) * T], identb[:, :], xmask[:, qt, :],
                                              start=False, stop=True)
                                last.then_inc(ring.full(f"{n}{u}"), 1)
                        elif s.startswith("xattn_t"):
                            u = int(s[7:])
                            ring.taken(pe, f"xSB{u}")
                            for n, k in (("xTA", 0), ("xTB", 1)):
                                bk = ring.open(pe, f"{n}{u}")
                                for m in range(4):
                                    last = pe.transpose(bk[:, m * P:(m + 1) * P],
                                                        xpr[:, u % 2, m * T + k * P:m * T + (k + 1) * P], ident[:, :])
                                last.then_inc(ring.full(f"{n}{u}"), 1)
                        elif s.startswith("xattn_o") and s != "xattn_out":
                            j = int(s[7:])
                            if j == 0:
                                ring.taken(pe, "xv")
                            ring.taken(pe, f"xTA{4 * j + 3}")
                            ring.taken(pe, f"xTB{4 * j + 3}")
                            bk = ring.open(pe, f"xO{j}")
                            for ones in (0, 1):
                                for n, (m, k) in enumerate((m, k) for m in range(2) for k in range(2)):
                                    for i in range(4):
                                        g, hh = i // 2, 2 * (i % 2) + m
                                        head = 8 * j + 4 * g + hh
                                        lh = onesp[:, m, :] if ones else vp[:, k, head, :]
                                        last = mm(bk[32 * i:32 * i + 32, 256 * ones:256 * ones + T], lh,
                                                  xpT[:, g, k, hh, :], start=(n == 0), stop=(n == 3))
                            last.then_inc(ring.full(f"xO{j}"), 1)
                        elif s == "xattn_out":
                            ring.taken(pe, "xO1")
                            tokens("y4", xoT, W["xwo"], DT)
                        elif s == "moe_in":
                            pe.wait_ge(sig("grep_ready"), 2)
                            bk = ring.open(pe, "grow")
                            for t in range(TT):
                                last = pe.transpose(bk[:, t * P:(t + 1) * P], grep[:, t, :], ident[:, :])
                            last.then_inc(ring.full("grow"), 1)
                            pe.wait_ge(sig("perm_ready"), 2)
                            bk = ring.open(pe, "xsel")
                            for d in range(DT):
                                for t in range(TT):
                                    last = mm(bk[:, d * CAP:(d + 1) * CAP], x5[:, t, d * P:(d + 1) * P],
                                              perm[:, t, :], start=(t == 0), stop=(t == TT - 1))
                            last.then_inc(ring.full("xsel"), 1)
                            bk = ring.open(pe, "permT")
                            for t in range(TT):
                                last = pe.transpose(bk[:, t * P:(t + 1) * P], perm[:, t, :], ident[:, :])
                            last.then_inc(ring.full("permT"), 1)
                            ring.taken(pe, "xsel")
                            project("fq", W["fwq"], 0, xselT, n=CAP)
                            project("fk", W["fwk"], 0, xselT, n=CAP)
                            bk = ring.open(pe, "fv")
                            for k in range(DT):
                                last = mm(bk[:, 0:D], xselT[:, k, :], W["fwv"][:, k, :], start=(k == 0),
                                          stop=(k == DT - 1))
                            last.then_inc(ring.full("fv"), 1)
                        elif s.startswith("moe_s"):
                            g = int(s[5:])
                            j, r = g // 2, 64 * (g % 2)
                            if g == 0:
                                ring.taken(pe, "fq")
                                ring.taken(pe, "fk")
                            bk = ring.open(pe, f"fS{g}")
                            for m in range(4):
                                last = mm(bk[:, m * P:(m + 1) * P], xqm[r:r + 64, m, j, 0:CAP],
                                          xkT[r:r + 64, j, 0:CAP], start=True, stop=True)
                            last.then_inc(ring.full(f"fS{g}"), 1)
                        elif s.startswith("moe_t"):
                            g = int(s[5:])
                            ring.taken(pe, f"fS{g}")
                            bk = ring.open(pe, f"fT{g}")
                            for m in range(4):
                                last = pe.transpose(bk[:, m * P:(m + 1) * P], xpr[:, g % 2, m * P:(m + 1) * P],
                                                    ident[:, :])
                            last.then_inc(ring.full(f"fT{g}"), 1)
                        elif s.startswith("moe_o") and s != "moe_out":
                            j = int(s[5:])
                            if j == 0:
                                ring.taken(pe, "fv")
                            ring.taken(pe, f"fT{2 * j + 1}")
                            bk = ring.open(pe, f"fO{j}")
                            for ones in (0, 1):
                                for m in range(2):
                                    for i in range(4):
                                        g, hh = 2 * j + i // 2, 2 * (i % 2) + m
                                        lh = onesp[:, m, :] if ones else vp[:, 0, 4 * g + hh, :]
                                        last = mm(bk[32 * i:32 * i + 32, CAP * ones:CAP * ones + CAP], lh,
                                                  xpT[:, g // 2, g % 2, hh, 0:CAP], start=(m == 0), stop=(m == 1))
                            last.then_inc(ring.full(f"fO{j}"), 1)
                        elif s == "moe_out":
                            ring.taken(pe, "fO1")
                            bk = ring.open(pe, "fo")
                            for k in range(DT):
                                last = mm(bk[:, 0:D], xoT[:, k, 0:CAP], W["fwo"][:, k, :], start=(k == 0),
                                          stop=(k == DT - 1))
                            last.then_inc(ring.full("fo"), 1)
                            ring.taken(pe, "fo")
                            ring.taken(pe, "permT")
                            bk = ring.open(pe, "y5")
                            for t in range(TT):
                                last = mm(bk[:, t * D:(t + 1) * D], permT[:, t, :], fo, start=True, stop=True)
                            last.then_inc(ring.full("y5"), 1)

                pe.wait_ge(const_ready, 1)
                pe.wait_ge(s_set, 1)
                for d in range(DT):
                    last = pe.transpose(banks[0][:, d * NCOL:(d + 1) * NCOL], cen[:, d * P:(d + 1) * P],
                                        ident[0:NCOL, 0:NCOL])
                last.then_inc(s_set, 1)
                pe.wait_ge(go, 1)
                run(FRONT)
                pe.drain().then_inc(arrived, 1)
                pe.wait_ge(go, 2)
                with pe.Fori(1, NB) as b:
                    run(BOTH)
                    pe.drain().then_inc(arrived, 1)
                    pe.wait_ge(go, b + 2)
                run(BACK)
                pe.drain().then_inc(arrived, 1)

            @block.scalar
            def _(act):
                A = act.activation

                def run(steps):
                    ring = Ring(steps)
                    link = Chain(act, chain["act"])

                    def rstd(ag, ln, rs, eps, stats, ready):
                        act.wait_ge(sig(stats[0]), stats[1])
                        link(A(ln[:, :], ag[:, :, 1], ACT.Ln, bias=epsc[:, eps:eps + 1]))
                        A(rs[:, :], ln[:, :], ACT.Exp, scale=-0.5).then_inc(sig(ready), 1)

                    def copy_out(name, dst, **how):
                        bk = ring.made(act, name)
                        n = 1
                        for w in dst.shape[1:]:
                            n *= w
                        src = bk[:, 0:n]
                        if len(dst.shape) == 3:
                            src = src.rearrange("p (a b) -> p a b", a=dst.shape[1])
                        A(dst, src, ACT.Copy).then_inc(ring.free(name), 1)

                    def inverse(name, n, ri):
                        bk = ring.made(act, name)
                        link(A(ri, bk[:, n:2 * n], ACT.Ln))
                        A(ri, ri, ACT.Exp, scale=-1.0).then_inc(sig("inverse_" + name[0]), 1)

                    def softplus_parts(name, i):
                        bk = ring.made(act, name)
                        for m in range(2):
                            c = 2 * i + m
                            A(dtv[:, c, :], bk[:, m * T:(m + 1) * T], ACT.Abs, bias=W["bdt"][:, c:c + 1])
                            last = A(yb[:, c, :], bk[:, m * T:(m + 1) * T], ACT.Relu, bias=W["bdt"][:, c:c + 1])
                        last.then_inc(ring.free(name), 1)

                    for s in steps:
                        if s == "attn0_in":
                            copy_out("x0T", xT[:, :, :])
                            for i in range(2):
                                copy_out(f"k{i}", kT[:, 2 * i:2 * i + 2, :])
                            for t in range(TT):
                                copy_out(f"v{t}", v0[:, t, :])
                        elif s.startswith("attn0_s"):
                            p = int(s[7:])
                            act.wait_ge(sig("attn0_max"), p + 1)
                            if p >= 2:
                                ring.made(act, f"aTB{p - 2}")
                            bA, bB = ring.made(act, f"aSA{p}"), ring.made(act, f"aSB{p}")
                            d = pr[:, p % 2, :]
                            for h in range(2):
                                A(d[:, h * P:(h + 1) * P], bA[:, h * P:(h + 1) * P], ACT.Exp,
                                  bias=nmx[:, p % 2, h:h + 1])
                            A(d[:, T:2 * T], bA[:, T:2 * T], ACT.Exp, bias=nmx[:, p % 2, 2:3])\
                                .then_inc(ring.free(f"aSA{p}"), 1)
                            A(d[:, 2 * T:3 * T], bB[:, 0:T], ACT.Exp, bias=nmx[:, p % 2, 3:4])\
                                .then_inc(ring.free(f"aSB{p}"), 1)
                        elif s.startswith("attn0_t"):
                            p = int(s[7:])
                            if p >= 4:
                                ring.made(act, f"aO{(p - 4) // 2}")
                            copy_out(f"aTB{p}", pT[:, p % 4, 512:768])
                        elif s.startswith("attn0_o") and s != "attn0_out":
                            j = int(s[7:])
                            if j >= 2:
                                ring.taken(act, f"aO{j - 2}")
                            inverse(f"aO{j}", T, rinv[:, j % 2, :])
                        elif s == "attn0_out":
                            rstd(agF, lnF, rsF, 0, ("statsF", 1), "rstdF")
                        elif s == "mlstm_in":
                            copy_out("cT", cT)
                            ring.taken(act, "gates")
                            link(A(row(2), row(1), ACT.Abs))
                            link(A(row(3), row(2), ACT.Exp, scale=-1.0))
                            A(row(4), row(3), ACT.Ln, bias=1.0).then_inc(sig("lnf"), 1)
                        elif s == "mlstm_rows":
                            copy_out("acol", acol[:, :, :])
                            act.wait_ge(sig("maxd"), 1)
                            A(er[0:8, :], row(7), ACT.Exp, scale=-1.0).then_inc(sig("er_ready"), 1)
                            copy_out("ebc", ebc)
                        elif s.startswith("mlstm_s"):
                            q = int(s[7:])
                            ring.taken(act, "acol")
                            if q >= 2:
                                ring.taken(act, f"mKB{q - 2}")
                            bA = ring.made(act, f"mMA{q}")
                            d = pr[:, q % 2, :]
                            for h in range(2):
                                last = A(d[:, h * T:(h + 1) * T], bA[:, h * T:(h + 1) * T], ACT.Exp,
                                         bias=acol[:, 0, 2 * q + h:2 * q + h + 1])
                            last.then_inc(ring.free(f"mMA{q}"), 1)
                            bB = ring.made(act, f"mMB{q}")
                            for h in range(2):
                                last = A(d[:, 512 + h * P:512 + (h + 1) * P], bB[:, h * P:(h + 1) * P], ACT.Exp,
                                         bias=acol[:, 1, 2 * q + h:2 * q + h + 1])
                            last.then_inc(ring.free(f"mMB{q}"), 1)
                        elif s == "mlstm_norm":
                            ring.taken(act, "mean")
                            A(hsq, hcT, ACT.Square).then_inc(sig("hsq_ready"), 1)
                            bk = ring.made(act, "var")
                            A(hT, bk[:, :].rearrange("p (a b) -> p a b", a=2), ACT.Ln, bias=epsc[:, 1:2])\
                                .then_inc(ring.free("var"), 1)
                            ring.taken(act, "var")
                            A(hT, hT, ACT.Exp, scale=-0.5).then_inc(sig("hrs_ready"), 1)
                            rstd(agF, lnF, rsF, 0, ("statsF", 2), "rstdF")
                        elif s == "ffn0_in":
                            copy_out("x2T", xT[:, :, :])
                            for t in range(TT):
                                last = A(sqj[:, :], x2[:, t, :], ACT.Square, accum_out=s2[:, 0, t:t + 1])
                                if t == 0:
                                    link(last)
                            last.then_inc(sig("ssq_ready"), 1)
                            act.wait_ge(sig("ss_ready"), 1)
                            link(A(s2[:, 2, :], s2[:, 1, :], ACT.Ln, scale=float(2 ** 40)))
                            A(s2[:, 3, :], s2[:, 2, :], ACT.Exp, scale=-0.5).then_inc(sig("rn_ready"), 1)
                            bk = ring.made(act, "hid")
                            A(hidT[:, :], bk[:, 0:T], ACT.Gelu, bias=W["b1"][:, 0:1]).then_inc(ring.free("hid"), 1)
                        elif s == "ffn0_cols":
                            for c in range(4):
                                bk = ring.made(act, f"c{c}")
                                for m in range(2):
                                    last = A(cols[:, 2 * c + m, :], bk[:, m * T:(m + 1) * T], ACT.Gelu,
                                             bias=W["bcols"][:, 2 * c + m:2 * c + m + 1])
                                last.then_inc(ring.free(f"c{c}"), 1)
                            act.preload_act_table_set(LOG_EXP)
                        elif s == "ffn0_gate":
                            ring.taken(act, "gate")
                            A(sm[:, 2, :, :], sm[:, 1, :, :], ACT.Exp, scale=-1.0).then_inc(sig("gexp_ready"), 1)
                            act.wait_ge(sig("shifted"), 1)
                            A(sm[:, 6, :, :], sm[:, 5, :, :], ACT.Exp).then_inc(sig("pexp_ready"), 1)
                        elif s == "ffn0_out":
                            rstd(agF, lnF, rsF, 0, ("statsF", 3), "rstdF")
                            rstd(agF, lnF, rsF, 0, ("statsF", 4), "rstdF")
                        elif s == "mamba_in":
                            copy_out("x3T", bT[:, :, :])
                            for i in range(2):
                                copy_out(f"xi{i}", xp[:, 2 * i:2 * i + 2, KC - 1:])
                            for i in range(2):
                                bk = ring.made(act, f"z{i}")
                                A(zs[:, 2 * i:2 * i + 2, :], bk[:, :].rearrange("p (a b) -> p a b", a=2), ACT.Silu)\
                                    .then_inc(ring.free(f"z{i}"), 1)
                            act.wait_ge(sig("conv_ready"), 1)
                            A(xc, yb, ACT.Silu).then_inc(sig("xc_ready"), 1)
                            act.preload_act_table_set(LOG_EXP)
                        elif s == "mamba_dt":
                            copy_out("xdbl", xd[:, :])
                            softplus_parts("dt0", 0)
                            softplus_parts("dt1", 1)
                            ring.taken(act, "dt1")
                            link(A(dtv, dtv, ACT.Exp, scale=-1.0))
                            A(dtv, dtv, ACT.Ln, bias=1.0).then_inc(sig("sp_ready"), 1)
                        elif s.startswith("mamba_u"):
                            u = int(s[7:])
                            nq, ct = u // JI, u % JI
                            if u == 0:
                                act.wait_ge(sig("dt_ready"), 1)
                                act.wait_ge(sig("dA_zeroed"), 2)
                            if u >= 2:
                                act.wait_ge(sig("scanned"), u - 1)
                            for n in range(HN):
                                nn = nq * HN + n
                                last = A(dA[u % 2][:, n, 1:T], dtv[:, ct, 1:T], ACT.Exp, scale=anew[:, ct, nn:nn + 1])
                            last.then_inc(sig("dA_ready"), 1)
                        elif s == "mamba_out":
                            rstd(agB, lnB, rsB, 0, ("statsB", 1), "rstdB")
                        elif s == "xattn_in":
                            copy_out("x4T", bT[:, :, :])
                            copy_out("c4T", c4T)
                            bk = ring.made(act, "xk")
                            for j in range(DT):
                                last = A(xkT[:, j, :], bk[:, j * T:(j + 1) * T], ACT.Identity,
                                         bias=W["xbk"][:, j:j + 1])
                            last.then_inc(ring.free("xk"), 1)
                        elif s.startswith("xattn_s"):
                            u = int(s[7:])
                            act.wait_ge(sig("xattn_max"), u + 1)
                            if u >= 2:
                                ring.made(act, f"xTB{u - 2}")
                            for n, m0 in (("xSA", 0), ("xSB", 2)):
                                bk = ring.made(act, f"{n}{u}")
                                for m in range(2):
                                    last = A(xpr[:, u % 2, (m0 + m) * T:(m0 + m + 1) * T], bk[:, m * T:(m + 1) * T],
                                             ACT.Exp, bias=xnm[:, u % 2, m0 + m:m0 + m + 1])
                                last.then_inc(ring.free(f"{n}{u}"), 1)
                        elif s.startswith("xattn_t"):
                            u = int(s[7:])
                            g, qt = u // 2, u % 2
                            if u >= 4:
                                ring.made(act, "xO0")
                            bk = ring.made(act, f"xTB{u}")
                            A(xpT[:, g % 2, 1, :, qt * P:(qt + 1) * P], bk[:, :].rearrange("p (m q) -> p m q", m=4),
                              ACT.Copy).then_inc(ring.free(f"xTB{u}"), 1)
                        elif s.startswith("xattn_o") and s != "xattn_out":
                            j = int(s[7:])
                            inverse(f"xO{j}", T, xri[:, j, :])
                        elif s == "xattn_out":
                            rstd(agB, lnB, rsB, 0, ("statsB", 2), "rstdB")
                        elif s == "moe_in":
                            act.wait_ge(sig("fz_ready"), 2)
                            A(gg[:, 1, :], gg[:, 0, :], ACT.Exp, scale=-1.0).then_inc(sig("fexp_ready"), 1)
                            copy_out("grow", grow)
                            copy_out("xsel", xselT)
                            copy_out("permT", permT)
                            bk = ring.made(act, "fk")
                            A(xkT[:, :, 0:CAP], bk[:, 0:DT * CAP].rearrange("p (j t) -> p j t", j=DT), ACT.Copy)\
                                .then_inc(ring.free("fk"), 1)
                        elif s.startswith("moe_s"):
                            g = int(s[5:])
                            act.wait_ge(sig("moe_max"), g + 1)
                            if g >= 2:
                                ring.made(act, f"fT{g - 2}")
                            bk = ring.made(act, f"fS{g}")
                            for m in range(4):
                                last = A(xpr[:, g % 2, m * P:(m + 1) * P], bk[:, m * P:(m + 1) * P], ACT.Exp,
                                         bias=xnm[:, g % 2, m:m + 1])
                            last.then_inc(ring.free(f"fS{g}"), 1)
                        elif s.startswith("moe_o") and s != "moe_out":
                            j = int(s[5:])
                            inverse(f"fO{j}", CAP, xri[:, j, 0:CAP])
                        elif s == "moe_out":
                            copy_out("fo", fo)
                            rstd(agB, lnB, rsB, 0, ("statsB", 3), "rstdB")

                act.wait_ge(loaded, 16 * NLOAD)
                act.wait_ge(const_ready, 1)
                A(anew[:, :, :], W["alog"][:, :, :], ACT.Exp).then_inc(chain["act"], 1)
                A(junk[0:NCOL, :], cemb, ACT.Square, accum_out=cst[:, 0:1]).then_inc(chain["act"], 1)
                act.wait_ge(chain["act"], 2)
                A(cst[:, 1:2], cst[:, 0:1], ACT.Sqrt).then_inc(chain["act"], 1)
                act.preload_act_table_set(LOG_EXP)
                act.wait_ge(go, 1)
                run(FRONT)
                act.drain().then_inc(arrived, 1)
                act.wait_ge(go, 2)
                with act.Fori(1, NB) as b:
                    run(BOTH)
                    act.drain().then_inc(arrived, 1)
                    act.wait_ge(go, b + 2)
                run(BACK)
                act.drain().then_inc(arrived, 1)

            @block.vector
            def _(dve):
                TS, TTn, STT = dve.tensor_scalar, dve.tensor_tensor, dve.scalar_tensor_tensor

                def over(v, shape):
                    return v.unsqueeze(2).to_broadcast(shape)

                def run(steps):
                    ring = Ring(steps)
                    link = Chain(dve, chain["dve"])
                    count = {"F": 0, "B": 0}

                    def layernorm(half, y, x, ready):
                        st, ag, rs = (stF, agF, rsF) if half == "F" else (stB, agB, rsB)
                        count[half] += 1
                        for t in range(TT):
                            last = dve.bn_stats(st[:, t, :], y[:, t, :])
                        link(last)
                        for t in range(TT):
                            last = dve.bn_aggr(ag[:, t, :], st[:, t, :])
                        last.then_inc(sig("stats" + half), 1)
                        dve.wait_ge(sig("rstd" + half), count[half])
                        for t in range(TT):
                            TS(x[:, t, :], y[:, t, :], ag[:, t, 0:1], rs[:, t:t + 1], ALU.subtract, ALU.mult)\
                                .then_inc(sig(ready), 1)

                    def halves(bk):
                        return bk[:, :].rearrange("p (a b) -> p a b", a=2)

                    def weighted(name, n, ri, dst):
                        bk = ring.made(dve, name)
                        dve.wait_ge(sig("inverse_" + name[0]), int(name[2:]) + 1)
                        TTn(dst, bk[:, 0:n], ri, ALU.mult).then_inc(ring.free(name), 1)

                    for s in steps:
                        if s == "attn0_in":
                            for i in range(2):
                                bk = ring.made(dve, f"q{i}")
                                for h in range(2):
                                    last = TS(qm[:, h, 2 * i:2 * i + 2, :], halves(bk), hmask0[:, h:h + 1], None,
                                              ALU.mult)
                                last.then_inc(ring.free(f"q{i}"), 1)
                        elif s.startswith("attn0_s"):
                            p = int(s[7:])
                            if p >= 2:
                                ring.taken(dve, f"aSB{p - 2}")
                            bk = ring.made(dve, f"aSA{p}")
                            m = nmx[:, p % 2, :]
                            dve.tensor_reduce(m[:, 0:2], bk[:, 0:T].rearrange("p (h k) -> p h k", h=2), AX.X, ALU.max,
                                              negate=True)
                            dve.tensor_reduce(m[:, 2:3], bk[:, T:2 * T], AX.X, ALU.max, negate=True)
                            bk = ring.made(dve, f"aSB{p}")
                            dve.tensor_reduce(m[:, 3:4], bk[:, 0:T], AX.X, ALU.max, negate=True)\
                                .then_inc(sig("attn0_max"), 1)
                        elif s.startswith("attn0_t"):
                            p = int(s[7:])
                            if p >= 4:
                                ring.made(dve, f"aO{(p - 4) // 2}")
                            bk = ring.made(dve, f"aTA{p}")
                            dve.tensor_copy(pT[:, p % 4, 0:512], bk[:, :]).then_inc(ring.free(f"aTA{p}"), 1)
                        elif s.startswith("attn0_o") and s != "attn0_out":
                            j = int(s[7:])
                            weighted(f"aO{j}", T, rinv[:, j % 2, :], oT[:, j, :])
                        elif s == "attn0_out":
                            bk = ring.made(dve, "y0")
                            TTn(yF[:, :, :], halves(bk), x0[:, :, :], ALU.add).then_inc(ring.free("y0"), 1)
                            ring.taken(dve, "y0")
                            layernorm("F", yF, x1, "x1_ready")
                        elif s == "mlstm_in":
                            bk = ring.made(dve, "x1T")
                            dve.tensor_copy(xT[:, :, :], halves(bk))
                            for h in range(2):
                                last = TS(xTm[:, h, :, :], halves(bk), hmask0[:, h:h + 1], None, ALU.mult)
                            last.then_inc(ring.free("x1T"), 1)
                            bk = ring.made(dve, "gates")
                            TS(row(0), bk[0:8, 0:T], W["gib"][:, 0:1], None, ALU.add)
                            TS(row(1), bk[0:8, T:2 * T], W["gfb"][:, 0:1], None, ALU.add)\
                                .then_inc(ring.free("gates"), 1)
                            ring.taken(dve, "gates")
                            dve.wait_ge(sig("lnf"), 1)
                            link(STT(row(3), row(1), 0.0, row(4), ALU.min, ALU.subtract))
                            link(dve.tensor_tensor_scan(row(6), ones8[:, :], row(3), 0.0, ALU.mult, ALU.add))
                            TTn(row(5), row(0), row(6), ALU.subtract).then_inc(sig("rows_ready"), 1)
                            dve.wait_ge(sig("rows_ready"), 1)
                            link(dve.tensor_tensor_scan(row(2), row(5), row(5), -3.0e38, ALU.max, ALU.max))
                            TS(nmr[0:8, :], row(2), -1.0, None, ALU.mult).then_inc(sig("nmr_ready"), 1)
                            TTn(row(7), row(6), row(2), ALU.add).then_inc(sig("maxd"), 1)
                        elif s.startswith("mlstm_s"):
                            q = int(s[7:])
                            bk = ring.made(dve, f"mKA{q}")
                            ring.taken(dve, f"mMA{q}")
                            TTn(pT[:, q, 0:512], bk[:, :], pr[:, q % 2, 0:512], ALU.mult)\
                                .then_inc(ring.free(f"mKA{q}"), 1)
                            bk = ring.made(dve, f"mKB{q}")
                            ring.taken(dve, f"mMB{q}")
                            TTn(pT[:, q, 512:768], bk[:, 0:256], pr[:, q % 2, 512:768], ALU.mult)\
                                .then_inc(ring.free(f"mKB{q}"), 1)
                        elif s.startswith("mlstm_o"):
                            j = int(s[7:])
                            bk = ring.made(dve, f"mO{j}")
                            ring.taken(dve, "ebc")
                            r = rinv[:, j, :]
                            link(STT(r, bk[:, T:2 * T], -1.0, ebc[:, j, :], ALU.mult, ALU.max))
                            link(TTn(r, bk[:, T:2 * T], r, ALU.max))
                            link(TS(r, r, 1e-6, None, ALU.add))
                            link(dve.reciprocal(r, r))
                            TTn(hT[:, j, :], bk[:, 0:T], r, ALU.mult).then_inc(ring.free(f"mO{j}"), 1)
                        elif s == "mlstm_norm":
                            bk = ring.made(dve, "mean")
                            ring.taken(dve, "mO1")
                            TTn(hcT, hT, halves(bk), ALU.subtract).then_inc(ring.free("mean"), 1)
                            dve.wait_ge(sig("hrs_ready"), 1)
                            for t in range(2):
                                STT(hnT[:, t, :], hcT[:, t, :], W["onw"][:, t:t + 1], hT[:, t, :], ALU.mult, ALU.mult)\
                                    .then_inc(sig("hnT_ready"), 1)
                            bk = ring.made(dve, "hnT")
                            TTn(yF[:, :, :], halves(bk), x1[:, :, :], ALU.add).then_inc(ring.free("hnT"), 1)
                            ring.taken(dve, "hnT")
                            layernorm("F", yF, x2, "x2_ready")
                        elif s == "ffn0_in":
                            dve.wait_ge(sig("ssq_ready"), 1)
                            TS(s2[:, 1, :], s2[:, 0, :], 1e-24, None, ALU.max).then_inc(sig("ss_ready"), 1)
                            dve.wait_ge(sig("rn_ready"), 1)
                            bk = ring.made(dve, "sim")
                            for t in range(TT):
                                last = TS(sm[:, 0, t, :], bk[:, t * NCOL:(t + 1) * NCOL], s2[:, 3, t:t + 1],
                                          float(2 ** 20), ALU.mult, ALU.mult)
                            last.then_inc(ring.free("sim"), 1)
                        elif s == "ffn0_gate":
                            v = [P, TT, NCOL]
                            bk = ring.made(dve, "gate")
                            TTn(sm[:, 1, :, :], bk[:, 0:TT * NCOL].rearrange("p (t c) -> p t c", t=TT),
                                W["b2r"][:, :].unsqueeze(1).to_broadcast(v), ALU.add).then_inc(ring.free("gate"), 1)
                            dve.wait_ge(sig("gexp_ready"), 1)
                            link(TS(sm[:, 3, :, :], sm[:, 2, :, :], 1.0, None, ALU.add))
                            link(dve.reciprocal(sm[:, 10, :, :], sm[:, 3, :, :]))
                            link(TTn(sm[:, 4, :, :], sm[:, 10, :, :], sm[:, 0, :, :], ALU.add))
                            link(dve.reduce_max(s2[:, 4, :], sm[:, 4, :, :], AX.X))
                            TTn(sm[:, 5, :, :], sm[:, 4, :, :], over(s2[:, 4, :], v), ALU.subtract)\
                                .then_inc(sig("shifted"), 1)
                            link(TTn(sm[:, 7, :, :], sm[:, 4, :, :], over(s2[:, 4, :], v), ALU.is_ge))
                            link(TTn(sm[:, 8, :, :], sm[:, 7, :, :], revc[:, :, :], ALU.mult))
                            link(dve.reduce_max(s2[:, 7, :], sm[:, 8, :, :], AX.X))
                            TTn(ohb[:, :, :], sm[:, 8, :, :], over(s2[:, 7, :], v), ALU.is_equal)\
                                .then_inc(sig("onehot_ready"), 1)
                            dve.wait_ge(sig("pexp_ready"), 1)
                            link(dve.reduce_sum(s2[:, 5, :], sm[:, 6, :, :], AX.X))
                            link(dve.reciprocal(s2[:, 6, :], s2[:, 5, :]))
                        elif s == "ffn0_out":
                            for c in range(4):
                                ring.taken(dve, f"c{c}")
                                bk = ring.made(dve, f"m{c}")
                                TTn(cols[:, 2 * c:2 * c + 2, :], halves(bk), cols[:, 2 * c:2 * c + 2, :], ALU.mult)\
                                    .then_inc(ring.free(f"m{c}"), 1)
                            bk = ring.made(dve, "y2")
                            dve.wait_ge(sig("ffn_base"), 1)
                            for t in range(TT):
                                last = STT(yF[:, t, :], bk[:, t * D:(t + 1) * D], s2[:, 6, t:t + 1], x1[:, t, :],
                                           ALU.mult, ALU.add)
                            last.then_inc(ring.free("y2"), 1)
                            ring.taken(dve, "y2")
                            layernorm("F", yF, x1, "ffn_norm")
                            dve.wait_ge(sig("ffn_norm"), 2)
                            v = [P, TT, D]
                            link(TTn(x1[:, :, :], x1[:, :, :], W["lngr"][:, :].unsqueeze(1).to_broadcast(v), ALU.mult))
                            link(TTn(x1[:, :, :], x1[:, :, :], W["lnbr"][:, :].unsqueeze(1).to_broadcast(v), ALU.add))
                            link(TTn(yF[:, :, :], x1[:, :, :], x2[:, :, :], ALU.add))
                            if "mamba_in" in steps:
                                dve.wait_ge(sig("x3b_ready"), 1)
                            layernorm("F", yF, x3, "x3_ready")
                        elif s == "mamba_in":
                            ring.taken(dve, "xi1")
                            dve.wait_ge(sig("xp_zeroed"), 1)
                            for ct in range(JI):
                                last = TS(yb[:, ct, :], xp[:, ct, KC - 1:], W["convw"][:, ct, KC - 1:KC],
                                          W["convb"][:, ct:ct + 1], ALU.mult, ALU.add)
                            link(last)
                            for k in range(KC - 1):
                                for ct in range(JI):
                                    last = STT(yb[:, ct, :], xp[:, ct, k:k + T], W["convw"][:, ct, k:k + 1],
                                               yb[:, ct, :], ALU.mult, ALU.add)
                                if k < KC - 2:
                                    link(last)
                            last.then_inc(sig("conv_ready"), 1)
                        elif s == "mamba_dt":
                            dve.wait_ge(sig("sp_ready"), 1)
                            TTn(dtv, dtv, yb, ALU.add).then_inc(sig("dt_ready"), 1)
                            dve.wait_ge(sig("dt_ready"), 1)
                            dve.wait_ge(sig("xc_ready"), 1)
                            link(TTn(sg, dtv, xc, ALU.mult))
                        elif s.startswith("mamba_u"):
                            u = int(s[7:])
                            nq, ct = u // JI, u % JI
                            if ct == 0:
                                dve.wait_ge(sig(f"bc_loaded{nq % 2}"), 32 * (nq // 2 + 1))
                            if u >= 2:
                                dve.wait_ge(sig("summed"), u - 1)
                            v = hs[u % 2]
                            link(TTn(v, bq[nq % 2],
                                     sg[:, ct, :].unsqueeze(1).to_broadcast([P, HN, T]), ALU.mult))
                            dve.wait_ge(sig("dA_ready"), u + 1)
                            flat = v.rearrange("p n t -> p (n t)")
                            dve.tensor_tensor_scan(flat, dA[u % 2].rearrange("p n t -> p (n t)"), flat, 0.0, ALU.mult,
                                                   ALU.add).then_inc(sig("scanned"), 1)
                        elif s == "mamba_out":
                            dve.wait_ge(sig("summed"), JI * NS // HN)
                            for ct in range(JI):
                                last = STT(yb[:, ct, :], xc[:, ct, :], W["dp"][:, ct:ct + 1], yb[:, ct, :], ALU.mult,
                                           ALU.add)
                            link(last)
                            for ct in range(JI):
                                TTn(yb[:, ct, :], yb[:, ct, :], zs[:, ct, :], ALU.mult).then_inc(sig("yb_ready"), 1)
                            bk = ring.made(dve, "y3")
                            TTn(yB[:, :, :], halves(bk), x3b[:, :, :], ALU.add).then_inc(ring.free("y3"), 1)
                            ring.taken(dve, "y3")
                            layernorm("B", yB, x4, "x4_ready")
                        elif s == "xattn_in":
                            bk = ring.made(dve, "xq")
                            for m in range(4):
                                for j in range(DT):
                                    last = TS(xqm[:, m, j, :], bk[:, j * T:(j + 1) * T], W["xbq"][:, j:j + 1],
                                              hmask1[:, m:m + 1], ALU.add, ALU.mult)
                            last.then_inc(ring.free("xq"), 1)
                            bk = ring.made(dve, "xv")
                            dve.wait_ge(sig("vp_zeroed"), 1)
                            for t in range(TT):
                                src = bk[:, t * D:(t + 1) * D].rearrange("p (h o d) -> p h o d", o=2, d=16)
                                bias = W["xbvr"][:, :].rearrange("p (h o d) -> p h o d", o=2, d=16)
                                dst = vp[:, t, :, :].rearrange("p (h o) d -> p h o d", o=2)
                                for o in range(2):
                                    last = TTn(dst[:, :, o, 16 * o:16 * o + 16], src[:, :, o, :], bias[:, :, o, :],
                                               ALU.add)
                            last.then_inc(ring.free("xv"), 1)
                        elif s.startswith("xattn_s"):
                            u = int(s[7:])
                            if u >= 2:
                                ring.taken(dve, f"xSB{u - 2}")
                            for n, m0 in (("xSA", 0), ("xSB", 2)):
                                bk = ring.made(dve, f"{n}{u}")
                                last = dve.tensor_reduce(xnm[:, u % 2, m0:m0 + 2], halves(bk), AX.X, ALU.max,
                                                         negate=True)
                            last.then_inc(sig("xattn_max"), 1)
                        elif s.startswith("xattn_t"):
                            u = int(s[7:])
                            g, qt = u // 2, u % 2
                            if u >= 4:
                                ring.made(dve, "xO0")
                            bk = ring.made(dve, f"xTA{u}")
                            dve.tensor_copy(xpT[:, g % 2, 0, :, qt * P:(qt + 1) * P],
                                            bk[:, :].rearrange("p (m q) -> p m q", m=4))\
                                .then_inc(ring.free(f"xTA{u}"), 1)
                        elif s.startswith("xattn_o") and s != "xattn_out":
                            j = int(s[7:])
                            weighted(f"xO{j}", T, xri[:, j, :], xoT[:, j, :])
                        elif s == "xattn_out":
                            bk = ring.made(dve, "y4")
                            dve.wait_ge(sig("xattn_base"), 1)
                            TTn(yB[:, :, :], halves(bk), yB[:, :, :], ALU.add).then_inc(ring.free("y4"), 1)
                            ring.taken(dve, "y4")
                            layernorm("B", yB, x5, "x5_ready")
                        elif s == "moe_in":
                            dve.wait_ge(sig("x5_ready"), 2)
                            for t in range(TT):
                                STT(junk, x5[:, t, :], 1.0, W["wgr"][:, :], ALU.mult, ALU.mult,
                                    accum_out=gg[:, 0, t:t + 1]).then_inc(sig("fz_ready"), 1)
                                dve.wait_ge(sig("fz_ready"), t + 1)
                            dve.wait_ge(sig("fexp_ready"), 1)
                            link(TS(gg[:, 2, :], gg[:, 1, :], 1.0, None, ALU.add))
                            link(dve.reciprocal(gg[:, 3, :], gg[:, 2, :]))
                            for t in range(TT):
                                dve.tensor_copy(grep[:, t, :], gg[:, 3, t:t + 1].to_broadcast([P, P]))\
                                    .then_inc(sig("grep_ready"), 1)
                            ring.taken(dve, "grow")
                            for t in range(TT):
                                g = gg[:, 3, t:t + 1]
                                link(TS(junk, grow, g, None, ALU.is_gt, ALU.add,
                                        accum_out=gg[:, 4, t:t + 1]))
                                link(STT(junk, grow, g, lower[:, t, :], ALU.is_equal, ALU.mult,
                                         accum_out=gg[:, 5, t:t + 1]))
                            link(TTn(gg[:, 6, :], gg[:, 4, :], gg[:, 5, :], ALU.add))
                            for t in range(TT):
                                TS(perm[:, t, :], iota[:, :], gg[:, 6, t:t + 1], None, ALU.is_equal)\
                                    .then_inc(sig("perm_ready"), 1)
                            bk = ring.made(dve, "fq")
                            for m in range(4):
                                last = TS(xqm[:, m, :, 0:CAP], bk[:, 0:DT * CAP].rearrange("p (j t) -> p j t", j=DT),
                                          hmask1[:, m:m + 1], None, ALU.mult)
                            last.then_inc(ring.free("fq"), 1)
                            bk = ring.made(dve, "fv")
                            src = bk[:, 0:D].rearrange("p (h o d) -> p h o d", o=2, d=16)
                            dst = vp[:, 0, :, :].rearrange("p (h o) d -> p h o d", o=2)
                            for o in range(2):
                                last = dve.tensor_copy(dst[:, :, o, 16 * o:16 * o + 16], src[:, :, o, :])
                            last.then_inc(ring.free("fv"), 1)
                        elif s.startswith("moe_s"):
                            g = int(s[5:])
                            if g >= 2:
                                ring.taken(dve, f"fS{g - 2}")
                            bk = ring.made(dve, f"fS{g}")
                            dve.tensor_reduce(xnm[:, g % 2, 0:4], bk[:, :].rearrange("p (m k) -> p m k", m=4), AX.X,
                                              ALU.max, negate=True).then_inc(sig("moe_max"), 1)
                        elif s.startswith("moe_t"):
                            g = int(s[5:])
                            bk = ring.made(dve, f"fT{g}")
                            dve.tensor_copy(xpT[:, g // 2, g % 2, :, 0:CAP],
                                            bk[:, :].rearrange("p (m q) -> p m q", m=4))\
                                .then_inc(ring.free(f"fT{g}"), 1)
                        elif s.startswith("moe_o") and s != "moe_out":
                            j = int(s[5:])
                            weighted(f"fO{j}", CAP, xri[:, j, 0:CAP], xoT[:, j, 0:CAP])
                        elif s == "moe_out":
                            bk = ring.made(dve, "y5")
                            for t in range(TT):
                                last = STT(yB[:, t, :], bk[:, t * D:(t + 1) * D], gg[:, 3, t:t + 1], x5[:, t, :],
                                           ALU.mult, ALU.add)
                            last.then_inc(ring.free("y5"), 1)
                            ring.taken(dve, "y5")
                            layernorm("B", yB, x6, "x6_ready")

                link = Chain(dve, chain["dve"])
                dve.wait_ge(loaded, 16 * NLOAD)
                dve.wait_ge(const_ready, 1)
                dve.wait_ge(chain["act"], 3)
                link(TS(anew[:, :, :], anew[:, :, :], -1.0, None, ALU.mult))
                link(TS(cst[:, 2:3], cst[:, 1:2], 1e-12, None, ALU.max))
                link(dve.reciprocal(cst[:, 3:4], cst[:, 2:3]))
                TS(cen, cemb, cst[:, 3:4], None, ALU.mult).then_inc(s_set, 1)
                dve.tensor_copy(gwc[:, 0:2, :], W["gw"][:, 0:2, :])
                link(TTn(gwc[:, 2:4, :], W["gw"][:, 2:4, :], W["gw"][:, 4:6, :], ALU.add))
                link(dve.tensor_copy(maskf, maski))
                link(TS(xmask[:, :, :], maskf, 0.0, MASKED, ALU.is_equal, ALU.mult))
                dve.wait_ge(s_set, 2)
                dve.tensor_copy(cenT[:, :, :], banks[0][:, 0:DT * NCOL].rearrange("p (d c) -> p d c", d=DT))\
                    .then_inc(s_set, 1)
                dve.wait_ge(go, 1)
                run(FRONT)
                dve.drain().then_inc(arrived, 1)
                dve.wait_ge(go, 2)
                with dve.Fori(1, NB) as b:
                    run(BOTH)
                    dve.drain().then_inc(arrived, 1)
                    dve.wait_ge(go, b + 2)
                run(BACK)
                dve.drain().then_inc(arrived, 1)

            @block.gpsimd
            def _(pool):
                def run(steps):
                    link = Chain(pool, chain["pool"])
                    for s in steps:
                        if s == "ffn0_out":
                            pool.wait_ge(sig("x2_ready"), 2)
                            pool.tensor_tensor(x1[:, :, :], x2[:, :, :],
                                               W["pbr"][:, :].unsqueeze(1).to_broadcast([P, TT, D]), ALU.add)\
                                .then_inc(sig("ffn_base"), 1)
                            pool.wait_ge(sig("onehot_ready"), 1)
                            pool.tensor_copy(ohx[:, :, :, :].rearrange("p t c n -> p (t c) n"),
                                             ohb[:, :, :].rearrange("p t c -> p (t c)").unsqueeze(2)
                                             .to_broadcast([P, TT * NCOL, NNEU])).then_inc(sig("onehot_wide"), 1)
                        elif s == "mamba_in":
                            pool.tensor_copy(x3b[:, :, :], x3[:, :, :]).then_inc(sig("x3b_ready"), 1)
                            for i in range(2):
                                pool.memset(dA[i][:, :, 0:1], 0.0).then_inc(sig("dA_zeroed"), 1)
                            pool.memset(xp[:, :, 0:KC - 1], 0.0).then_inc(sig("xp_zeroed"), 1)
                        elif s.startswith("mamba_u"):
                            u = int(s[7:])
                            nq, ct = u // JI, u % JI
                            v = hs[u % 2]
                            if ct == 0:
                                pool.wait_ge(sig(f"bc_loaded{nq % 2}"), 32 * (nq // 2 + 1))
                            pool.wait_ge(sig("scanned"), u + 1)
                            link(pool.tensor_tensor(v, v, cq[nq % 2], ALU.mult))
                            link(pool.tensor_tensor(v[:, 0:2, :], v[:, 0:2, :], v[:, 2:4, :], ALU.add))
                            if nq == 0:
                                pool.tensor_tensor(yb[:, ct, :], v[:, 0, :], v[:, 1, :], ALU.add)\
                                    .then_inc(sig("summed"), 1)
                            else:
                                link(pool.tensor_tensor(v[:, 0, :], v[:, 0, :], v[:, 1, :], ALU.add))
                                pool.tensor_tensor(yb[:, ct, :], yb[:, ct, :], v[:, 0, :], ALU.add)\
                                    .then_inc(sig("summed"), 1)
                        elif s == "xattn_in":
                            pool.wait_ge(sig("x4_ready"), 2)
                            pool.memset(vp[:, :, :, :], 0.0).then_inc(sig("vp_zeroed"), 1)
                            pool.tensor_tensor(yB[:, :, :], x4[:, :, :],
                                               W["xbor"][:, :].unsqueeze(1).to_broadcast([P, TT, D]), ALU.add)\
                                .then_inc(sig("xattn_base"), 1)

                n = [0]

                def step(ins):
                    n[0] += 1
                    ins.then_inc(chain["pool"], 1)
                    pool.wait_ge(chain["pool"], n[0])

                for v, val in ((ident, 0.0), (triq, 0.0), (trik, 0.0), (lower, 1.0), (onesv, 1.0), (onesp, 0.0),
                               (blk, 0.0), (selh, 0.0), (sele, 0.0), (hmask0, 0.0), (ones8, 1.0), (nmr, 0.0),
                               (er, 0.0), (blk16, 1.0)):
                    last = pool.memset(v[:] if len(v.shape) < 3 else v[:, :, :], val)
                pool.memset(epsc[:, 0:1], 1e-5)
                pool.memset(epsc[:, 1:2], 1e-6)
                step(pool.memset(cst[:, :], 0.0))
                step(pool.affine_select(out=ident[:, :], in_=ident[:, :], compare_op=ALU.not_equal, fill=1.0, base=0,
                                        pattern=[[-1, P]], channel_multiplier=1))
                step(pool.tensor_copy(identb[:, :], ident[:, :]))
                step(pool.affine_select(out=triq[:, :], in_=triq[:, :], compare_op=ALU.is_ge, fill=MASKED, base=0,
                                        pattern=[[-1, P]], channel_multiplier=1))
                step(pool.affine_select(out=trik[:, :], in_=trik[:, :], compare_op=ALU.is_ge, fill=MASKED, base=0,
                                        pattern=[[1, P]], channel_multiplier=-1))
                step(pool.affine_select(out=lower[:, :, :], in_=lower[:, :, :], compare_op=ALU.is_gt, fill=0.0, base=0,
                                        pattern=[[P, TT], [-1, T]], channel_multiplier=1))
                step(pool.affine_select(out=selh[:, :, :], in_=selh[:, :, :], compare_op=ALU.not_equal, fill=1.0,
                                        base=0, pattern=[[-1, NH_M], [0, P]], channel_multiplier=1))
                step(pool.affine_select(out=sele[:, :, :].rearrange("p t (h c) -> p t h c", c=32),
                                        in_=sele[:, :, :].rearrange("p t (h c) -> p t h c", c=32),
                                        compare_op=ALU.not_equal, fill=1.0, base=0,
                                        pattern=[[-4, 2], [-1, 4], [0, 32]], channel_multiplier=1))
                step(pool.affine_select(out=blk16[:, :], in_=blk16[:, :], compare_op=ALU.is_ge, fill=0.0, base=0,
                                        pattern=[[-16, 8]], channel_multiplier=1))
                step(pool.affine_select(out=blk16[:, :], in_=blk16[:, :], compare_op=ALU.is_ge, fill=0.0, base=15,
                                        pattern=[[16, 8]], channel_multiplier=-1))
                step(pool.tensor_tensor(hmask1[:, :], blk16[:, 0:4], blk16[:, 4:8], ALU.add))
                step(pool.tensor_scalar(hmask1[:, :], hmask1[:, :], 16 ** -0.5, None, ALU.mult))
                for i in range(4):
                    step(pool.memset(blk[32 * i:32 * i + 32, 32 * i:32 * i + 32], 1.0 / 32))
                    step(pool.memset(hmask0[32 * i:32 * i + 32, i % 2:i % 2 + 1], 32 ** -0.5))
                for o in range(2):
                    pool.memset(onesp[:, o, 16 * o:16 * o + 16], 1.0)
                pool.iota(iota[:, :], pattern=[[1, P]], base=0, channel_multiplier=0,
                          allow_small_or_imprecise_dtypes=True)
                pool.iota(revc[:, :, :], pattern=[[0, TT], [-1, NCOL]], base=NCOL, channel_multiplier=0,
                          allow_small_or_imprecise_dtypes=True).then_inc(const_ready, 1)
                pool.wait_ge(const_ready, 1)
                pool.wait_ge(go, 1)
                run(FRONT)
                pool.drain().then_inc(arrived, 1)
                pool.wait_ge(go, 2)
                with pool.Fori(1, NB) as b:
                    run(BOTH)
                    pool.drain().then_inc(arrived, 1)
                    pool.wait_ge(go, b + 2)
                run(BACK)
                pool.drain().then_inc(arrived, 1)

            @block.sync
            def _(sp):
                def tiles(v):
                    return v.rearrange("b (t p) d -> p (b t) d", p=P)

                def of(v, b):
                    return tiles(v[b:b + 1, :, :] if isinstance(b, int) else v[bass.ds(b, 1), :, :])

                def run(steps, b, bb):
                    ring = Ring(steps)
                    for s in steps:
                        if s == "attn0_in":
                            sp.dma_start(x0[:, :, :], of(a["x"], b)).then_inc(sig("x0_ready"), 16)
                        elif s == "mlstm_in":
                            sp.dma_start(cF, of(a["ctx"], b)).then_inc(sig("cF_ready"), 16)
                        elif s == "mamba_dt":
                            ring.taken(sp, "xdbl")
                            sp.dma_start(scratch[0, :, :], xd[B_ROW:B_ROW + NS, :]).then_inc(sig("bc_stored"), 16)
                            sp.dma_start(scratch[1, :, :], xd[C_ROW:C_ROW + NS, :]).then_inc(sig("bc_stored"), 16)
                            sp.wait_ge(sig("bc_stored"), 32)
                        elif s.startswith("mamba_u") and int(s[7:]) % JI == 0:
                            nq = int(s[7:]) // JI
                            for n in ((0, 1) if nq == 0 else (nq + 1,) if nq < 3 else ()):
                                if n >= 2:
                                    sp.wait_ge(sig("summed"), JI * (n - 1))
                                for i, v in enumerate((bq, cq)):
                                    sp.dma_start(v[n % 2], scratch[i:i + 1, n * HN:(n + 1) * HN, :]
                                                 .to_broadcast([P, HN, T])).then_inc(sig(f"bc_loaded{n % 2}"), 16)
                        elif s == "xattn_in":
                            sp.wait_ge(sig("x4_ready"), 2)
                            sp.dma_start(c4, of(a["ctx"], bb)).then_inc(sig("c4_ready"), 16)
                        elif s == "moe_out":
                            sp.wait_ge(sig("x6_ready"), 2)
                            sp.dma_start(of(out, bb), x6[:, :, :]).then_inc(stored, 16)

                for n in W:
                    if n in ROWS:
                        sp.dma_start(W[n][:, :], a[n].to_broadcast([P, ROWS[n]])).then_inc(loaded, 16)
                    elif n != "cemb":
                        v = W[n]
                        sp.dma_start(v[:, :] if len(v.shape) == 2 else v[:, :, :], a[n]).then_inc(loaded, 16)
                sp.dma_start(cemb, a["cemb"]).then_inc(loaded, 16)
                sp.dma_start(maski, a["mask"]).then_inc(loaded, 16)
                sp.wait_ge(loaded, 16 * NLOAD)
                sp.wait_ge(s_set, 3)
                run_clear(sp)
                sp.sem_inc(go, 1)
                run(FRONT, 0, None)
                sp.wait_ge(arrived, 4)
                run_clear(sp)
                sp.sem_inc(go, 1)
                with sp.Fori(1, NB) as b:
                    run(BOTH, b, b - 1)
                    sp.wait_ge(arrived, 4)
                    run_clear(sp)
                    sp.wait_ge(stored, b * 16)
                    sp.sem_inc(go, 1)
                run(BACK, None, NB - 1)
                sp.wait_ge(arrived, 4)
                sp.wait_ge(stored, NB * 16)


_OUT = ((NB, T, D), "float32")


def _layout(i):
    import numpy as np

    def f(n):
        return np.asarray(i[n])

    def kt(w):
        return np.ascontiguousarray(w.reshape(-1, P, w.shape[1]).transpose(1, 0, 2))

    def col(v):
        return np.ascontiguousarray(v.reshape(-1, P).T)

    def gates(w):
        return w

    wx = np.zeros((DI, P), np.float32)
    xw = f("L1_attn_x_proj_w").T
    wx[:, 0:16], wx[:, B_ROW:B_ROW + NS], wx[:, C_ROW:C_ROW + NS] = xw[:, 0:16], xw[:, 16:32], xw[:, 32:48]
    wdt = np.zeros((P, DI), np.float32)
    wdt[0:16] = f("L1_attn_dt_proj_w").T
    gw = np.concatenate([f("L0_xattn_igate_kernel"), f("L0_xattn_fgate_kernel")], axis=1)
    wc = f("L0_ffn_W_cols").transpose(1, 0, 2).reshape(D, NCOL * NNEU)
    return {
        "x": f("x"), "ctx": f("ctx_1024"), "mask": kt(f("mask_1x1xSxS2_ik0").reshape(T, T)),
        "wq0": kt(f("L0_attn_wq").T), "wk0": kt(f("L0_attn_wk").T), "wv0": kt(f("L0_attn_wv").T),
        "wo0": kt(f("L0_attn_wo").T), "gw": kt(gw), "w1": kt(f("L0_ffn_gate_w1")), "w2": f("L0_ffn_gate_w2"),
        "wcols": kt(wc), "wproj": kt(f("L0_ffn_proj_w")), "win": kt(f("L1_attn_in_proj_w").T), "wx": kt(wx),
        "wdt": wdt, "wout": kt(f("L1_attn_out_proj_w").T), "xwq": kt(f("L1_xattn_Wq")), "xwk": kt(f("L1_xattn_Wk")),
        "xwv": kt(f("L1_xattn_Wv")), "xwo": kt(f("L1_xattn_Wo")), "fwq": kt(f("L1_ffn_Wq")), "fwk": kt(f("L1_ffn_Wk")),
        "fwv": kt(f("L1_ffn_Wv")), "fwo": kt(f("L1_ffn_Wo")), "onw": col(f("L0_xattn_outnorm_weight").reshape(-1)),
        "b1": col(f("L0_ffn_gate_b1")), "bcols": col(f("L0_ffn_b_cols").reshape(-1)),
        "convw": kt(f("L1_attn_conv_w")), "convb": col(f("L1_attn_conv_b")), "bdt": col(f("L1_attn_dt_proj_b")),
        "alog": kt(f("L1_attn_A_log")), "dp": col(f("L1_attn_Dp")), "xbq": col(f("L1_xattn_bq")),
        "xbk": col(f("L1_xattn_bk")), "gib": f("L0_xattn_igate_bias").reshape(8, 1),
        "gfb": f("L0_xattn_fgate_bias").reshape(8, 1), "cemb": f("L0_ffn_col_emb"),
        "b2r": f("L0_ffn_gate_b2").reshape(1, -1), "pbr": f("L0_ffn_proj_b").reshape(1, -1),
        "lngr": f("L0_ffn_ln_g").reshape(1, -1), "lnbr": f("L0_ffn_ln_b").reshape(1, -1),
        "xbvr": f("L1_xattn_bv").reshape(1, -1), "xbor": f("L1_xattn_bo").reshape(1, -1),
        "wgr": f("L1_ffn_Wg").reshape(1, -1),
    }


def kernel(**inputs):
    import numpy as np
    import concourse.bacc as bacc
    from concourse.bass_utils import run_bass_kernel_spmd

    nc = bacc.Bacc("TRN2", target_bir_lowering=False, num_devices=1)
    arrays, aps = {}, {}
    for name, v in _layout(inputs).items():
        v = np.ascontiguousarray(v)
        arrays[f"in_{name}"] = v
        aps[name] = nc.dram_tensor(f"in_{name}", v.shape, mybir.dt.from_np(v.dtype), kind="ExternalInput").ap()
    out = nc.dram_tensor("out_0", _OUT[0], mybir.dt.float32, kind="ExternalOutput").ap()
    build(nc, aps, out)
    r = run_bass_kernel_spmd(nc, [arrays], core_ids=[0])
    return r.results[0]["out_0"]
```

```python
import concourse.bass as bass
from concourse import mybir
from contextlib import ExitStack

NB, T, D, P = 32, 256, 256, 128
TT, DT = T // P, D // P
QKV0, HD0 = 512, 32
J0 = QKV0 // P
NH_M, HD_M = 8, 32
HID, NCOL, NNEU = 128, 16, 64
CM = NCOL * NNEU // P
DI, NS, KC = 512, 16, 4
JI = DI // P
HN = 4
B_ROW, C_ROW = 32, 64
CAP = T // 2
NBANK = 8
LOG_EXP = "natural_log_exp_and_others"
MASKED = -float(2 ** 126)

FILLS = {
    "attn0_x": ["x0T"],
    "attn0_q": ["q0", "q1"],
    "attn0_k": ["k0", "k1"],
    "attn0_v": ["v0", "v1"],
    "mlstm_c": ["cT"],
    "mlstm_x": ["x1T"],
    "mlstm_gates": ["gates"],
    "mlstm_acol": ["acol"],
    "mlstm_ebc": ["ebc"],
    "mlstm_mean": ["mean"],
    "mlstm_var": ["var"],
    "mlstm_hn": ["hnT"],
    "ffn0_x": ["x2T"],
    "ffn0_in": ["hid", "sim"],
    "ffn0_gate": ["gate"],
    "ffn0_out": ["y2"],
    "mamba_x": ["x3T"],
    "mamba_xi": ["xi0", "xi1"],
    "mamba_z": ["z0", "z1"],
    "mamba_bc": ["xdbl"],
    "mamba_dt": ["dt0", "dt1"],
    "mamba_out": ["y3"],
    "xattn_x": ["x4T"],
    "xattn_c": ["c4T"],
    "xattn_q": ["xq0", "xq1"],
    "xattn_kv": ["xk", "xv"],
    "xattn_out": ["y4"],
    "moe_rank": ["grow"],
    "moe_pick": ["xsel", "permT"],
    "moe_qkv": ["fq0", "fq1", "fk", "fv"],
    "moe_out": ["fo"],
    "moe_y": ["y5"],
}
for _p in range(8):
    FILLS[f"attn0_s{_p}"] = [f"aSA{_p}", f"aSB{_p}"]
    FILLS[f"attn0_t{_p}"] = [f"aTA{_p}", f"aTB{_p}"]
for _j in range(4):
    FILLS[f"attn0_o{_j}"] = [f"aO{_j}"]
    FILLS[f"ffn0_c{_j}"] = [f"c{_j}"]
    FILLS[f"ffn0_m{_j}"] = [f"m{_j}"]
    FILLS[f"mlstm_p{_j}"] = [f"mMA{_j}", f"mMB{_j}", f"mKA{_j}", f"mKB{_j}"]
for _j in range(2):
    FILLS[f"mlstm_o{_j}"] = [f"mO{_j}"]
    FILLS[f"xattn_o{_j}"] = [f"xO{_j}"]
    FILLS[f"moe_o{_j}"] = [f"fO{_j}"]
FILLS["attn0_out"] = ["y0"]
for _g in range(8):
    FILLS[f"xattn_s{_g}"] = [f"xSA{_g}", f"xSB{_g}"]
    FILLS[f"xattn_t{_g}"] = [f"xTA{_g}", f"xTB{_g}"]
for _g in range(4):
    FILLS[f"moe_s{_g}"] = [f"fS{_g}"]
    FILLS[f"moe_t{_g}"] = [f"fT{_g}"]

FRONT = (["attn0_x", "attn0_q", "attn0_k", "attn0_s0", "attn0_v"]
         + [s for p in range(8) for s in ([f"attn0_s{p + 1}"] if p < 7 else [])
            + [f"attn0_t{p}"] + ([f"attn0_o{p // 2}"] if p % 2 else [])]
         + ["mlstm_c", "attn0_out", "attn0_ln", "mlstm_x", "mlstm_gates", "mlstm_scans", "mlstm_acol",
            "mlstm_p0", "mlstm_p1", "mlstm_ebc", "mlstm_o0", "mlstm_p2", "mlstm_p3", "mlstm_o1",
            "mlstm_mean", "mlstm_var", "mlstm_hn", "mlstm_ln",
            "ffn0_x", "ffn0_in", "ffn0_c0", "ffn0_c1", "ffn0_gate", "ffn0_c2", "ffn0_c3", "ffn0_top",
            "ffn0_m0", "ffn0_m1", "ffn0_m2", "ffn0_m3", "ffn0_out", "ffn0_ln", "ffn0_res",
            "mamba_x", "mamba_xi", "mamba_z", "mamba_conv", "mamba_bc", "mamba_dt", "mamba_sp"])
BACK = (["mamba_in"]
        + [s for u in range(JI * NS // HN) for s in [f"mamba_u{u}"] + ([f"mamba_y{u - 1}"] if u else [])]
        + ["mamba_y15", "xattn_c", "mamba_gate", "mamba_out", "xattn_kv", "mamba_ln", "xattn_x", "xattn_q",
           "xattn_s0"]
        + [s for g in range(8) for s in ([f"xattn_s{g + 1}"] if g < 7 else [])
           + [f"xattn_t{g}"] + ([f"xattn_o{g // 4}"] if g % 4 == 3 else [])]
        + ["xattn_out", "xattn_ln", "moe_gate", "moe_rank", "moe_pick", "moe_qkv", "moe_s0", "moe_s1", "moe_t0",
           "moe_s2", "moe_t1", "moe_s3", "moe_o0", "moe_t2", "moe_t3", "moe_o1", "moe_out", "moe_y", "moe_ln"])

BOTH = """
    mamba_in mamba_u0 attn0_x mamba_u1 mamba_y0 mamba_u2 attn0_q mamba_y1 mamba_u3 attn0_k attn0_s0 mamba_y2
    attn0_s1 attn0_t0 mamba_u4 mamba_y3 mamba_u5 attn0_v attn0_s2 attn0_t1 attn0_s3 attn0_s4 attn0_t2 attn0_o0
    attn0_s5 attn0_t3 attn0_t4 attn0_s6 attn0_s7 mamba_y4 attn0_t5 mamba_u6 attn0_t6 attn0_o1 mlstm_c attn0_t7
    mamba_y5 mamba_u7 attn0_o2 attn0_o3 mamba_y6 mamba_u8 mamba_y7 mamba_u9 attn0_out mamba_y8 attn0_ln mlstm_x
    mamba_u10 mamba_y9 mamba_u11 mlstm_gates mamba_y10 mamba_u12 mlstm_scans mamba_y11 mamba_u13 mamba_y12
    mlstm_acol mamba_u14 mlstm_p0 mlstm_ebc mlstm_p1 mamba_y13 mamba_u15 mlstm_p2 mamba_y14 mlstm_o0 mamba_y15
    mlstm_p3 xattn_c mamba_gate mlstm_o1 mamba_out mlstm_mean xattn_kv mamba_ln xattn_x mlstm_var xattn_q
    mlstm_hn mlstm_ln xattn_s0 xattn_s1 ffn0_x xattn_s2 xattn_t0 ffn0_in ffn0_c0 ffn0_c1 ffn0_c2 ffn0_gate
    ffn0_c3 xattn_s3 xattn_t1 xattn_t2 xattn_s4 xattn_t3 ffn0_top xattn_s5 xattn_o0 xattn_s6 xattn_t4 xattn_s7
    xattn_t5 xattn_t6 ffn0_m0 xattn_t7 ffn0_m1 ffn0_m2 ffn0_m3 xattn_o1 xattn_out xattn_ln moe_gate ffn0_out
    moe_rank ffn0_ln moe_pick moe_qkv ffn0_res moe_s0 moe_s1 mamba_x moe_s2 moe_s3 moe_t0 moe_t1 mamba_xi moe_t2
    mamba_z mamba_conv moe_t3 moe_o0 moe_o1 mamba_bc moe_out mamba_dt moe_y moe_ln mamba_sp
""".split()
assert sorted(BOTH) == sorted(FRONT + BACK)


def build(nc, a, out):
    f32, bf16, i32 = mybir.dt.float32, mybir.dt.bfloat16, mybir.dt.int32
    ALU, ACT, AX = mybir.AluOpType, mybir.ActivationFunctionType, mybir.AxisListType
    ctx = ExitStack()
    with ctx:
        def sb(name, shape, dt=f32):
            return ctx.enter_context(nc.sbuf_tensor(name, shape, dt))

        def sem(name):
            return ctx.enter_context(nc.semaphore(name))

        W = {}
        for n, shp in (("wq0", [P, DT, QKV0]), ("wk0", [P, DT, QKV0]), ("wv0", [P, DT, QKV0]), ("wo0", [P, J0, D]),
                       ("gw", [P, 6, 16]), ("w1", [P, DT, HID]), ("w2", [P, NCOL]), ("wcols", [P, DT, NCOL * NNEU]),
                       ("wproj", [P, CM, D]), ("win", [P, DT, 2 * DI]), ("wx", [P, JI, P]), ("wdt", [P, DI]),
                       ("wout", [P, JI, D]), ("xwq", [P, DT, D]), ("xwk", [P, DT, D]), ("xwv", [P, DT, D]),
                       ("xwo", [P, DT, D]), ("fwq", [P, DT, D]), ("fwk", [P, DT, D]), ("fwv", [P, DT, D]),
                       ("fwo", [P, DT, D]),
                       ("onw", [P, 2]), ("b1", [P, 1]), ("bcols", [P, CM]), ("convw", [P, JI, KC]), ("convb", [P, JI]),
                       ("bdt", [P, JI]), ("alog", [P, JI, NS]), ("dp", [P, JI]), ("xbq", [P, DT]), ("xbk", [P, DT]),
                       ("gib", [8, 1]), ("gfb", [8, 1])):
            W[n] = sb(n, shp)
        ROWS = {"b2r": NCOL, "pbr": D, "lngr": D, "lnbr": D, "xbvr": D, "xbor": D, "wgr": D}
        for n, w in ROWS.items():
            W[n] = sb(n, [P, w])

        ident, identb = sb("ident", [P, P]), sb("identb", [P, P], bf16)
        triq = sb("triq", [P, P], bf16)
        trik = sb("trik", [P, P], bf16)
        lower = sb("lower", [P, TT, T])
        onesv = sb("onesv", [P, 32])
        onesp = sb("onesp", [P, 2, 32])
        blk = sb("blk", [P, P])
        selh = sb("selh", [P, NH_M, P])
        sele = sb("sele", [P, 2, P])
        hmask0 = sb("hmask0", [P, 2])
        hmask1 = sb("hmask1", [P, 4])
        iota = sb("iota", [P, P])
        revc = sb("revc", [P, TT, NCOL])
        ones8 = sb("ones8", [8, T])
        xmask = sb("xmask", [P, TT, T], bf16)
        anew = sb("anew", [P, JI, NS])
        cst = sb("cst", [NCOL, 4])
        cenT = sb("cenT", [P, DT, NCOL])
        gwc = sb("gwc", [P, 4, 16])
        epsc = sb("epsc", [P, 2])
        blk16 = sb("blk16", [P, 8])
        xbqm = sb("xbqm", [P, 4])

        def arena(name, size):
            whole, top = sb(name, [P, size]), [0]

            def room(*shape, at=None):
                n = 1
                for w in shape:
                    n *= w
                o = top[0] if at is None else at
                top[0] = o + n
                assert top[0] <= size, (name, top[0])
                return whole[:, o:o + n]

            return room

        room = arena("front", 11 * 1024)
        qm = room(2, J0, T).rearrange("p (a j t) -> p a j t", a=2, j=J0)
        kT = room(J0, T)
        ohx = kT.bitcast(bf16).rearrange("p (t c n) -> p t c n", t=TT, c=NCOL)
        kT = kT.rearrange("p (j t) -> p j t", j=J0)
        v0 = room(TT, QKV0).rearrange("p (t n) -> p t n", t=TT)
        pr = room(2, 768)
        hidT, sqj = pr[:, 0:T], pr[:, T:T + D]
        pr = pr.rearrange("p (s n) -> p s n", s=2)
        pTw = room(4, 768)
        pT = pTw.rearrange("p (s n) -> p s n", s=4)
        oT = room(J0, T).rearrange("p (j t) -> p j t", j=J0)
        rinv = room(2, T).rearrange("p (s t) -> p s t", s=2)
        cF = room(TT, D).rearrange("p (t d) -> p t d", t=TT)
        cT = room(DT, T).rearrange("p (d t) -> p d t", d=DT)
        xTm = qm[:, :, 0:2, :]
        ebc, hT, hcT, hsq, hnT = oT[:, 2:4, :], oT[:, 0:2, :], kT[:, 0:2, :], kT[:, 2:4, :], rinv
        cols = qm.rearrange("p a j t -> p (a j) t")
        xcF, dtF, zsF = (pTw[:, i * JI * T:(i + 1) * JI * T].rearrange("p (j t) -> p j t", j=JI) for i in range(3))
        ybF = oT
        xp = room(JI, KC - 1 + T, at=3 * J0 * T).rearrange("p (j t) -> p j t", j=JI)
        v0r = v0.rearrange("p t (r n) -> p (t r) n", r=2)

        def row(i):
            return kT[0:8, i, :] if i < 4 else v0r[0:8, i - 4, :]

        room = arena("back", 13 * 1024)
        bq, cq, dA, hs = ([room(HN, T).rearrange("p (n t) -> p n t", n=HN) for _ in range(2)] for _ in range(4))
        xc, sg, zs, dtv, yb = (room(JI, T).rearrange("p (j t) -> p j t", j=JI) for _ in range(5))
        c4 = room(TT, D, at=0).rearrange("p (t d) -> p t d", t=TT)
        c4T = room(DT, T).rearrange("p (d t) -> p d t", d=DT)
        xqm = room(4, DT, T).rearrange("p (m j t) -> p m j t", m=4, j=DT)
        xkT = room(DT, T).rearrange("p (j t) -> p j t", j=DT)
        vp = room(TT, 16, 32).rearrange("p (t h d) -> p t h d", t=TT, h=16)
        xpr = room(2, 1024).rearrange("p (s n) -> p s n", s=2)
        xpT = room(2, 2, 4, T).rearrange("p (s k h q) -> p s k h q", s=2, k=2, h=4)
        xoT = room(DT, T).rearrange("p (j t) -> p j t", j=DT)
        perm = room(TT, CAP).rearrange("p (t c) -> p t c", t=TT)
        permT, grep = (room(TT, P).rearrange("p (t c) -> p t c", t=TT) for _ in range(2))
        xselT = room(DT, CAP).rearrange("p (t c) -> p t c", t=DT)
        fo, grow, junk = room(D), room(T), room(D)
        maski = room(TT, T, at=0).bitcast(i32).rearrange("p (t k) -> p t k", t=TT)
        maskf = room(TT, T).rearrange("p (t k) -> p t k", t=TT)
        cemb, cen = room(D)[0:NCOL, :], room(D)[0:NCOL, :]

        x0, x1, x3 = sb("x0", [P, TT, D]), sb("x1", [P, TT, D]), sb("x3", [P, TT, D])
        x2 = x0
        xT = sb("xT", [P, DT, T])
        nmx = sb("nmx", [P, 2, 4])
        yF = sb("yF", [P, TT, D])
        stF, agF, lnF, rsF = sb("stF", [P, TT, 6]), sb("agF", [P, TT, 2]), sb("lnF", [P, TT]), sb("rsF", [P, TT])
        nmr, er = sb("nmr", [P, T]), sb("er", [P, T])
        acol = sb("acol", [P, TT, 8])
        sm = sb("sm", [P, 12, TT, NCOL])
        s2 = sb("s2", [P, 8, TT])
        ohb = sb("ohb", [P, TT, NCOL], bf16)

        x4, x5 = sb("x4", [P, TT, D]), sb("x5", [P, TT, D])
        x6 = x4
        bT = sb("bT", [P, DT, T])
        xd, x3b = sb("xd", [P, T]), sb("x3b", [P, TT, D])
        xnm, xri = sb("xnm", [P, 2, 4]), sb("xri", [P, 2, T])
        yB = sb("yB", [P, TT, D])
        stB, agB, lnB, rsB = sb("stB", [P, TT, 6]), sb("agB", [P, TT, 2]), sb("lnB", [P, TT]), sb("rsB", [P, TT])
        gg = sb("gg", [P, 8, TT])

        scratch = nc.dram_tensor("bc_rows", (2, NS, T), f32, kind="Internal").ap()

        banks = [ctx.enter_context(nc.psum_tensor(f"bank{i}", [P, 512], f32)) for i in range(NBANK)]

        loaded, const_ready, go, stored = sem("loaded"), sem("const_ready"), sem("go"), sem("stored")
        s_set = sem("set_up")
        arrived = sem("arrived")
        bank_full = [sem(f"bank_full{i}") for i in range(NBANK)]
        bank_free = [sem(f"bank_free{i}") for i in range(NBANK)]
        chain = {n: sem(f"{n}_done") for n in ("dve", "act", "pool")}
        signals = {}
        last_sem = [chain["pool"].num]

        def sig(name):
            if name not in signals:
                signals[name] = sem(name)
                assert signals[name].num == last_sem[0] + 1 or not signals, name
                last_sem[0] = signals[name].num
            return signals[name]

        class Ring:

            def __init__(self, steps):
                self.at = {}
                for s in steps:
                    for f in FILLS.get(s, []):
                        self.at[f] = len(self.at)

            def open(self, pe, name):
                n = self.at[name]
                if n >= NBANK:
                    pe.wait_ge(bank_free[n % NBANK], n // NBANK)
                return banks[n % NBANK]

            def full(self, name):
                return bank_full[self.at[name] % NBANK]

            def made(self, eng, name):
                n = self.at[name]
                eng.wait_ge(bank_full[n % NBANK], n // NBANK + 1)
                return banks[n % NBANK]

            def taken(self, eng, name):
                n = self.at[name]
                eng.wait_ge(bank_free[n % NBANK], n // NBANK + 1)

            def free(self, name):
                return bank_free[self.at[name] % NBANK]

        class Chain:

            def __init__(self, eng, s):
                self.eng, self.s, self.n = eng, s, 0

            def __call__(self, ins):
                self.n += 1
                ins.then_inc(self.s, 1)
                self.eng.wait_ge(self.s, self.n)

        NLOAD = len(W) + 2

        def run_clear(sp):
            sp.sem_clear(range(arrived.num, last_sem[0] + 1))

        with nc.Block() as block:

            @block.tensor
            def _(pe):
                mm = pe.matmul

                def run(steps):
                    ring = Ring(steps)

                    def transposes(name, src, kt=TT):
                        bk = ring.open(pe, name)
                        for d in range(DT):
                            for t in range(TT):
                                last = pe.transpose(bk[:, d * T + t * P:d * T + t * P + P],
                                                    src[:, t, d * P:d * P + P], ident[:, :])
                        last.then_inc(ring.full(name), 1)

                    def project(name, w, m0, src, n=T, nm=2, kt=DT):
                        bk = ring.open(pe, name)
                        for m in range(nm):
                            for k in range(kt):
                                last = mm(bk[:, m * n:(m + 1) * n], w[:, k, (m0 + m) * P:(m0 + m + 1) * P],
                                          src[:, k, 0:n], start=(k == 0), stop=(k == kt - 1))
                        last.then_inc(ring.full(name), 1)

                    def tokens(name, src, w, kt):
                        bk = ring.open(pe, name)
                        for t in range(TT):
                            for k in range(kt):
                                last = mm(bk[:, t * D:(t + 1) * D], src[:, k, t * P:(t + 1) * P], w[:, k, :],
                                          start=(k == 0), stop=(k == kt - 1))
                        last.then_inc(ring.full(name), 1)

                    for s in steps:
                        if s == "attn0_x":
                            pe.wait_ge(sig("x0_ready"), 16)
                            transposes("x0T", x0)
                        elif s in ("attn0_q", "attn0_k"):
                            ring.taken(pe, "x0T")
                            for i in range(2):
                                project(f"{s[6]}{i}", W[f"w{s[6]}0"], 2 * i, xT)
                        elif s == "attn0_v":
                            for t in range(TT):
                                bk = ring.open(pe, f"v{t}")
                                for k in range(DT):
                                    last = mm(bk[:, :], xT[:, k, t * P:(t + 1) * P], W["wv0"][:, k, :],
                                              start=(k == 0), stop=(k == DT - 1))
                                last.then_inc(ring.full(f"v{t}"), 1)
                        elif s.startswith("attn0_s"):
                            p = int(s[7:])
                            if p == 0:
                                ring.taken(pe, "q1")
                                ring.taken(pe, "k1")
                            j, r = p // 2, 64 * (p % 2)
                            A = ring.open(pe, f"aSA{p}")
                            for h in range(2):
                                mm(A[:, h * P:(h + 1) * P], qm[r:r + 64, h, j, 0:P], kT[r:r + 64, j, 0:P],
                                   start=True, stop=False)
                                mm(A[:, h * P:(h + 1) * P], identb[:, :], triq[:, :], start=False, stop=True)
                            for h in range(2):
                                bk, c = (A, 256) if h == 0 else (ring.open(pe, f"aSB{p}"), 0)
                                mm(bk[:, c:c + T], qm[r:r + 64, h, j, P:T], kT[r:r + 64, j, :], start=True, stop=False)
                                mm(bk[:, c + P:c + T], identb[:, :], triq[:, :], start=False,
                                   stop=True).then_inc(ring.full(f"aSA{p}" if h == 0 else f"aSB{p}"), 1)
                        elif s.startswith("attn0_t"):
                            p = int(s[7:])
                            ring.taken(pe, f"aSB{p}")
                            A = ring.open(pe, f"aTA{p}")
                            src = pr[:, p % 2, :]
                            for h in range(2):
                                pe.transpose(A[:, h * T:h * T + P], src[:, h * P:(h + 1) * P], ident[:, :])
                                last = pe.transpose(A[:, h * T + P:(h + 1) * T], src[:, T + h * T:T + h * T + P],
                                                    ident[:, :])
                            last.then_inc(ring.full(f"aTA{p}"), 1)
                            Bk = ring.open(pe, f"aTB{p}")
                            for h in range(2):
                                last = pe.transpose(Bk[:, h * P:(h + 1) * P],
                                                    src[:, T + h * T + P:T + (h + 1) * T], ident[:, :])
                            last.then_inc(ring.full(f"aTB{p}"), 1)
                        elif s.startswith("attn0_o") and s != "attn0_out":
                            j = int(s[7:])
                            if j == 0:
                                ring.taken(pe, "v1")
                            ring.taken(pe, f"aTA{2 * j + 1}")
                            ring.taken(pe, f"aTB{2 * j + 1}")
                            bk = ring.open(pe, f"aO{j}")
                            for ones in (0, 1):
                                for k in range(2):
                                    for i in range(4):
                                        sl, h = (2 * j + i // 2) % 4, i % 2
                                        rhs = pT[:, sl, h * T:(h + 1) * T] if k == 0 else \
                                            pT[:, sl, 512 + h * P:512 + (h + 1) * P]
                                        c = 256 * ones + (P if k else 0)
                                        lh = onesv[:, :] if ones else v0[:, k, 128 * j + 32 * i:128 * j + 32 * i + 32]
                                        last = mm(bk[32 * i:32 * i + 32, c:256 * ones + T], lh, rhs,
                                                  start=(k == 0), stop=(k == 1))
                            last.then_inc(ring.full(f"aO{j}"), 1)
                        elif s == "attn0_out":
                            ring.taken(pe, "aO3")
                            tokens("y0", oT, W["wo0"], J0)
                        elif s == "mlstm_c":
                            pe.wait_ge(sig("cF_ready"), 16)
                            transposes("cT", cF)
                        elif s == "mlstm_x":
                            pe.wait_ge(sig("x1_ready"), 2)
                            transposes("x1T", x1)
                        elif s == "mlstm_gates":
                            ring.taken(pe, "x1T")
                            ring.taken(pe, "cT")
                            bk = ring.open(pe, "gates")
                            for g in range(2):
                                for k in range(4):
                                    last = mm(bk[0:8, g * T:(g + 1) * T], gwc[:, k, g * 8:g * 8 + 8],
                                              (xT if k < 2 else cT)[:, k % 2, :], start=(k == 0), stop=(k == 3))
                            last.then_inc(ring.full("gates"), 1)
                        elif s == "mlstm_acol":
                            pe.wait_ge(sig("rows_ready"), 1)
                            bk = ring.open(pe, "acol")
                            for t in range(TT):
                                last = pe.transpose(bk[:, t * 8:t * 8 + 8], row(5)[:, t * P:(t + 1) * P],
                                                    ident[0:8, 0:8])
                            last.then_inc(ring.full("acol"), 1)
                        elif s == "mlstm_ebc":
                            pe.wait_ge(sig("er_ready"), 1)
                            bk = ring.open(pe, "ebc")
                            for t in range(2):
                                last = mm(bk[:, t * T:(t + 1) * T], sele[:, t, :], er[:, :], start=True, stop=True)
                            last.then_inc(ring.full("ebc"), 1)
                        elif s.startswith("mlstm_p"):
                            q = int(s[7:])
                            j, r = q // 2, 64 * (q % 2)
                            if q == 0:
                                pe.wait_ge(sig("nmr_ready"), 1)
                            A = ring.open(pe, f"mMA{q}")
                            for h in range(2):
                                mm(A[:, h * T:(h + 1) * T], selh[:, 2 * q + h, :], nmr[:, :], start=True, stop=False)
                                last = mm(A[:, h * T:h * T + P], identb[:, :], trik[:, :], start=False, stop=True)
                            last.then_inc(ring.full(f"mMA{q}"), 1)
                            Bk = ring.open(pe, f"mMB{q}")
                            for h in range(2):
                                mm(Bk[:, h * P:(h + 1) * P], selh[:, 2 * q + h, :], nmr[:, P:T], start=True, stop=False)
                                last = mm(Bk[:, h * P:(h + 1) * P], identb[:, :], trik[:, :], start=False, stop=True)
                            last.then_inc(ring.full(f"mMB{q}"), 1)
                            if q == 0:
                                pe.wait_ge(sig("xTm_ready"), 2)
                            A = ring.open(pe, f"mKA{q}")
                            for h in range(2):
                                last = mm(A[:, h * T:(h + 1) * T], cT[r:r + 64, j, 0:P], xTm[r:r + 64, h, j, :],
                                          start=True, stop=True)
                            last.then_inc(ring.full(f"mKA{q}"), 1)
                            Bk = ring.open(pe, f"mKB{q}")
                            for h in range(2):
                                last = mm(Bk[:, h * P:(h + 1) * P], cT[r:r + 64, j, P:T], xTm[r:r + 64, h, j, P:T],
                                          start=True, stop=True)
                            last.then_inc(ring.full(f"mKB{q}"), 1)
                        elif s.startswith("mlstm_o"):
                            j = int(s[7:])
                            ring.taken(pe, f"mKB{2 * j + 1}")
                            bk = ring.open(pe, f"mO{j}")
                            for ones in (0, 1):
                                for k in range(2):
                                    for i in range(4):
                                        sl, h = 2 * j + i // 2, i % 2
                                        rhs = pT[:, sl, h * T:(h + 1) * T] if k == 0 else \
                                            pT[:, sl, 512 + h * P:512 + (h + 1) * P]
                                        c = 256 * ones + (P if k else 0)
                                        lh = onesv[:, :] if ones else cF[:, k, 128 * j + 32 * i:128 * j + 32 * i + 32]
                                        last = mm(bk[32 * i:32 * i + 32, c:256 * ones + T], lh, rhs,
                                                  start=(k == 0), stop=(k == 1))
                            last.then_inc(ring.full(f"mO{j}"), 1)
                        elif s in ("mlstm_mean", "mlstm_var"):
                            n = s[6:]
                            src = hT if n == "mean" else hsq
                            if n == "mean":
                                ring.taken(pe, "mO1")
                            else:
                                pe.wait_ge(sig("hsq_ready"), 1)
                            bk = ring.open(pe, n)
                            for t in range(2):
                                last = mm(bk[:, t * T:(t + 1) * T], blk[:, :], src[:, t, :], start=True, stop=True)
                            last.then_inc(ring.full(n), 1)
                        elif s == "mlstm_hn":
                            pe.wait_ge(sig("hnT_ready"), 2)
                            bk = ring.open(pe, "hnT")
                            for t in range(TT):
                                for d in range(DT):
                                    last = pe.transpose(bk[:, t * D + d * P:t * D + d * P + P],
                                                        hnT[:, d, t * P:(t + 1) * P], ident[:, :])
                            last.then_inc(ring.full("hnT"), 1)
                        elif s == "ffn0_x":
                            pe.wait_ge(sig("x2_ready"), 2)
                            transposes("x2T", x2)
                        elif s == "ffn0_in":
                            ring.taken(pe, "x2T")
                            project("hid", W["w1"], 0, xT, nm=1)
                            bk = ring.open(pe, "sim")
                            for t in range(TT):
                                for k in range(DT):
                                    last = mm(bk[:, t * NCOL:(t + 1) * NCOL], xT[:, k, t * P:(t + 1) * P],
                                              cenT[:, k, :], start=(k == 0), stop=(k == DT - 1))
                            last.then_inc(ring.full("sim"), 1)
                        elif s.startswith("ffn0_c"):
                            project(f"c{s[6:]}", W["wcols"], 2 * int(s[6:]), xT)
                        elif s == "ffn0_gate":
                            ring.taken(pe, "hid")
                            bk = ring.open(pe, "gate")
                            for t in range(TT):
                                last = mm(bk[:, t * NCOL:(t + 1) * NCOL], hidT[:, t * P:(t + 1) * P], W["w2"][:, :],
                                          start=True, stop=True)
                            last.then_inc(ring.full("gate"), 1)
                        elif s.startswith("ffn0_m"):
                            c = int(s[6:])
                            if c == 0:
                                pe.wait_ge(sig("onehot_wide"), 1)
                            bk = ring.open(pe, f"m{c}")
                            for m in range(2):
                                for t in range(TT):
                                    cc = 2 * (2 * c + m)
                                    lh = ohx[:, t, cc:cc + 2, :].rearrange("p c n -> p (c n)")
                                    last = mm(bk[:, m * T + t * P:m * T + (t + 1) * P], lh, identb[:, :],
                                              start=True, stop=True)
                            last.then_inc(ring.full(f"m{c}"), 1)
                        elif s == "ffn0_out":
                            ring.taken(pe, "m3")
                            tokens("y2", cols, W["wproj"], CM)
                        elif s == "mamba_x":
                            pe.wait_ge(sig("x3_ready"), 2)
                            transposes("x3T", x3)
                        elif s == "mamba_xi":
                            ring.taken(pe, "x3T")
                            for i in range(2):
                                project(f"xi{i}", W["win"], 2 * i, xT)
                        elif s == "mamba_z":
                            for i in range(2):
                                project(f"z{i}", W["win"], 4 + 2 * i, xT)
                        elif s == "mamba_bc":
                            pe.wait_ge(sig("xc_ready"), 1)
                            project("xdbl", W["wx"], 0, xcF, nm=1, kt=JI)
                        elif s == "mamba_dt":
                            ring.taken(pe, "xdbl")
                            for i in range(2):
                                bk = ring.open(pe, f"dt{i}")
                                for m in range(2):
                                    c = (2 * i + m) * P
                                    last = mm(bk[:, m * T:(m + 1) * T], W["wdt"][:, c:c + P], xd[:, :],
                                              start=True, stop=True)
                                last.then_inc(ring.full(f"dt{i}"), 1)
                        elif s == "mamba_out":
                            pe.wait_ge(sig("yb_ready"), 4)
                            tokens("y3", yb, W["wout"], JI)
                        elif s == "xattn_x":
                            pe.wait_ge(sig("x4_ready"), 2)
                            transposes("x4T", x4)
                        elif s == "xattn_c":
                            pe.wait_ge(sig("c4_ready"), 16)
                            transposes("c4T", c4)
                        elif s == "xattn_q":
                            ring.taken(pe, "x4T")
                            for j in range(DT):
                                project(f"xq{j}", W["xwq"], j, bT, nm=1)
                        elif s == "xattn_kv":
                            ring.taken(pe, "c4T")
                            project("xk", W["xwk"], 0, c4T)
                            tokens("xv", c4T, W["xwv"], DT)
                        elif s.startswith("xattn_s"):
                            u = int(s[7:])
                            g, qt = u // 2, u % 2
                            j, r = g // 2, 64 * (g % 2)
                            if u == 0:
                                ring.taken(pe, "xq0")
                                ring.taken(pe, "xq1")
                                ring.taken(pe, "xk")
                            for n, m0 in (("xSA", 0), ("xSB", 2)):
                                bk = ring.open(pe, f"{n}{u}")
                                for m in range(2):
                                    mm(bk[:, m * T:(m + 1) * T], xqm[r:r + 64, m0 + m, j, qt * P:(qt + 1) * P],
                                       xkT[r:r + 64, j, :], start=True, stop=False)
                                    last = mm(bk[:, m * T:(m + 1) * T], identb[:, :], xmask[:, qt, :],
                                              start=False, stop=True)
                                last.then_inc(ring.full(f"{n}{u}"), 1)
                        elif s.startswith("xattn_t"):
                            u = int(s[7:])
                            ring.taken(pe, f"xSB{u}")
                            for n, k in (("xTA", 0), ("xTB", 1)):
                                bk = ring.open(pe, f"{n}{u}")
                                for m in range(4):
                                    last = pe.transpose(bk[:, m * P:(m + 1) * P],
                                                        xpr[:, u % 2, m * T + k * P:m * T + (k + 1) * P], ident[:, :])
                                last.then_inc(ring.full(f"{n}{u}"), 1)
                        elif s.startswith("xattn_o") and s != "xattn_out":
                            j = int(s[7:])
                            if j == 0:
                                ring.taken(pe, "xv")
                            ring.taken(pe, f"xTA{4 * j + 3}")
                            ring.taken(pe, f"xTB{4 * j + 3}")
                            bk = ring.open(pe, f"xO{j}")
                            for ones in (0, 1):
                                for n, (m, k) in enumerate((m, k) for m in range(2) for k in range(2)):
                                    for i in range(4):
                                        g, hh = i // 2, 2 * (i % 2) + m
                                        head = 8 * j + 4 * g + hh
                                        lh = onesp[:, m, :] if ones else vp[:, k, head, :]
                                        last = mm(bk[32 * i:32 * i + 32, 256 * ones:256 * ones + T], lh,
                                                  xpT[:, g, k, hh, :], start=(n == 0), stop=(n == 3))
                            last.then_inc(ring.full(f"xO{j}"), 1)
                        elif s == "xattn_out":
                            ring.taken(pe, "xO1")
                            tokens("y4", xoT, W["xwo"], DT)
                        elif s == "moe_rank":
                            pe.wait_ge(sig("grep_ready"), 2)
                            bk = ring.open(pe, "grow")
                            for t in range(TT):
                                last = pe.transpose(bk[:, t * P:(t + 1) * P], grep[:, t, :], ident[:, :])
                            last.then_inc(ring.full("grow"), 1)
                        elif s == "moe_pick":
                            pe.wait_ge(sig("perm_ready"), 2)
                            bk = ring.open(pe, "xsel")
                            for d in range(DT):
                                for t in range(TT):
                                    last = mm(bk[:, d * CAP:(d + 1) * CAP], x5[:, t, d * P:(d + 1) * P],
                                              perm[:, t, :], start=(t == 0), stop=(t == TT - 1))
                            last.then_inc(ring.full("xsel"), 1)
                            bk = ring.open(pe, "permT")
                            for t in range(TT):
                                last = pe.transpose(bk[:, t * P:(t + 1) * P], perm[:, t, :], ident[:, :])
                            last.then_inc(ring.full("permT"), 1)
                        elif s == "moe_qkv":
                            ring.taken(pe, "xsel")
                            for j in range(DT):
                                project(f"fq{j}", W["fwq"], j, xselT, n=CAP, nm=1)
                            project("fk", W["fwk"], 0, xselT, n=CAP)
                            bk = ring.open(pe, "fv")
                            for k in range(DT):
                                last = mm(bk[:, 0:D], xselT[:, k, :], W["fwv"][:, k, :], start=(k == 0),
                                          stop=(k == DT - 1))
                            last.then_inc(ring.full("fv"), 1)
                        elif s.startswith("moe_s"):
                            g = int(s[5:])
                            j, r = g // 2, 64 * (g % 2)
                            if g == 0:
                                ring.taken(pe, "fq0")
                                ring.taken(pe, "fq1")
                                ring.taken(pe, "fk")
                            bk = ring.open(pe, f"fS{g}")
                            for m in range(4):
                                last = mm(bk[:, m * P:(m + 1) * P], xqm[r:r + 64, m, j, 0:CAP],
                                          xkT[r:r + 64, j, 0:CAP], start=True, stop=True)
                            last.then_inc(ring.full(f"fS{g}"), 1)
                        elif s.startswith("moe_t"):
                            g = int(s[5:])
                            ring.taken(pe, f"fS{g}")
                            bk = ring.open(pe, f"fT{g}")
                            for m in range(4):
                                last = pe.transpose(bk[:, m * P:(m + 1) * P], xpr[:, g % 2, m * P:(m + 1) * P],
                                                    ident[:, :])
                            last.then_inc(ring.full(f"fT{g}"), 1)
                        elif s.startswith("moe_o") and s != "moe_out":
                            j = int(s[5:])
                            if j == 0:
                                ring.taken(pe, "fv")
                            ring.taken(pe, f"fT{2 * j + 1}")
                            bk = ring.open(pe, f"fO{j}")
                            for ones in (0, 1):
                                for m in range(2):
                                    for i in range(4):
                                        g, hh = 2 * j + i // 2, 2 * (i % 2) + m
                                        lh = onesp[:, m, :] if ones else vp[:, 0, 4 * g + hh, :]
                                        last = mm(bk[32 * i:32 * i + 32, CAP * ones:CAP * ones + CAP], lh,
                                                  xpT[:, g // 2, g % 2, hh, 0:CAP], start=(m == 0), stop=(m == 1))
                            last.then_inc(ring.full(f"fO{j}"), 1)
                        elif s == "moe_out":
                            ring.taken(pe, "fO1")
                            bk = ring.open(pe, "fo")
                            for k in range(DT):
                                last = mm(bk[:, 0:D], xoT[:, k, 0:CAP], W["fwo"][:, k, :], start=(k == 0),
                                          stop=(k == DT - 1))
                            last.then_inc(ring.full("fo"), 1)
                        elif s == "moe_y":
                            ring.taken(pe, "fo")
                            ring.taken(pe, "permT")
                            bk = ring.open(pe, "y5")
                            for t in range(TT):
                                last = mm(bk[:, t * D:(t + 1) * D], permT[:, t, :], fo, start=True, stop=True)
                            last.then_inc(ring.full("y5"), 1)

                pe.wait_ge(const_ready, 1)
                pe.wait_ge(s_set, 1)
                for d in range(DT):
                    last = pe.transpose(banks[0][:, d * NCOL:(d + 1) * NCOL], cen[:, d * P:(d + 1) * P],
                                        ident[0:NCOL, 0:NCOL])
                last.then_inc(s_set, 1)
                pe.wait_ge(go, 1)
                run(FRONT)
                pe.drain().then_inc(arrived, 1)
                pe.wait_ge(go, 2)
                with pe.Fori(1, NB) as b:
                    run(BOTH)
                    pe.drain().then_inc(arrived, 1)
                    pe.wait_ge(go, b + 2)
                run(BACK)
                pe.drain().then_inc(arrived, 1)

            @block.scalar
            def _(act):
                A = act.activation

                def run(steps):
                    ring = Ring(steps)
                    link = Chain(act, chain["act"])

                    def rstd(ag, ln, rs, eps, stats, ready):
                        act.wait_ge(sig(stats[0]), stats[1])
                        link(A(ln[:, :], ag[:, :, 1], ACT.Ln, bias=epsc[:, eps:eps + 1]))
                        A(rs[:, :], ln[:, :], ACT.Exp, scale=-0.5).then_inc(sig(ready), 1)

                    def copy_out(name, dst):
                        bk = ring.made(act, name)
                        n = 1
                        for w in dst.shape[1:]:
                            n *= w
                        src = bk[:, 0:n]
                        if len(dst.shape) == 3:
                            src = src.rearrange("p (a b) -> p a b", a=dst.shape[1])
                        A(dst, src, ACT.Copy).then_inc(ring.free(name), 1)

                    def inverse(name, n, ri):
                        bk = ring.made(act, name)
                        link(A(ri, bk[:, n:2 * n], ACT.Ln))
                        A(ri, ri, ACT.Exp, scale=-1.0).then_inc(sig("inverse_" + name[0]), 1)

                    def softplus_parts(name, i):
                        bk = ring.made(act, name)
                        for m in range(2):
                            c = 2 * i + m
                            A(dtF[:, c, :], bk[:, m * T:(m + 1) * T], ACT.Abs, bias=W["bdt"][:, c:c + 1])
                            last = A(ybF[:, c, :], bk[:, m * T:(m + 1) * T], ACT.Relu, bias=W["bdt"][:, c:c + 1])
                        last.then_inc(ring.free(name), 1)

                    for s in steps:
                        if s == "attn0_x":
                            copy_out("x0T", xT[:, :, :])
                        elif s == "attn0_q":
                            for i in range(2):
                                bk = ring.made(act, f"q{i}")
                                for h in range(2):
                                    last = A(qm[:, h, 2 * i:2 * i + 2, :],
                                             bk[:, :].rearrange("p (a b) -> p a b", a=2), ACT.Copy,
                                             scale=hmask0[:, h:h + 1])
                                last.then_inc(ring.free(f"q{i}"), 1)
                        elif s == "attn0_k":
                            for i in range(2):
                                copy_out(f"k{i}", kT[:, 2 * i:2 * i + 2, :])
                        elif s == "attn0_v":
                            for t in range(TT):
                                copy_out(f"v{t}", v0[:, t, :])
                        elif s.startswith("attn0_s"):
                            p = int(s[7:])
                            act.wait_ge(sig("attn0_max"), p + 1)
                            if p >= 2:
                                ring.made(act, f"aTB{p - 2}")
                            bA, bB = ring.made(act, f"aSA{p}"), ring.made(act, f"aSB{p}")
                            d = pr[:, p % 2, :]
                            for h in range(2):
                                A(d[:, h * P:(h + 1) * P], bA[:, h * P:(h + 1) * P], ACT.Exp,
                                  bias=nmx[:, p % 2, h:h + 1])
                            A(d[:, T:2 * T], bA[:, T:2 * T], ACT.Exp, bias=nmx[:, p % 2, 2:3])\
                                .then_inc(ring.free(f"aSA{p}"), 1)
                            A(d[:, 2 * T:3 * T], bB[:, 0:T], ACT.Exp, bias=nmx[:, p % 2, 3:4])\
                                .then_inc(ring.free(f"aSB{p}"), 1)
                        elif s.startswith("attn0_t"):
                            p = int(s[7:])
                            if p >= 4:
                                ring.made(act, f"aO{(p - 4) // 2}")
                            elif p == 0 and "mamba_in" in steps:
                                act.wait_ge(sig("handed_over"), 3)
                                act.wait_ge(sig("sg_ready"), 1)
                            copy_out(f"aTB{p}", pT[:, p % 4, 512:768])
                        elif s.startswith("attn0_o") and s != "attn0_out":
                            j = int(s[7:])
                            if j >= 2:
                                ring.taken(act, f"aO{j - 2}")
                            inverse(f"aO{j}", T, rinv[:, j % 2, :])
                        elif s == "attn0_ln":
                            rstd(agF, lnF, rsF, 0, ("statsF", 1), "rstdF")
                        elif s == "mlstm_c":
                            copy_out("cT", cT)
                        elif s == "mlstm_scans":
                            ring.taken(act, "gates")
                            link(A(row(2), row(1), ACT.Abs))
                            link(A(row(3), row(2), ACT.Exp, scale=-1.0))
                            A(row(4), row(3), ACT.Ln, bias=1.0).then_inc(sig("lnf"), 1)
                        elif s == "mlstm_acol":
                            copy_out("acol", acol[:, :, :])
                        elif s == "mlstm_ebc":
                            act.wait_ge(sig("maxd"), 1)
                            A(er[0:8, :], row(7), ACT.Exp, scale=-1.0).then_inc(sig("er_ready"), 1)
                            copy_out("ebc", ebc)
                        elif s.startswith("mlstm_p"):
                            q = int(s[7:])
                            ring.taken(act, "acol")
                            if q >= 2:
                                ring.taken(act, f"mKB{q - 2}")
                            bA = ring.made(act, f"mMA{q}")
                            d = pr[:, q % 2, :]
                            for h in range(2):
                                last = A(d[:, h * T:(h + 1) * T], bA[:, h * T:(h + 1) * T], ACT.Exp,
                                         bias=acol[:, 0, 2 * q + h:2 * q + h + 1])
                            last.then_inc(ring.free(f"mMA{q}"), 1)
                            bB = ring.made(act, f"mMB{q}")
                            for h in range(2):
                                last = A(d[:, 512 + h * P:512 + (h + 1) * P], bB[:, h * P:(h + 1) * P], ACT.Exp,
                                         bias=acol[:, 1, 2 * q + h:2 * q + h + 1])
                            last.then_inc(ring.free(f"mMB{q}"), 1)
                        elif s == "mlstm_mean":
                            ring.taken(act, "mean")
                            A(hsq, hcT, ACT.Square).then_inc(sig("hsq_ready"), 1)
                        elif s == "mlstm_var":
                            bk = ring.made(act, "var")
                            A(hT, bk[:, :].rearrange("p (a b) -> p a b", a=2), ACT.Ln, bias=epsc[:, 1:2])\
                                .then_inc(ring.free("var"), 1)
                            ring.taken(act, "var")
                            A(hT, hT, ACT.Exp, scale=-0.5).then_inc(sig("hrs_ready"), 1)
                        elif s == "mlstm_ln":
                            rstd(agF, lnF, rsF, 0, ("statsF", 2), "rstdF")
                        elif s == "ffn0_x":
                            copy_out("x2T", xT[:, :, :])
                            for t in range(TT):
                                last = A(sqj[:, :], x2[:, t, :], ACT.Square, accum_out=s2[:, 0, t:t + 1])
                                if t == 0:
                                    link(last)
                            last.then_inc(sig("ssq_ready"), 1)
                            act.wait_ge(sig("ss_ready"), 1)
                            link(A(s2[:, 2, :], s2[:, 1, :], ACT.Ln, scale=float(2 ** 40)))
                            A(s2[:, 3, :], s2[:, 2, :], ACT.Exp, scale=-0.5).then_inc(sig("rn_ready"), 1)
                        elif s == "ffn0_in":
                            bk = ring.made(act, "hid")
                            A(hidT[:, :], bk[:, 0:T], ACT.Gelu, bias=W["b1"][:, 0:1]).then_inc(ring.free("hid"), 1)
                        elif s.startswith("ffn0_c"):
                            c = int(s[6:])
                            bk = ring.made(act, f"c{c}")
                            for m in range(2):
                                last = A(cols[:, 2 * c + m, :], bk[:, m * T:(m + 1) * T], ACT.Gelu,
                                         bias=W["bcols"][:, 2 * c + m:2 * c + m + 1])
                            last.then_inc(ring.free(f"c{c}"), 1)
                            if c == 3:
                                act.preload_act_table_set(LOG_EXP)
                        elif s == "ffn0_top":
                            ring.taken(act, "gate")
                            A(sm[:, 2, :, :], sm[:, 1, :, :], ACT.Exp, scale=-1.0).then_inc(sig("gexp_ready"), 1)
                            act.wait_ge(sig("shifted"), 1)
                            A(sm[:, 6, :, :], sm[:, 5, :, :], ACT.Exp).then_inc(sig("pexp_ready"), 1)
                        elif s == "ffn0_ln":
                            rstd(agF, lnF, rsF, 0, ("statsF", 3), "rstdF")
                        elif s == "ffn0_res":
                            rstd(agF, lnF, rsF, 0, ("statsF", 4), "rstdF")
                        elif s == "mamba_x":
                            copy_out("x3T", xT[:, :, :])
                        elif s == "mamba_xi":
                            for i in range(2):
                                copy_out(f"xi{i}", xp[:, 2 * i:2 * i + 2, KC - 1:])
                        elif s == "mamba_z":
                            for i in range(2):
                                bk = ring.made(act, f"z{i}")
                                A(zsF[:, 2 * i:2 * i + 2, :], bk[:, :].rearrange("p (a b) -> p a b", a=2), ACT.Silu)\
                                    .then_inc(ring.free(f"z{i}"), 1)
                        elif s == "mamba_conv":
                            act.wait_ge(sig("conv_ready"), 1)
                            A(xcF, ybF, ACT.Silu).then_inc(sig("xc_ready"), 1)
                            act.preload_act_table_set(LOG_EXP)
                        elif s == "mamba_bc":
                            copy_out("xdbl", xd[:, :])
                        elif s == "mamba_dt":
                            softplus_parts("dt0", 0)
                            softplus_parts("dt1", 1)
                        elif s == "mamba_sp":
                            ring.taken(act, "dt1")
                            link(A(dtF, dtF, ACT.Exp, scale=-1.0))
                            A(dtF, dtF, ACT.Ln, bias=1.0).then_inc(sig("sp_ready"), 1)
                        elif s.startswith("mamba_u"):
                            u = int(s[7:])
                            nq, ct = u // JI, u % JI
                            if u == 0:
                                act.wait_ge(sig("handed_over"), 1)
                                act.wait_ge(sig("dA_zeroed"), 2)
                            if u >= 2:
                                act.wait_ge(sig("scanned"), u - 1)
                            for n in range(HN):
                                nn = nq * HN + n
                                last = A(dA[u % 2][:, n, 1:T], dtv[:, ct, 1:T], ACT.Exp, scale=anew[:, ct, nn:nn + 1])
                            last.then_inc(sig("dA_ready"), 1)
                        elif s == "mamba_ln":
                            rstd(agB, lnB, rsB, 0, ("statsB", 1), "rstdB")
                        elif s == "xattn_x":
                            copy_out("x4T", bT[:, :, :])
                        elif s == "xattn_c":
                            copy_out("c4T", c4T)
                        elif s == "xattn_q":
                            bk = ring.made(act, "xq1")
                            for m in range(4):
                                last = A(xqm[:, m, 1, :], bk[:, 0:T], ACT.Identity, bias=xbqm[:, m:m + 1],
                                         scale=hmask1[:, m:m + 1])
                            last.then_inc(ring.free("xq1"), 1)
                        elif s == "xattn_kv":
                            bk = ring.made(act, "xk")
                            for j in range(DT):
                                last = A(xkT[:, j, :], bk[:, j * T:(j + 1) * T], ACT.Identity,
                                         bias=W["xbk"][:, j:j + 1])
                            last.then_inc(ring.free("xk"), 1)
                        elif s.startswith("xattn_s"):
                            u = int(s[7:])
                            act.wait_ge(sig("xattn_max"), u + 1)
                            if u >= 2:
                                ring.made(act, f"xTB{u - 2}")
                            for n, m0 in (("xSA", 0), ("xSB", 2)):
                                bk = ring.made(act, f"{n}{u}")
                                for m in range(2):
                                    last = A(xpr[:, u % 2, (m0 + m) * T:(m0 + m + 1) * T], bk[:, m * T:(m + 1) * T],
                                             ACT.Exp, bias=xnm[:, u % 2, m0 + m:m0 + m + 1])
                                last.then_inc(ring.free(f"{n}{u}"), 1)
                        elif s.startswith("xattn_t"):
                            u = int(s[7:])
                            g, qt = u // 2, u % 2
                            if u >= 4:
                                ring.made(act, "xO0")
                            bk = ring.made(act, f"xTB{u}")
                            A(xpT[:, g % 2, 1, :, qt * P:(qt + 1) * P], bk[:, :].rearrange("p (m q) -> p m q", m=4),
                              ACT.Copy).then_inc(ring.free(f"xTB{u}"), 1)
                        elif s.startswith("xattn_o") and s != "xattn_out":
                            j = int(s[7:])
                            inverse(f"xO{j}", T, xri[:, j, :])
                        elif s == "xattn_ln":
                            rstd(agB, lnB, rsB, 0, ("statsB", 2), "rstdB")
                        elif s == "moe_gate":
                            act.wait_ge(sig("fz_ready"), 2)
                            A(gg[:, 1, :], gg[:, 0, :], ACT.Exp, scale=-1.0).then_inc(sig("fexp_ready"), 1)
                        elif s == "moe_rank":
                            copy_out("grow", grow)
                        elif s == "moe_pick":
                            copy_out("xsel", xselT)
                            copy_out("permT", permT)
                        elif s == "moe_qkv":
                            bk = ring.made(act, "fq1")
                            for m in range(4):
                                last = A(xqm[:, m, 1, 0:CAP], bk[:, 0:CAP], ACT.Copy, scale=hmask1[:, m:m + 1])
                            last.then_inc(ring.free("fq1"), 1)
                            bk = ring.made(act, "fk")
                            A(xkT[:, :, 0:CAP], bk[:, 0:DT * CAP].rearrange("p (j t) -> p j t", j=DT), ACT.Copy)\
                                .then_inc(ring.free("fk"), 1)
                        elif s.startswith("moe_s"):
                            g = int(s[5:])
                            act.wait_ge(sig("moe_max"), g + 1)
                            if g >= 2:
                                ring.made(act, f"fT{g - 2}")
                            bk = ring.made(act, f"fS{g}")
                            for m in range(4):
                                last = A(xpr[:, g % 2, m * P:(m + 1) * P], bk[:, m * P:(m + 1) * P], ACT.Exp,
                                         bias=xnm[:, g % 2, m:m + 1])
                            last.then_inc(ring.free(f"fS{g}"), 1)
                        elif s.startswith("moe_o") and s != "moe_out":
                            j = int(s[5:])
                            inverse(f"fO{j}", CAP, xri[:, j, 0:CAP])
                        elif s == "moe_out":
                            copy_out("fo", fo)
                        elif s == "moe_ln":
                            rstd(agB, lnB, rsB, 0, ("statsB", 3), "rstdB")

                act.wait_ge(loaded, 16 * NLOAD)
                act.wait_ge(const_ready, 1)
                A(anew[:, :, :], W["alog"][:, :, :], ACT.Exp).then_inc(chain["act"], 1)
                A(junk[0:NCOL, :], cemb, ACT.Square, accum_out=cst[:, 0:1]).then_inc(chain["act"], 1)
                act.wait_ge(chain["act"], 2)
                A(cst[:, 1:2], cst[:, 0:1], ACT.Sqrt).then_inc(chain["act"], 1)
                act.preload_act_table_set(LOG_EXP)
                act.wait_ge(go, 1)
                run(FRONT)
                act.drain().then_inc(arrived, 1)
                act.wait_ge(go, 2)
                with act.Fori(1, NB) as b:
                    run(BOTH)
                    act.drain().then_inc(arrived, 1)
                    act.wait_ge(go, b + 2)
                run(BACK)
                act.drain().then_inc(arrived, 1)

            @block.vector
            def _(dve):
                TS, TTn, STT = dve.tensor_scalar, dve.tensor_tensor, dve.scalar_tensor_tensor

                def over(v, shape):
                    return v.unsqueeze(2).to_broadcast(shape)

                def run(steps):
                    ring = Ring(steps)
                    link = Chain(dve, chain["dve"])
                    count = {"F": 0, "B": 0}

                    def stats(half, y):
                        st, ag = (stF, agF) if half == "F" else (stB, agB)
                        for t in range(TT):
                            last = dve.bn_stats(st[:, t, :], y[:, t, :])
                        link(last)
                        for t in range(TT):
                            last = dve.bn_aggr(ag[:, t, :], st[:, t, :])
                        last.then_inc(sig("stats" + half), 1)

                    def normalise(half, y, x, ready):
                        ag, rs = (agF, rsF) if half == "F" else (agB, rsB)
                        count[half] += 1
                        dve.wait_ge(sig("rstd" + half), count[half])
                        for t in range(TT):
                            TS(x[:, t, :], y[:, t, :], ag[:, t, 0:1], rs[:, t:t + 1], ALU.subtract, ALU.mult)\
                                .then_inc(sig(ready), 1)

                    def halves(bk):
                        return bk[:, :].rearrange("p (a b) -> p a b", a=2)

                    def weighted(name, n, ri, dst):
                        bk = ring.made(dve, name)
                        dve.wait_ge(sig("inverse_" + name[0]), int(name[2:]) + 1)
                        TTn(dst, bk[:, 0:n], ri, ALU.mult).then_inc(ring.free(name), 1)

                    for s in steps:
                        if s.startswith("attn0_s"):
                            p = int(s[7:])
                            if p >= 2:
                                ring.taken(dve, f"aSB{p - 2}")
                            bk = ring.made(dve, f"aSA{p}")
                            m = nmx[:, p % 2, :]
                            dve.tensor_reduce(m[:, 0:2], bk[:, 0:T].rearrange("p (h k) -> p h k", h=2), AX.X, ALU.max,
                                              negate=True)
                            dve.tensor_reduce(m[:, 2:3], bk[:, T:2 * T], AX.X, ALU.max, negate=True)
                            bk = ring.made(dve, f"aSB{p}")
                            dve.tensor_reduce(m[:, 3:4], bk[:, 0:T], AX.X, ALU.max, negate=True)\
                                .then_inc(sig("attn0_max"), 1)
                        elif s.startswith("attn0_t"):
                            p = int(s[7:])
                            if p >= 4:
                                ring.made(dve, f"aO{(p - 4) // 2}")
                            elif p == 0 and "mamba_in" in steps:
                                dve.wait_ge(sig("handed_over"), 3)
                            bk = ring.made(dve, f"aTA{p}")
                            dve.tensor_copy(pT[:, p % 4, 0:512], bk[:, :]).then_inc(ring.free(f"aTA{p}"), 1)
                        elif s.startswith("attn0_o") and s != "attn0_out":
                            j = int(s[7:])
                            weighted(f"aO{j}", T, rinv[:, j % 2, :], oT[:, j, :])
                        elif s == "attn0_out":
                            bk = ring.made(dve, "y0")
                            TTn(yF[:, :, :], halves(bk), x0[:, :, :], ALU.add).then_inc(ring.free("y0"), 1)
                            ring.taken(dve, "y0")
                            stats("F", yF)
                        elif s == "attn0_ln":
                            normalise("F", yF, x1, "x1_ready")
                        elif s == "mlstm_x":
                            bk = ring.made(dve, "x1T")
                            dve.tensor_copy(xT[:, :, :], halves(bk)).then_inc(ring.free("x1T"), 1)
                        elif s == "mlstm_gates":
                            bk = ring.made(dve, "gates")
                            TS(row(0), bk[0:8, 0:T], W["gib"][:, 0:1], None, ALU.add)
                            TS(row(1), bk[0:8, T:2 * T], W["gfb"][:, 0:1], None, ALU.add)\
                                .then_inc(ring.free("gates"), 1)
                        elif s == "mlstm_scans":
                            ring.taken(dve, "gates")
                            dve.wait_ge(sig("lnf"), 1)
                            link(STT(row(3), row(1), 0.0, row(4), ALU.min, ALU.subtract))
                            link(dve.tensor_tensor_scan(row(6), ones8[:, :], row(3), 0.0, ALU.mult, ALU.add))
                            TTn(row(5), row(0), row(6), ALU.subtract).then_inc(sig("rows_ready"), 1)
                            dve.wait_ge(sig("rows_ready"), 1)
                            link(dve.tensor_tensor_scan(row(2), row(5), row(5), -3.0e38, ALU.max, ALU.max))
                            TS(nmr[0:8, :], row(2), -1.0, None, ALU.mult).then_inc(sig("nmr_ready"), 1)
                            TTn(row(7), row(6), row(2), ALU.add).then_inc(sig("maxd"), 1)
                        elif s.startswith("mlstm_p"):
                            q = int(s[7:])
                            bk = ring.made(dve, f"mKA{q}")
                            ring.taken(dve, f"mMA{q}")
                            TTn(pT[:, q, 0:512], bk[:, :], pr[:, q % 2, 0:512], ALU.mult)\
                                .then_inc(ring.free(f"mKA{q}"), 1)
                            bk = ring.made(dve, f"mKB{q}")
                            ring.taken(dve, f"mMB{q}")
                            TTn(pT[:, q, 512:768], bk[:, 0:256], pr[:, q % 2, 512:768], ALU.mult)\
                                .then_inc(ring.free(f"mKB{q}"), 1)
                        elif s.startswith("mlstm_o"):
                            j = int(s[7:])
                            bk = ring.made(dve, f"mO{j}")
                            ring.taken(dve, "ebc")
                            r = rinv[:, j, :]
                            link(STT(r, bk[:, T:2 * T], -1.0, ebc[:, j, :], ALU.mult, ALU.max))
                            link(TTn(r, bk[:, T:2 * T], r, ALU.max))
                            link(TS(r, r, 1e-6, None, ALU.add))
                            link(dve.reciprocal(r, r))
                            TTn(hT[:, j, :], bk[:, 0:T], r, ALU.mult).then_inc(ring.free(f"mO{j}"), 1)
                        elif s == "mlstm_mean":
                            bk = ring.made(dve, "mean")
                            ring.taken(dve, "mO1")
                            TTn(hcT, hT, halves(bk), ALU.subtract).then_inc(ring.free("mean"), 1)
                        elif s == "mlstm_hn":
                            dve.wait_ge(sig("hrs_ready"), 1)
                            for t in range(2):
                                STT(hnT[:, t, :], hcT[:, t, :], W["onw"][:, t:t + 1], hT[:, t, :], ALU.mult, ALU.mult)\
                                    .then_inc(sig("hnT_ready"), 1)
                            bk = ring.made(dve, "hnT")
                            TTn(yF[:, :, :], halves(bk), x1[:, :, :], ALU.add).then_inc(ring.free("hnT"), 1)
                            ring.taken(dve, "hnT")
                            stats("F", yF)
                        elif s == "mlstm_ln":
                            normalise("F", yF, x2, "x2_ready")
                        elif s == "ffn0_x":
                            dve.wait_ge(sig("ssq_ready"), 1)
                            TS(s2[:, 1, :], s2[:, 0, :], 1e-24, None, ALU.max).then_inc(sig("ss_ready"), 1)
                        elif s == "ffn0_in":
                            dve.wait_ge(sig("rn_ready"), 1)
                            bk = ring.made(dve, "sim")
                            for t in range(TT):
                                last = TS(sm[:, 0, t, :], bk[:, t * NCOL:(t + 1) * NCOL], s2[:, 3, t:t + 1],
                                          float(2 ** 20), ALU.mult, ALU.mult)
                            last.then_inc(ring.free("sim"), 1)
                        elif s == "ffn0_gate":
                            v = [P, TT, NCOL]
                            bk = ring.made(dve, "gate")
                            TTn(sm[:, 1, :, :], bk[:, 0:TT * NCOL].rearrange("p (t c) -> p t c", t=TT),
                                W["b2r"][:, :].unsqueeze(1).to_broadcast(v), ALU.add).then_inc(ring.free("gate"), 1)
                        elif s == "ffn0_top":
                            v = [P, TT, NCOL]
                            dve.wait_ge(sig("gexp_ready"), 1)
                            link(TS(sm[:, 3, :, :], sm[:, 2, :, :], 1.0, None, ALU.add))
                            link(dve.reciprocal(sm[:, 10, :, :], sm[:, 3, :, :]))
                            link(TTn(sm[:, 4, :, :], sm[:, 10, :, :], sm[:, 0, :, :], ALU.add))
                            link(dve.reduce_max(s2[:, 4, :], sm[:, 4, :, :], AX.X))
                            TTn(sm[:, 5, :, :], sm[:, 4, :, :], over(s2[:, 4, :], v), ALU.subtract)\
                                .then_inc(sig("shifted"), 1)
                            link(TTn(sm[:, 7, :, :], sm[:, 4, :, :], over(s2[:, 4, :], v), ALU.is_ge))
                            link(TTn(sm[:, 8, :, :], sm[:, 7, :, :], revc[:, :, :], ALU.mult))
                            link(dve.reduce_max(s2[:, 7, :], sm[:, 8, :, :], AX.X))
                            TTn(ohb[:, :, :], sm[:, 8, :, :], over(s2[:, 7, :], v), ALU.is_equal)\
                                .then_inc(sig("onehot_ready"), 1)
                            dve.wait_ge(sig("pexp_ready"), 1)
                            link(dve.reduce_sum(s2[:, 5, :], sm[:, 6, :, :], AX.X))
                            link(dve.reciprocal(s2[:, 6, :], s2[:, 5, :]))
                        elif s.startswith("ffn0_m"):
                            c = int(s[6:])
                            ring.taken(dve, f"c{c}")
                            bk = ring.made(dve, f"m{c}")
                            TTn(cols[:, 2 * c:2 * c + 2, :], halves(bk), cols[:, 2 * c:2 * c + 2, :], ALU.mult)\
                                .then_inc(ring.free(f"m{c}"), 1)
                        elif s == "ffn0_out":
                            bk = ring.made(dve, "y2")
                            dve.wait_ge(sig("ffn_base"), 1)
                            for t in range(TT):
                                last = STT(yF[:, t, :], bk[:, t * D:(t + 1) * D], s2[:, 6, t:t + 1], x1[:, t, :],
                                           ALU.mult, ALU.add)
                            last.then_inc(ring.free("y2"), 1)
                            ring.taken(dve, "y2")
                            stats("F", yF)
                        elif s == "ffn0_ln":
                            count["F"] += 1
                            dve.wait_ge(sig("rstdF"), count["F"])
                            dve.wait_ge(sig("res_base"), 1)
                            for t in range(TT):
                                last = STT(x1[:, t, :], yF[:, t, :], agF[:, t, 0:1], W["lngr"][:, :], ALU.subtract,
                                           ALU.mult)
                            link(last)
                            for t in range(TT):
                                last = STT(yF[:, t, :], x1[:, t, :], rsF[:, t:t + 1], cF[:, t, :], ALU.mult, ALU.add)
                            link(last)
                            stats("F", yF)
                        elif s == "ffn0_res":
                            if "mamba_in" in steps:
                                dve.wait_ge(sig("x3b_ready"), 1)
                            normalise("F", yF, x3, "x3_ready")
                        elif s == "mamba_conv":
                            ring.taken(dve, "xi1")
                            dve.wait_ge(sig("xp_zeroed"), 1)
                            for ct in range(JI):
                                last = TS(ybF[:, ct, :], xp[:, ct, KC - 1:], W["convw"][:, ct, KC - 1:KC],
                                          W["convb"][:, ct:ct + 1], ALU.mult, ALU.add)
                            link(last)
                            for k in range(KC - 1):
                                for ct in range(JI):
                                    last = STT(ybF[:, ct, :], xp[:, ct, k:k + T], W["convw"][:, ct, k:k + 1],
                                               ybF[:, ct, :], ALU.mult, ALU.add)
                                if k < KC - 2:
                                    link(last)
                            last.then_inc(sig("conv_ready"), 1)
                        elif s == "mamba_sp":
                            dve.wait_ge(sig("sp_ready"), 1)
                            TTn(dtF, dtF, ybF, ALU.add)
                        elif s == "mamba_in":
                            TTn(sg, dtF, xcF, ALU.mult).then_inc(sig("sg_ready"), 1)
                            dve.wait_ge(sig("sg_ready"), 1)
                        elif s.startswith("mamba_u"):
                            u = int(s[7:])
                            nq, ct = u // JI, u % JI
                            if ct == 0:
                                dve.wait_ge(sig(f"bc_loaded{nq % 2}"), 32 * (nq // 2 + 1))
                            v = hs[u % 2]
                            link(TTn(v, bq[nq % 2],
                                     sg[:, ct, :].unsqueeze(1).to_broadcast([P, HN, T]), ALU.mult))
                            dve.wait_ge(sig("dA_ready"), u + 1)
                            flat = v.rearrange("p n t -> p (n t)")
                            dve.tensor_tensor_scan(flat, dA[u % 2].rearrange("p n t -> p (n t)"), flat, 0.0, ALU.mult,
                                                   ALU.add).then_inc(sig("scanned"), 1)
                        elif s.startswith("mamba_y"):
                            u = int(s[7:])
                            ct, v = u % JI, hs[u % 2]
                            dve.wait_ge(sig("paired"), u + 1)
                            if u < JI and u % 2 == 0:
                                TTn(yb[:, ct, :], v[:, 0, :], v[:, 1, :], ALU.add).then_inc(sig("summed"), 1)
                            elif u < JI:
                                dve.tensor_copy(yb[:, ct, :], v[:, 0, :]).then_inc(sig("summed"), 1)
                            else:
                                if u % 2 == 0:
                                    link(TTn(v[:, 0, :], v[:, 0, :], v[:, 1, :], ALU.add))
                                TTn(yb[:, ct, :], yb[:, ct, :], v[:, 0, :], ALU.add).then_inc(sig("summed"), 1)
                            dve.wait_ge(sig("summed"), u + 1)
                        elif s == "mamba_gate":
                            dve.wait_ge(sig("handed_over"), 3)
                            dve.wait_ge(sig("summed"), JI * NS // HN)
                            for ct in range(JI):
                                last = STT(yb[:, ct, :], xc[:, ct, :], W["dp"][:, ct:ct + 1], yb[:, ct, :], ALU.mult,
                                           ALU.add)
                            link(last)
                            for ct in range(JI):
                                TTn(yb[:, ct, :], yb[:, ct, :], zs[:, ct, :], ALU.mult).then_inc(sig("yb_ready"), 1)
                        elif s == "mamba_out":
                            bk = ring.made(dve, "y3")
                            TTn(yB[:, :, :], halves(bk), x3b[:, :, :], ALU.add).then_inc(ring.free("y3"), 1)
                            ring.taken(dve, "y3")
                            stats("B", yB)
                        elif s == "mamba_ln":
                            dve.wait_ge(sig("x4_free"), 1)
                            normalise("B", yB, x4, "x4_ready")
                        elif s == "xattn_q":
                            bk = ring.made(dve, "xq0")
                            for m in range(4):
                                last = TS(xqm[:, m, 0, :], bk[:, 0:T], W["xbq"][:, 0:1], hmask1[:, m:m + 1],
                                          ALU.add, ALU.mult)
                            last.then_inc(ring.free("xq0"), 1)
                        elif s == "xattn_kv":
                            bk = ring.made(dve, "xv")
                            dve.wait_ge(sig("vp_zeroed"), 1)
                            for t in range(TT):
                                src = bk[:, t * D:(t + 1) * D].rearrange("p (h o d) -> p h o d", o=2, d=16)
                                bias = W["xbvr"][:, :].rearrange("p (h o d) -> p h o d", o=2, d=16)
                                dst = vp[:, t, :, :].rearrange("p (h o) d -> p h o d", o=2)
                                for o in range(2):
                                    last = TTn(dst[:, :, o, 16 * o:16 * o + 16], src[:, :, o, :], bias[:, :, o, :],
                                               ALU.add)
                            last.then_inc(ring.free("xv"), 1)
                        elif s.startswith("xattn_s"):
                            u = int(s[7:])
                            if u >= 2:
                                ring.taken(dve, f"xSB{u - 2}")
                            for n, m0 in (("xSA", 0), ("xSB", 2)):
                                bk = ring.made(dve, f"{n}{u}")
                                last = dve.tensor_reduce(xnm[:, u % 2, m0:m0 + 2], halves(bk), AX.X, ALU.max,
                                                         negate=True)
                            last.then_inc(sig("xattn_max"), 1)
                        elif s.startswith("xattn_t"):
                            u = int(s[7:])
                            g, qt = u // 2, u % 2
                            if u >= 4:
                                ring.made(dve, "xO0")
                            bk = ring.made(dve, f"xTA{u}")
                            dve.tensor_copy(xpT[:, g % 2, 0, :, qt * P:(qt + 1) * P],
                                            bk[:, :].rearrange("p (m q) -> p m q", m=4))\
                                .then_inc(ring.free(f"xTA{u}"), 1)
                        elif s.startswith("xattn_o") and s != "xattn_out":
                            j = int(s[7:])
                            weighted(f"xO{j}", T, xri[:, j, :], xoT[:, j, :])
                        elif s == "xattn_out":
                            bk = ring.made(dve, "y4")
                            dve.wait_ge(sig("xattn_base"), 1)
                            TTn(yB[:, :, :], halves(bk), yB[:, :, :], ALU.add).then_inc(ring.free("y4"), 1)
                            ring.taken(dve, "y4")
                            stats("B", yB)
                        elif s == "xattn_ln":
                            normalise("B", yB, x5, "x5_ready")
                        elif s == "moe_gate":
                            dve.wait_ge(sig("x5_ready"), 2)
                            for t in range(TT):
                                STT(junk, x5[:, t, :], 1.0, W["wgr"][:, :], ALU.mult, ALU.mult,
                                    accum_out=gg[:, 0, t:t + 1]).then_inc(sig("fz_ready"), 1)
                                dve.wait_ge(sig("fz_ready"), t + 1)
                            dve.wait_ge(sig("fexp_ready"), 1)
                            link(TS(gg[:, 2, :], gg[:, 1, :], 1.0, None, ALU.add))
                            link(dve.reciprocal(gg[:, 3, :], gg[:, 2, :]))
                            for t in range(TT):
                                dve.tensor_copy(grep[:, t, :], gg[:, 3, t:t + 1].to_broadcast([P, P]))\
                                    .then_inc(sig("grep_ready"), 1)
                        elif s == "moe_rank":
                            ring.taken(dve, "grow")
                            for t in range(TT):
                                g = gg[:, 3, t:t + 1]
                                link(TS(junk, grow, g, None, ALU.is_gt, ALU.add,
                                        accum_out=gg[:, 4, t:t + 1]))
                                link(STT(junk, grow, g, lower[:, t, :], ALU.is_equal, ALU.mult,
                                         accum_out=gg[:, 5, t:t + 1]))
                            link(TTn(gg[:, 6, :], gg[:, 4, :], gg[:, 5, :], ALU.add))
                            for t in range(TT):
                                TS(perm[:, t, :], iota[:, :], gg[:, 6, t:t + 1], None, ALU.is_equal)\
                                    .then_inc(sig("perm_ready"), 1)
                        elif s == "moe_qkv":
                            bk = ring.made(dve, "fq0")
                            for m in range(4):
                                last = TS(xqm[:, m, 0, 0:CAP], bk[:, 0:CAP], hmask1[:, m:m + 1], None, ALU.mult)
                            last.then_inc(ring.free("fq0"), 1)
                            bk = ring.made(dve, "fv")
                            src = bk[:, 0:D].rearrange("p (h o d) -> p h o d", o=2, d=16)
                            dst = vp[:, 0, :, :].rearrange("p (h o) d -> p h o d", o=2)
                            for o in range(2):
                                last = dve.tensor_copy(dst[:, :, o, 16 * o:16 * o + 16], src[:, :, o, :])
                            last.then_inc(ring.free("fv"), 1)
                        elif s.startswith("moe_s"):
                            g = int(s[5:])
                            if g >= 2:
                                ring.taken(dve, f"fS{g - 2}")
                            bk = ring.made(dve, f"fS{g}")
                            dve.tensor_reduce(xnm[:, g % 2, 0:4], bk[:, :].rearrange("p (m k) -> p m k", m=4), AX.X,
                                              ALU.max, negate=True).then_inc(sig("moe_max"), 1)
                        elif s.startswith("moe_t"):
                            g = int(s[5:])
                            bk = ring.made(dve, f"fT{g}")
                            dve.tensor_copy(xpT[:, g // 2, g % 2, :, 0:CAP],
                                            bk[:, :].rearrange("p (m q) -> p m q", m=4))\
                                .then_inc(ring.free(f"fT{g}"), 1)
                        elif s.startswith("moe_o") and s != "moe_out":
                            j = int(s[5:])
                            weighted(f"fO{j}", CAP, xri[:, j, 0:CAP], xoT[:, j, 0:CAP])
                        elif s == "moe_y":
                            bk = ring.made(dve, "y5")
                            for t in range(TT):
                                last = STT(yB[:, t, :], bk[:, t * D:(t + 1) * D], gg[:, 3, t:t + 1], x5[:, t, :],
                                           ALU.mult, ALU.add)
                            last.then_inc(ring.free("y5"), 1)
                            ring.taken(dve, "y5")
                            stats("B", yB)
                        elif s == "moe_ln":
                            normalise("B", yB, x6, "x6_ready")

                link = Chain(dve, chain["dve"])
                dve.wait_ge(loaded, 16 * NLOAD)
                dve.wait_ge(const_ready, 1)
                dve.wait_ge(chain["act"], 3)
                TS(xbqm[:, :], hmask1[:, :], W["xbq"][:, 1:2], None, ALU.mult)
                link(TS(anew[:, :, :], anew[:, :, :], -1.0, None, ALU.mult))
                link(TS(cst[:, 2:3], cst[:, 1:2], 1e-12, None, ALU.max))
                link(dve.reciprocal(cst[:, 3:4], cst[:, 2:3]))
                TS(cen, cemb, cst[:, 3:4], None, ALU.mult).then_inc(s_set, 1)
                dve.tensor_copy(gwc[:, 0:2, :], W["gw"][:, 0:2, :])
                link(TTn(gwc[:, 2:4, :], W["gw"][:, 2:4, :], W["gw"][:, 4:6, :], ALU.add))
                link(dve.tensor_copy(maskf, maski))
                link(TS(xmask[:, :, :], maskf, 0.0, MASKED, ALU.is_equal, ALU.mult))
                dve.wait_ge(s_set, 2)
                dve.tensor_copy(cenT[:, :, :], banks[0][:, 0:DT * NCOL].rearrange("p (d c) -> p d c", d=DT))\
                    .then_inc(s_set, 1)
                dve.wait_ge(go, 1)
                run(FRONT)
                dve.drain().then_inc(arrived, 1)
                dve.wait_ge(go, 2)
                with dve.Fori(1, NB) as b:
                    run(BOTH)
                    dve.drain().then_inc(arrived, 1)
                    dve.wait_ge(go, b + 2)
                run(BACK)
                dve.drain().then_inc(arrived, 1)

            @block.gpsimd
            def _(pool):
                def run(steps):
                    ring = Ring(steps)
                    link = Chain(pool, chain["pool"])
                    for s in steps:
                        if s == "mlstm_x":
                            ring.taken(pool, "x1T")
                            for h in range(2):
                                pool.tensor_scalar(xTm[:, h, :, :], xT[:, :, :], hmask0[:, h:h + 1], None, ALU.mult)\
                                    .then_inc(sig("xTm_ready"), 1)
                        elif s == "ffn0_top":
                            pool.wait_ge(sig("x2_ready"), 2)
                            pool.tensor_tensor(x1[:, :, :], x2[:, :, :],
                                               W["pbr"][:, :].unsqueeze(1).to_broadcast([P, TT, D]), ALU.add)\
                                .then_inc(sig("ffn_base"), 1)
                            pool.tensor_tensor(cF, x2[:, :, :],
                                               W["lnbr"][:, :].unsqueeze(1).to_broadcast([P, TT, D]), ALU.add)\
                                .then_inc(sig("res_base"), 1)
                            pool.wait_ge(sig("onehot_ready"), 1)
                            pool.tensor_copy(ohx[:, :, :, :].rearrange("p t c n -> p (t c) n"),
                                             ohb[:, :, :].rearrange("p t c -> p (t c)").unsqueeze(2)
                                             .to_broadcast([P, TT * NCOL, NNEU])).then_inc(sig("onehot_wide"), 1)
                        elif s == "mamba_in":
                            pool.tensor_copy(dtv, dtF).then_inc(sig("handed_over"), 1)
                            for i in range(2):
                                pool.memset(dA[i][:, :, 0:1], 0.0).then_inc(sig("dA_zeroed"), 1)
                            pool.tensor_copy(xc, xcF).then_inc(sig("handed_over"), 1)
                            pool.tensor_copy(zs, zsF).then_inc(sig("handed_over"), 1)
                            pool.tensor_copy(x3b[:, :, :], x3[:, :, :]).then_inc(sig("x3b_ready"), 1)
                        elif s == "mamba_x":
                            pool.wait_ge(sig("x3_ready"), 2)
                            pool.memset(xp[:, :, 0:KC - 1], 0.0).then_inc(sig("xp_zeroed"), 1)
                        elif s.startswith("mamba_u"):
                            u = int(s[7:])
                            nq, ct = u // JI, u % JI
                            v = hs[u % 2]
                            if ct == 0:
                                pool.wait_ge(sig(f"bc_loaded{nq % 2}"), 32 * (nq // 2 + 1))
                            pool.wait_ge(sig("scanned"), u + 1)
                            link(pool.tensor_tensor(v, v, cq[nq % 2], ALU.mult))
                            pair = pool.tensor_tensor(v[:, 0:2, :], v[:, 0:2, :], v[:, 2:4, :], ALU.add)
                            if u % 2 == 0:
                                pair.then_inc(sig("paired"), 1)
                            else:
                                link(pair)
                                pool.tensor_tensor(v[:, 0, :], v[:, 0, :], v[:, 1, :], ALU.add)\
                                    .then_inc(sig("paired"), 1)
                        elif s == "xattn_c":
                            pool.wait_ge(sig("summed"), JI * NS // HN)
                            pool.memset(vp[:, :, :, :], 0.0).then_inc(sig("vp_zeroed"), 1)
                        elif s == "xattn_x":
                            pool.wait_ge(sig("x4_ready"), 2)
                            pool.tensor_tensor(yB[:, :, :], x4[:, :, :],
                                               W["xbor"][:, :].unsqueeze(1).to_broadcast([P, TT, D]), ALU.add)\
                                .then_inc(sig("xattn_base"), 1)

                n = [0]

                def step(ins):
                    n[0] += 1
                    ins.then_inc(chain["pool"], 1)
                    pool.wait_ge(chain["pool"], n[0])

                for v, val in ((ident, 0.0), (triq, 0.0), (trik, 0.0), (lower, 1.0), (onesv, 1.0), (onesp, 0.0),
                               (blk, 0.0), (selh, 0.0), (sele, 0.0), (hmask0, 0.0), (ones8, 1.0), (nmr, 0.0),
                               (er, 0.0), (blk16, 1.0)):
                    last = pool.memset(v[:] if len(v.shape) < 3 else v[:, :, :], val)
                pool.memset(epsc[:, 0:1], 1e-5)
                pool.memset(epsc[:, 1:2], 1e-6)
                step(pool.memset(cst[:, :], 0.0))
                step(pool.affine_select(out=ident[:, :], in_=ident[:, :], compare_op=ALU.not_equal, fill=1.0, base=0,
                                        pattern=[[-1, P]], channel_multiplier=1))
                step(pool.tensor_copy(identb[:, :], ident[:, :]))
                step(pool.affine_select(out=triq[:, :], in_=triq[:, :], compare_op=ALU.is_ge, fill=MASKED, base=0,
                                        pattern=[[-1, P]], channel_multiplier=1))
                step(pool.affine_select(out=trik[:, :], in_=trik[:, :], compare_op=ALU.is_ge, fill=MASKED, base=0,
                                        pattern=[[1, P]], channel_multiplier=-1))
                step(pool.affine_select(out=lower[:, :, :], in_=lower[:, :, :], compare_op=ALU.is_gt, fill=0.0, base=0,
                                        pattern=[[P, TT], [-1, T]], channel_multiplier=1))
                step(pool.affine_select(out=selh[:, :, :], in_=selh[:, :, :], compare_op=ALU.not_equal, fill=1.0,
                                        base=0, pattern=[[-1, NH_M], [0, P]], channel_multiplier=1))
                step(pool.affine_select(out=sele[:, :, :].rearrange("p t (h c) -> p t h c", c=32),
                                        in_=sele[:, :, :].rearrange("p t (h c) -> p t h c", c=32),
                                        compare_op=ALU.not_equal, fill=1.0, base=0,
                                        pattern=[[-4, 2], [-1, 4], [0, 32]], channel_multiplier=1))
                step(pool.affine_select(out=blk16[:, :], in_=blk16[:, :], compare_op=ALU.is_ge, fill=0.0, base=0,
                                        pattern=[[-16, 8]], channel_multiplier=1))
                step(pool.affine_select(out=blk16[:, :], in_=blk16[:, :], compare_op=ALU.is_ge, fill=0.0, base=15,
                                        pattern=[[16, 8]], channel_multiplier=-1))
                step(pool.tensor_tensor(hmask1[:, :], blk16[:, 0:4], blk16[:, 4:8], ALU.add))
                step(pool.tensor_scalar(hmask1[:, :], hmask1[:, :], 16 ** -0.5, None, ALU.mult))
                for i in range(4):
                    step(pool.memset(blk[32 * i:32 * i + 32, 32 * i:32 * i + 32], 1.0 / 32))
                    step(pool.memset(hmask0[32 * i:32 * i + 32, i % 2:i % 2 + 1], 32 ** -0.5))
                for o in range(2):
                    pool.memset(onesp[:, o, 16 * o:16 * o + 16], 1.0)
                pool.iota(iota[:, :], pattern=[[1, P]], base=0, channel_multiplier=0,
                          allow_small_or_imprecise_dtypes=True)
                pool.iota(revc[:, :, :], pattern=[[0, TT], [-1, NCOL]], base=NCOL, channel_multiplier=0,
                          allow_small_or_imprecise_dtypes=True).then_inc(const_ready, 1)
                pool.wait_ge(const_ready, 1)
                pool.wait_ge(go, 1)
                run(FRONT)
                pool.drain().then_inc(arrived, 1)
                pool.wait_ge(go, 2)
                with pool.Fori(1, NB) as b:
                    run(BOTH)
                    pool.drain().then_inc(arrived, 1)
                    pool.wait_ge(go, b + 2)
                run(BACK)
                pool.drain().then_inc(arrived, 1)

            @block.sync
            def _(sp):
                def tiles(v):
                    return v.rearrange("b (t p) d -> p (b t) d", p=P)

                def of(v, b):
                    return tiles(v[b:b + 1, :, :] if isinstance(b, int) else v[bass.ds(b, 1), :, :])

                def run(steps, b, bb):
                    ring = Ring(steps)
                    for s in steps:
                        if s == "attn0_x":
                            sp.dma_start(x0[:, :, :], of(a["x"], b)).then_inc(sig("x0_ready"), 16)
                        elif s == "mlstm_c":
                            sp.dma_start(cF, of(a["ctx"], b)).then_inc(sig("cF_ready"), 16)
                        elif s == "mamba_bc":
                            ring.taken(sp, "xdbl")
                            if "mamba_in" in steps:
                                for i in range(2):
                                    sp.wait_ge(sig(f"bc_loaded{i}"), 64)
                            sp.dma_start(scratch[0, :, :], xd[B_ROW:B_ROW + NS, :]).then_inc(sig("bc_stored"), 16)
                            sp.dma_start(scratch[1, :, :], xd[C_ROW:C_ROW + NS, :]).then_inc(sig("bc_stored"), 16)
                            sp.wait_ge(sig("bc_stored"), 32)
                        elif s.startswith("mamba_u") and int(s[7:]) % JI == 0:
                            nq = int(s[7:]) // JI
                            for n in ((0, 1) if nq == 0 else (nq + 1,) if nq < 3 else ()):
                                if n >= 2:
                                    sp.wait_ge(sig("summed"), JI * (n - 1))
                                for i, v in enumerate((bq, cq)):
                                    sp.dma_start(v[n % 2], scratch[i:i + 1, n * HN:(n + 1) * HN, :]
                                                 .to_broadcast([P, HN, T])).then_inc(sig(f"bc_loaded{n % 2}"), 16)
                        elif s == "xattn_c":
                            sp.wait_ge(sig("summed"), JI * NS // HN)
                            sp.dma_start(c4, of(a["ctx"], bb)).then_inc(sig("c4_ready"), 16)
                        elif s == "mamba_gate":
                            sp.wait_ge(stored, (bb + 1) * 16)
                            sp.sem_inc(sig("x4_free"), 1)
                        elif s == "moe_ln":
                            sp.wait_ge(sig("x6_ready"), 2)
                            sp.dma_start(of(out, bb), x6[:, :, :]).then_inc(stored, 16)

                for n in W:
                    if n in ROWS:
                        sp.dma_start(W[n][:, :], a[n].to_broadcast([P, ROWS[n]])).then_inc(loaded, 16)
                    elif n != "cemb":
                        v = W[n]
                        sp.dma_start(v[:, :] if len(v.shape) == 2 else v[:, :, :], a[n]).then_inc(loaded, 16)
                sp.dma_start(cemb, a["cemb"]).then_inc(loaded, 16)
                sp.dma_start(maski, a["mask"]).then_inc(loaded, 16)
                sp.wait_ge(loaded, 16 * NLOAD)
                sp.wait_ge(s_set, 3)
                sp.sem_inc(stored, 16)
                run_clear(sp)
                sp.sem_inc(go, 1)
                run(FRONT, 0, None)
                sp.wait_ge(arrived, 4)
                run_clear(sp)
                sp.sem_inc(go, 1)
                with sp.Fori(1, NB) as b:
                    run(BOTH, b, b - 1)
                    sp.wait_ge(arrived, 4)
                    run_clear(sp)
                    sp.sem_inc(go, 1)
                run(BACK, None, NB - 1)
                sp.wait_ge(arrived, 4)
                sp.wait_ge(stored, (NB + 1) * 16)


_OUT = ((NB, T, D), "float32")


def _layout(i):
    import numpy as np

    def f(n):
        return np.asarray(i[n])

    def kt(w):
        return np.ascontiguousarray(w.reshape(-1, P, w.shape[1]).transpose(1, 0, 2))

    def col(v):
        return np.ascontiguousarray(v.reshape(-1, P).T)

    wx = np.zeros((DI, P), np.float32)
    xw = f("L1_attn_x_proj_w").T
    wx[:, 0:16], wx[:, B_ROW:B_ROW + NS], wx[:, C_ROW:C_ROW + NS] = xw[:, 0:16], xw[:, 16:32], xw[:, 32:48]
    wdt = np.zeros((P, DI), np.float32)
    wdt[0:16] = f("L1_attn_dt_proj_w").T
    gw = np.concatenate([f("L0_xattn_igate_kernel"), f("L0_xattn_fgate_kernel")], axis=1)
    wc = f("L0_ffn_W_cols").transpose(1, 0, 2).reshape(D, NCOL * NNEU)
    return {
        "x": f("x"), "ctx": f("ctx_1024"), "mask": kt(f("mask_1x1xSxS2_ik0").reshape(T, T)),
        "wq0": kt(f("L0_attn_wq").T), "wk0": kt(f("L0_attn_wk").T), "wv0": kt(f("L0_attn_wv").T),
        "wo0": kt(f("L0_attn_wo").T), "gw": kt(gw), "w1": kt(f("L0_ffn_gate_w1")), "w2": f("L0_ffn_gate_w2"),
        "wcols": kt(wc), "wproj": kt(f("L0_ffn_proj_w")), "win": kt(f("L1_attn_in_proj_w").T), "wx": kt(wx),
        "wdt": wdt, "wout": kt(f("L1_attn_out_proj_w").T), "xwq": kt(f("L1_xattn_Wq")), "xwk": kt(f("L1_xattn_Wk")),
        "xwv": kt(f("L1_xattn_Wv")), "xwo": kt(f("L1_xattn_Wo")), "fwq": kt(f("L1_ffn_Wq")), "fwk": kt(f("L1_ffn_Wk")),
        "fwv": kt(f("L1_ffn_Wv")), "fwo": kt(f("L1_ffn_Wo")), "onw": col(f("L0_xattn_outnorm_weight").reshape(-1)),
        "b1": col(f("L0_ffn_gate_b1")), "bcols": col(f("L0_ffn_b_cols").reshape(-1)),
        "convw": kt(f("L1_attn_conv_w")), "convb": col(f("L1_attn_conv_b")), "bdt": col(f("L1_attn_dt_proj_b")),
        "alog": kt(f("L1_attn_A_log")), "dp": col(f("L1_attn_Dp")), "xbq": col(f("L1_xattn_bq")),
        "xbk": col(f("L1_xattn_bk")), "gib": f("L0_xattn_igate_bias").reshape(8, 1),
        "gfb": f("L0_xattn_fgate_bias").reshape(8, 1), "cemb": f("L0_ffn_col_emb"),
        "b2r": f("L0_ffn_gate_b2").reshape(1, -1), "pbr": f("L0_ffn_proj_b").reshape(1, -1),
        "lngr": f("L0_ffn_ln_g").reshape(1, -1), "lnbr": f("L0_ffn_ln_b").reshape(1, -1),
        "xbvr": f("L1_xattn_bv").reshape(1, -1), "xbor": f("L1_xattn_bo").reshape(1, -1),
        "wgr": f("L1_ffn_Wg").reshape(1, -1),
    }


def kernel(**inputs):
    import numpy as np
    import concourse.bacc as bacc
    from concourse.bass_utils import run_bass_kernel_spmd

    nc = bacc.Bacc("TRN2", target_bir_lowering=False, num_devices=1)
    arrays, aps = {}, {}
    for name, v in _layout(inputs).items():
        v = np.ascontiguousarray(v)
        arrays[f"in_{name}"] = v
        aps[name] = nc.dram_tensor(f"in_{name}", v.shape, mybir.dt.from_np(v.dtype), kind="ExternalInput").ap()
    out = nc.dram_tensor("out_0", _OUT[0], mybir.dt.float32, kind="ExternalOutput").ap()
    build(nc, aps, out)
    r = run_bass_kernel_spmd(nc, [arrays], core_ids=[0])
    return r.results[0]["out_0"]
```
